# Optimizing a Trainium2 kernel written in Bass

```python
import numpy as np
import jax
import jax.numpy as jnp

def _softmax(x, axis=-1):
    return jax.nn.softmax(x, axis=axis)

def _gelu(x):
    return jax.nn.gelu(x, approximate=True)

def _silu(x):
    return jax.nn.silu(x)

def _sigmoid(x):
    return jax.nn.sigmoid(x)

def _layernorm(x, axis=-1, eps=1e-05):
    m = jnp.mean(x, axis=axis, keepdims=True)
    v = jnp.var(x, axis=axis, keepdims=True)
    return (x - m) / jnp.sqrt(v + eps)

def _scatter_add(tgt, idx, src, axis=0):
    return tgt.at[idx].add(src)

def _segment_sum(src, seg, n):
    return jax.ops.segment_sum(src, seg, n)
kernel_name = 'mk_early_fusion_embed_d2_tok_img256_r4_0cb3f4'

def setup_inputs(seed: int=0):
    np.random.seed(seed)
    _w = jnp.asarray

    def _rec_inputs():
        import jax
        import jax.numpy as jnp
        _rk = jax.random.key(seed)
        x = -0.000125008 + 0.999885 * jax.random.normal(jax.random.fold_in(_rk, 1), (16, 64, 128, 128), jnp.float32)
        x_txt = jax.random.randint(jax.random.fold_in(_rk, 51), (16, 32), 0, 16, jnp.int32)
        pos_S = jnp.broadcast_to(jnp.arange(32, dtype=jnp.int32), (32,))
        return (x, x_txt, pos_S)
    x, x_txt, pos_S = _rec_inputs()

    def _L0_tok_setup():
        import jax, jax.numpy as jnp
        import numpy as np
        D_MODEL = 64
        NHEAD = 8
        DS = 4
        OFFSET_SCALE = 4.0

        def bilinear_sample(fm, pts):
            B, C, H, W = fm.shape
            x = (pts[..., 0] + 1.0) * 0.5 * (W - 1)
            y = (pts[..., 1] + 1.0) * 0.5 * (H - 1)
            x0 = jnp.clip(jnp.floor(x), 0.0, W - 2)
            y0 = jnp.clip(jnp.floor(y), 0.0, H - 2)
            wx = jnp.clip(x - x0, 0.0, 1.0)
            wy = jnp.clip(y - y0, 0.0, 1.0)
            x0i = x0.astype(jnp.int32)
            y0i = y0.astype(jnp.int32)
            fm2 = fm.reshape(B, C, H * W)
            N, P = (pts.shape[1], pts.shape[2])

            def gather(yi, xi):
                idx = (yi * W + xi).reshape(B, N * P)
                g = jnp.take_along_axis(fm2, idx[:, None, :], axis=2)
                return g.reshape(B, C, N, P)
            v00 = gather(y0i, x0i)
            v01 = gather(y0i, x0i + 1)
            v10 = gather(y0i + 1, x0i)
            v11 = gather(y0i + 1, x0i + 1)
            wx_ = wx[:, None]
            wy_ = wy[:, None]
            out = v00 * (1 - wx_) * (1 - wy_) + v01 * wx_ * (1 - wy_) + v10 * (1 - wx_) * wy_ + v11 * wx_ * wy_
            return jnp.moveaxis(out, 1, -1)

        def layer_norm(x, g, b, eps=1e-05):
            mu = jnp.mean(x, axis=-1, keepdims=True)
            var = jnp.var(x, axis=-1, keepdims=True)
            return (x - mu) * jax.lax.rsqrt(var + eps) * g + b

        def reference_points(B, H, W):
            yc = jnp.linspace(-1.0, 1.0, H // DS)
            xc = jnp.linspace(-1.0, 1.0, W // DS)
            yg, xg = jnp.meshgrid(yc, xc, indexing='ij')
            ref = jnp.stack([xg.reshape(-1), yg.reshape(-1)], axis=-1)
            return jnp.broadcast_to(ref[None], (B,) + ref.shape)
        key = jax.random.key(seed)
        ks = jax.random.split(key, 6)
        B, C, H, W = (8, D_MODEL, 128, 128)
        s = 0.05
        return {'feature_map': jax.random.normal(ks[0], (B, C, H, W), jnp.float32), 'W_q': jax.random.normal(ks[1], (C, C), jnp.float32) * s, 'W_k': jax.random.normal(ks[2], (C, C), jnp.float32) * s, 'W_v': jax.random.normal(ks[3], (C, C), jnp.float32) * s, 'W_o1': jax.random.normal(ks[4], (C, C // DS), jnp.float32) * s, 'b_o1': jnp.zeros((C // DS,), jnp.float32), 'ln_g': jnp.ones((C // DS,), jnp.float32), 'ln_b': jnp.zeros((C // DS,), jnp.float32), 'W_o2': jax.random.normal(ks[5], (C // DS, NHEAD * 2), jnp.float32) * s, 'b_o2': jnp.zeros((NHEAD * 2,), jnp.float32)}
    _L0_tok_all = _L0_tok_setup()
    _L0_tok_in = {k: v for k, v in _L0_tok_all.items() if k in ('W_q', 'W_k', 'W_v', 'W_o1', 'b_o1', 'ln_g', 'ln_b', 'W_o2', 'b_o2')}
    del _L0_tok_all

    def _L0_txt_setup():
        import jax, jax.numpy as jnp
        import numpy as np
        import math
        EMB_DIM = 64
        HEADS = 8
        HEAD_DIM = EMB_DIM // HEADS
        N_LAYERS = 6
        GRID_H = 32
        GRID_W = 32
        SEQ = GRID_H * GRID_W
        LN_EPS = 1e-05

        def _layernorm(x, w, b):
            mu = jnp.mean(x, axis=-1, keepdims=True)
            var = jnp.mean(jnp.square(x - mu), axis=-1, keepdims=True)
            return (x - mu) * jax.lax.rsqrt(var + LN_EPS) * w + b

        def _sinusoidal_table(num_pos, dim):
            inv_freq = 1.0 / 10000.0 ** (jnp.arange(0, dim, 2, dtype=jnp.float32) / dim)
            t = jnp.arange(num_pos, dtype=jnp.float32)
            sinusoid = t[:, None] * inv_freq[None, :]
            return jnp.concatenate([jnp.sin(sinusoid), jnp.cos(sinusoid)], axis=-1)

        def _alibi_bias(num_heads, seq_len):
            xs, ys = jnp.meshgrid(jnp.arange(GRID_H), jnp.arange(GRID_W), indexing='ij')
            xf = xs.reshape(-1).astype(jnp.float32)
            yf = ys.reshape(-1).astype(jnp.float32)
            dist = jnp.abs(xf[:, None] - xf[None, :]) + jnp.abs(yf[:, None] - yf[None, :])
            dist = jnp.abs(dist[:seq_len, :seq_len])
            i = jnp.arange(num_heads, dtype=jnp.float32)
            slopes_l = -2.0 ** (-(1.0 + i))
            slopes_r = -2.0 ** (-(0.5 + i))
            alibi_l = slopes_l[:, None, None] * dist[None]
            alibi_r = slopes_r[:, None, None] * dist[None]
            return jnp.triu(alibi_r) + jnp.tril(alibi_l)
        key = jax.random.key(seed)
        ks = jax.random.split(key, 8)
        B, S, D, L = (16, SEQ, EMB_DIM, N_LAYERS)
        H2 = 2 * 128
        return {'tokens': jax.random.randint(ks[0], (B, S), 0, 16), 'pos_ids': jnp.arange(S), 'emb_table': jax.random.normal(ks[1], (16, D), dtype=jnp.float32), 'input_weight': jnp.ones((1,), jnp.float32), 'position_weight': jnp.ones((1,), jnp.float32), 'ln1_w': jnp.ones((L, D), jnp.float32), 'ln1_b': jnp.zeros((L, D), jnp.float32), 'ln2_w': jnp.ones((L, D), jnp.float32), 'ln2_b': jnp.zeros((L, D), jnp.float32), 'w1': jax.random.normal(ks[2], (L, D, H2), dtype=jnp.float32) * (1.0 / np.sqrt(D)), 'b1': jnp.zeros((L, H2), jnp.float32), 'w2': jax.random.normal(ks[3], (L, H2, D), dtype=jnp.float32) * (1.0 / np.sqrt(H2)), 'b2': jnp.zeros((L, D), jnp.float32), 'lnf_w': jnp.ones((D,), jnp.float32), 'lnf_b': jnp.zeros((D,), jnp.float32)}
    _L0_txt_all = _L0_txt_setup()
    _L0_txt_in = {k: v for k, v in _L0_txt_all.items() if k in ('emb_table', 'input_weight', 'position_weight', 'ln1_w', 'ln1_b', 'ln2_w', 'ln2_b', 'w1', 'b1', 'w2', 'b2', 'lnf_w', 'lnf_b')}
    del _L0_txt_all

    def _L0_attn_setup():
        import jax, jax.numpy as jnp
        import numpy as np
        D_K = 64
        SPARSITY = 0.5
        key = jax.random.key(seed)
        k1, k2, k3, k4, k5 = jax.random.split(key, 5)
        B, N, d_model, d_k, d_v = (4, 1024, 64, 64, 64)
        x = jax.random.normal(k1, (B, N, d_model), dtype=jnp.float32)
        W_qkv = jax.random.normal(k2, (d_model, 2 * d_k + d_v), dtype=jnp.float32) * 0.02
        b_qkv = jnp.zeros((2 * d_k + d_v,), dtype=jnp.float32)
        W_out = jax.random.normal(k3, (d_v, d_model), dtype=jnp.float32) * 0.02
        b_out = jnp.zeros((d_model,), dtype=jnp.float32)
        return {'x': x, 'W_qkv': W_qkv, 'b_qkv': b_qkv, 'W_out': W_out, 'b_out': b_out}
    _L0_attn_all = _L0_attn_setup()
    _L0_attn_in = {k: v for k, v in _L0_attn_all.items() if k in ('W_qkv', 'b_qkv', 'W_out', 'b_out')}
    del _L0_attn_all

    def _L0_ffn_setup():
        import jax, jax.numpy as jnp
        import numpy as np
        B, S, H, NH, NE = (4, 256, 64, 4, 4)
        D = H // NH
        EPS = 1e-08

        def layernorm(x, g, b):
            m = jnp.mean(x, axis=-1, keepdims=True)
            v = jnp.mean((x - m) ** 2, axis=-1, keepdims=True)
            return (x - m) / jnp.sqrt(v + EPS) * g + b
        key = jax.random.key(seed)
        ks = jax.random.split(key, 18)
        sc = 0.05
        return {'x': jax.random.normal(ks[0], (B, S, H), jnp.float32), 'hl_w': jax.random.normal(ks[1], (NH, D, H), jnp.float32) * sc, 'hl_b': jax.random.normal(ks[2], (NH, D), jnp.float32) * sc, 'wq': jax.random.normal(ks[3], (NH, NE, D, D), jnp.float32) * sc, 'wk': jax.random.normal(ks[4], (NH, D, D), jnp.float32) * sc, 'wv': jax.random.normal(ks[5], (NH, D, D), jnp.float32) * sc, 'gate_w': jax.random.normal(ks[6], (NH, NE, NE * D), jnp.float32) * sc, 'gate_b': jax.random.normal(ks[7], (NH, NE), jnp.float32) * sc, 'ln_g': jnp.ones((D,), jnp.float32), 'ln_b': jnp.zeros((D,), jnp.float32), 'fc1_w': jax.random.normal(ks[8], (D, D), jnp.float32) * sc, 'fc1_b': jax.random.normal(ks[9], (D,), jnp.float32) * sc, 'fc2_w': jax.random.normal(ks[10], (D, D), jnp.float32) * sc, 'fc2_b': jax.random.normal(ks[11], (D,), jnp.float32) * sc, 'fnorm_g': jnp.ones((D,), jnp.float32), 'fnorm_b': jnp.zeros((D,), jnp.float32), 'fgate_w': jax.random.normal(ks[12], (NH, H), jnp.float32) * sc}
    _L0_ffn_all = _L0_ffn_setup()
    _L0_ffn_in = {k: v for k, v in _L0_ffn_all.items() if k in ('hl_w', 'hl_b', 'wq', 'wk', 'wv', 'gate_w', 'gate_b', 'ln_g', 'ln_b', 'fc1_w', 'fc1_b', 'fc2_w', 'fc2_b', 'fnorm_g', 'fnorm_b', 'fgate_w')}
    del _L0_ffn_all

    def _L1_attn_setup():
        import jax, jax.numpy as jnp
        import numpy as np
        B, N, D, H = (4, 256, 64, 8)
        key = jax.random.key(seed)
        k1, k2, k3 = jax.random.split(key, 3)
        x = jax.random.normal(k1, (B, N, D), dtype=jnp.float32)
        Wqkv = jax.random.normal(k2, (D, 3 * D * H), dtype=jnp.float32) * 0.02
        bqkv = jnp.zeros((3 * D * H,), dtype=jnp.float32)
        W0 = jax.random.normal(k3, (D * H, D), dtype=jnp.float32) * 0.02
        b0 = jnp.zeros((D,), dtype=jnp.float32)
        return {'x': x, 'Wqkv': Wqkv, 'bqkv': bqkv, 'W0': W0, 'b0': b0}
    _L1_attn_all = _L1_attn_setup()
    _L1_attn_in = {k: v for k, v in _L1_attn_all.items() if k in ('Wqkv', 'bqkv', 'W0', 'b0')}
    del _L1_attn_all

    def _L1_ffn_setup():
        import jax, jax.numpy as jnp
        import numpy as np
        B, S, H, F, E, K = (8, 1024, 64, 128, 16, 2)
        EPS = 1e-05
        key = jax.random.key(seed)
        ks = jax.random.split(key, 9)
        sc = 0.02
        return {'x': jax.random.normal(ks[0], (B, S, H), dtype=jnp.float32), 'gate_w': jax.random.normal(ks[1], (H, E), dtype=jnp.float32) * sc, 'gate_b': jnp.zeros((E,), dtype=jnp.float32), 'w1': jax.random.normal(ks[2], (E, H, F), dtype=jnp.float32) * sc, 'b1': jnp.zeros((E, F), dtype=jnp.float32), 'w2': jax.random.normal(ks[3], (E, F, H), dtype=jnp.float32) * sc, 'b2': jnp.zeros((E, H), dtype=jnp.float32), 'gamma': jnp.ones((H,), dtype=jnp.float32), 'beta': jnp.zeros((H,), dtype=jnp.float32)}
    _L1_ffn_all = _L1_ffn_setup()
    _L1_ffn_in = {k: v for k, v in _L1_ffn_all.items() if k in ('gate_w', 'gate_b', 'w1', 'b1', 'w2', 'b2', 'gamma', 'beta')}
    del _L1_ffn_all
    return {'x': x, 'x_txt': x_txt, 'pos_S': pos_S, 'L0_tok_W_q': _L0_tok_in['W_q'], 'L0_tok_W_k': _L0_tok_in['W_k'], 'L0_tok_W_v': _L0_tok_in['W_v'], 'L0_tok_W_o1': _L0_tok_in['W_o1'], 'L0_tok_b_o1': _L0_tok_in['b_o1'], 'L0_tok_ln_g': _L0_tok_in['ln_g'], 'L0_tok_ln_b': _L0_tok_in['ln_b'], 'L0_tok_W_o2': _L0_tok_in['W_o2'], 'L0_tok_b_o2': _L0_tok_in['b_o2'], 'L0_txt_emb_table': _L0_txt_in['emb_table'], 'L0_txt_input_weight': _L0_txt_in['input_weight'], 'L0_txt_position_weight': _L0_txt_in['position_weight'], 'L0_txt_ln1_w': _L0_txt_in['ln1_w'], 'L0_txt_ln1_b': _L0_txt_in['ln1_b'], 'L0_txt_ln2_w': _L0_txt_in['ln2_w'], 'L0_txt_ln2_b': _L0_txt_in['ln2_b'], 'L0_txt_w1': _L0_txt_in['w1'], 'L0_txt_b1': _L0_txt_in['b1'], 'L0_txt_w2': _L0_txt_in['w2'], 'L0_txt_b2': _L0_txt_in['b2'], 'L0_txt_lnf_w': _L0_txt_in['lnf_w'], 'L0_txt_lnf_b': _L0_txt_in['lnf_b'], 'L0_attn_W_qkv': _L0_attn_in['W_qkv'], 'L0_attn_b_qkv': _L0_attn_in['b_qkv'], 'L0_attn_W_out': _L0_attn_in['W_out'], 'L0_attn_b_out': _L0_attn_in['b_out'], 'L0_ffn_hl_w': _L0_ffn_in['hl_w'], 'L0_ffn_hl_b': _L0_ffn_in['hl_b'], 'L0_ffn_wq': _L0_ffn_in['wq'], 'L0_ffn_wk': _L0_ffn_in['wk'], 'L0_ffn_wv': _L0_ffn_in['wv'], 'L0_ffn_gate_w': _L0_ffn_in['gate_w'], 'L0_ffn_gate_b': _L0_ffn_in['gate_b'], 'L0_ffn_ln_g': _L0_ffn_in['ln_g'], 'L0_ffn_ln_b': _L0_ffn_in['ln_b'], 'L0_ffn_fc1_w': _L0_ffn_in['fc1_w'], 'L0_ffn_fc1_b': _L0_ffn_in['fc1_b'], 'L0_ffn_fc2_w': _L0_ffn_in['fc2_w'], 'L0_ffn_fc2_b': _L0_ffn_in['fc2_b'], 'L0_ffn_fnorm_g': _L0_ffn_in['fnorm_g'], 'L0_ffn_fnorm_b': _L0_ffn_in['fnorm_b'], 'L0_ffn_fgate_w': _L0_ffn_in['fgate_w'], 'L1_attn_Wqkv': _L1_attn_in['Wqkv'], 'L1_attn_bqkv': _L1_attn_in['bqkv'], 'L1_attn_W0': _L1_attn_in['W0'], 'L1_attn_b0': _L1_attn_in['b0'], 'L1_ffn_gate_w': _L1_ffn_in['gate_w'], 'L1_ffn_gate_b': _L1_ffn_in['gate_b'], 'L1_ffn_w1': _L1_ffn_in['w1'], 'L1_ffn_b1': _L1_ffn_in['b1'], 'L1_ffn_w2': _L1_ffn_in['w2'], 'L1_ffn_b2': _L1_ffn_in['b2'], 'L1_ffn_gamma': _L1_ffn_in['gamma'], 'L1_ffn_beta': _L1_ffn_in['beta']}

def reference(x, x_txt, pos_S, L0_tok_W_q, L0_tok_W_k, L0_tok_W_v, L0_tok_W_o1, L0_tok_b_o1, L0_tok_ln_g, L0_tok_ln_b, L0_tok_W_o2, L0_tok_b_o2, L0_txt_emb_table, L0_txt_input_weight, L0_txt_position_weight, L0_txt_ln1_w, L0_txt_ln1_b, L0_txt_ln2_w, L0_txt_ln2_b, L0_txt_w1, L0_txt_b1, L0_txt_w2, L0_txt_b2, L0_txt_lnf_w, L0_txt_lnf_b, L0_attn_W_qkv, L0_attn_b_qkv, L0_attn_W_out, L0_attn_b_out, L0_ffn_hl_w, L0_ffn_hl_b, L0_ffn_wq, L0_ffn_wk, L0_ffn_wv, L0_ffn_gate_w, L0_ffn_gate_b, L0_ffn_ln_g, L0_ffn_ln_b, L0_ffn_fc1_w, L0_ffn_fc1_b, L0_ffn_fc2_w, L0_ffn_fc2_b, L0_ffn_fnorm_g, L0_ffn_fnorm_b, L0_ffn_fgate_w, L1_attn_Wqkv, L1_attn_bqkv, L1_attn_W0, L1_attn_b0, L1_ffn_gate_w, L1_ffn_gate_b, L1_ffn_w1, L1_ffn_b1, L1_ffn_w2, L1_ffn_b2, L1_ffn_gamma, L1_ffn_beta):
    import jax
    import jax.numpy as jnp

    def _L0_tok_ref(feature_map, W_q, W_k, W_v, W_o1, b_o1, ln_g, ln_b, W_o2, b_o2):
        import jax, jax.numpy as jnp
        import numpy as np
        D_MODEL = 64
        NHEAD = 8
        DS = 4
        OFFSET_SCALE = 4.0

        def bilinear_sample(fm, pts):
            B, C, H, W = fm.shape
            x = (pts[..., 0] + 1.0) * 0.5 * (W - 1)
            y = (pts[..., 1] + 1.0) * 0.5 * (H - 1)
            x0 = jnp.clip(jnp.floor(x), 0.0, W - 2)
            y0 = jnp.clip(jnp.floor(y), 0.0, H - 2)
            wx = jnp.clip(x - x0, 0.0, 1.0)
            wy = jnp.clip(y - y0, 0.0, 1.0)
            x0i = x0.astype(jnp.int32)
            y0i = y0.astype(jnp.int32)
            fm2 = fm.reshape(B, C, H * W)
            N, P = (pts.shape[1], pts.shape[2])

            def gather(yi, xi):
                idx = (yi * W + xi).reshape(B, N * P)
                g = jnp.take_along_axis(fm2, idx[:, None, :], axis=2)
                return g.reshape(B, C, N, P)
            v00 = gather(y0i, x0i)
            v01 = gather(y0i, x0i + 1)
            v10 = gather(y0i + 1, x0i)
            v11 = gather(y0i + 1, x0i + 1)
            wx_ = wx[:, None]
            wy_ = wy[:, None]
            out = v00 * (1 - wx_) * (1 - wy_) + v01 * wx_ * (1 - wy_) + v10 * (1 - wx_) * wy_ + v11 * wx_ * wy_
            return jnp.moveaxis(out, 1, -1)

        def layer_norm(x, g, b, eps=1e-05):
            mu = jnp.mean(x, axis=-1, keepdims=True)
            var = jnp.var(x, axis=-1, keepdims=True)
            return (x - mu) * jax.lax.rsqrt(var + eps) * g + b

        def reference_points(B, H, W):
            yc = jnp.linspace(-1.0, 1.0, H // DS)
            xc = jnp.linspace(-1.0, 1.0, W // DS)
            yg, xg = jnp.meshgrid(yc, xc, indexing='ij')
            ref = jnp.stack([xg.reshape(-1), yg.reshape(-1)], axis=-1)
            return jnp.broadcast_to(ref[None], (B,) + ref.shape)
        B, C, H, W = feature_map.shape
        dh = C // NHEAD
        ref = reference_points(B, H, W)
        Nq = ref.shape[1]
        q_feat = bilinear_sample(feature_map, ref[:, :, None, :])[:, :, 0]
        queries = q_feat @ W_q.T
        h = jax.nn.gelu(layer_norm(q_feat @ W_o1 + b_o1, ln_g, ln_b))
        off = (h @ W_o2 + b_o2).reshape(B, Nq, NHEAD, 2) * OFFSET_SCALE
        scale = jnp.array([2.0 / (W - 1), 2.0 / (H - 1)], jnp.float32)
        sampling_points = ref[:, :, None, :] + off * scale
        sampled = bilinear_sample(feature_map, sampling_points)
        keys = jnp.einsum('bnpc,dc->bnpd', sampled, W_k)
        values = jnp.einsum('bnpc,dc->bnpd', sampled, W_v)
        q = queries.reshape(B, Nq, NHEAD, dh)
        k = keys.reshape(B, Nq, NHEAD, NHEAD, dh)
        v = values.reshape(B, Nq, NHEAD, NHEAD, dh)
        scores = jnp.einsum('bnhd,bnphd->bnhp', q, k) / jnp.sqrt(jnp.float32(dh))
        attn = jax.nn.softmax(scores, axis=-1)
        out = jnp.einsum('bnhp,bnphd->bnhd', attn, v).reshape(B, Nq, C)
        return out

    def _L0_txt_ref(tokens, pos_ids, emb_table, input_weight, position_weight, ln1_w, ln1_b, ln2_w, ln2_b, w1, b1, w2, b2, lnf_w, lnf_b):
        import jax, jax.numpy as jnp
        import numpy as np
        import math
        EMB_DIM = 64
        HEADS = 8
        HEAD_DIM = EMB_DIM // HEADS
        N_LAYERS = 6
        GRID_H = 32
        GRID_W = 32
        SEQ = GRID_H * GRID_W
        LN_EPS = 1e-05

        def _layernorm(x, w, b):
            mu = jnp.mean(x, axis=-1, keepdims=True)
            var = jnp.mean(jnp.square(x - mu), axis=-1, keepdims=True)
            return (x - mu) * jax.lax.rsqrt(var + LN_EPS) * w + b

        def _sinusoidal_table(num_pos, dim):
            inv_freq = 1.0 / 10000.0 ** (jnp.arange(0, dim, 2, dtype=jnp.float32) / dim)
            t = jnp.arange(num_pos, dtype=jnp.float32)
            sinusoid = t[:, None] * inv_freq[None, :]
            return jnp.concatenate([jnp.sin(sinusoid), jnp.cos(sinusoid)], axis=-1)

        def _alibi_bias(num_heads, seq_len):
            xs, ys = jnp.meshgrid(jnp.arange(GRID_H), jnp.arange(GRID_W), indexing='ij')
            xf = xs.reshape(-1).astype(jnp.float32)
            yf = ys.reshape(-1).astype(jnp.float32)
            dist = jnp.abs(xf[:, None] - xf[None, :]) + jnp.abs(yf[:, None] - yf[None, :])
            dist = jnp.abs(dist[:seq_len, :seq_len])
            i = jnp.arange(num_heads, dtype=jnp.float32)
            slopes_l = -2.0 ** (-(1.0 + i))
            slopes_r = -2.0 ** (-(0.5 + i))
            alibi_l = slopes_l[:, None, None] * dist[None]
            alibi_r = slopes_r[:, None, None] * dist[None]
            return jnp.triu(alibi_r) + jnp.tril(alibi_l)
        B, S = tokens.shape
        x_emb = emb_table[tokens]
        pos_emb = _sinusoidal_table(SEQ, EMB_DIM)[pos_ids][None]
        x = input_weight * x_emb + position_weight * pos_emb
        bias = _alibi_bias(HEADS, S)[None]
        scale = 1.0 / math.sqrt(HEAD_DIM)
        for l in range(N_LAYERS):
            xn = _layernorm(x, ln1_w[l], ln1_b[l])
            qkv = xn.reshape(B, S, HEADS, HEAD_DIM).transpose(0, 2, 1, 3)
            scores = jnp.einsum('bhsd,bhtd->bhst', qkv, qkv) * scale + bias
            attn = jax.nn.softmax(scores, axis=-1)
            out = jnp.einsum('bhst,bhtd->bhsd', attn, qkv)
            out = out.transpose(0, 2, 1, 3).reshape(B, S, EMB_DIM)
            x = x + out
            xn = _layernorm(x, ln2_w[l], ln2_b[l])
            h = jax.nn.gelu(xn @ w1[l] + b1[l], approximate=False)
            x = x + (h @ w2[l] + b2[l])
        return _layernorm(x, lnf_w, lnf_b)

    def _L0_attn_ref(x, W_qkv, b_qkv, W_out, b_out):
        import jax, jax.numpy as jnp
        import numpy as np
        D_K = 64
        SPARSITY = 0.5
        d_k = D_K
        qkv = x @ W_qkv + b_qkv
        q = qkv[..., :d_k]
        k = qkv[..., d_k:2 * d_k]
        v = qkv[..., 2 * d_k:]
        scores = jnp.einsum('bqd,bkd->bqk', q, k) / jnp.sqrt(jnp.float32(d_k))
        topk = int(SPARSITY * scores.shape[-1])
        thr = jax.lax.top_k(scores, topk)[0][..., -1:]
        sparse_mask = (scores >= thr).astype(scores.dtype)
        attn = jax.nn.softmax(scores * sparse_mask, axis=-1)
        out = jnp.einsum('bqk,bkd->bqd', attn, v)
        return out @ W_out + b_out

    def _L0_ffn_ref(x, hl_w, hl_b, wq, wk, wv, gate_w, gate_b, ln_g, ln_b, fc1_w, fc1_b, fc2_w, fc2_b, fnorm_g, fnorm_b, fgate_w):
        import jax, jax.numpy as jnp
        import numpy as np
        B, S, H, NH, NE = (4, 256, 64, 4, 4)
        D = H // NH
        EPS = 1e-08

        def layernorm(x, g, b):
            m = jnp.mean(x, axis=-1, keepdims=True)
            v = jnp.mean((x - m) ** 2, axis=-1, keepdims=True)
            return (x - m) / jnp.sqrt(v + EPS) * g + b
        b, s, h = x.shape
        nh, d, _ = wk.shape
        ne = wq.shape[1]
        sx = jnp.einsum('bsh,ndh->bnsd', x, hl_w) + hl_b[None, :, None, :]
        pad = sx == 0
        q = jnp.einsum('bnsd,neod->bneso', sx, wq)
        k = jnp.einsum('bnsd,nod->bnso', sx, wk)
        v = jnp.einsum('bnsd,nod->bnso', sx, wv)
        causal = jnp.where(jnp.tril(jnp.ones((s, s), bool)), 0.0, -jnp.inf).astype(x.dtype)
        scores = jnp.einsum('bnesd,bntd->bnest', q, k) * d ** 0.5 + causal
        att = jax.nn.softmax(scores, axis=-1)
        qkv = jnp.einsum('bnest,bntd->bnesd', att, v)
        qkv = jnp.where(pad[:, :, None], 0.0, qkv)
        out = jnp.transpose(qkv, (0, 1, 3, 2, 4)).reshape(b, nh, s, ne * d)
        gs = jax.nn.softmax(jnp.einsum('bnsf,nef->bnse', out, gate_w) + gate_b[None, :, None, :], axis=-1)
        mixed = jnp.einsum('bnsed,bnse->bnsd', out.reshape(b, nh, s, ne, d), gs)
        resid = sx[jnp.arange(nh), jnp.arange(nh)]
        hn = layernorm(mixed + resid, ln_g, ln_b)
        f_n = jnp.transpose(hn, (0, 2, 1, 3)).reshape(b, s, h)
        fx = f_n.reshape(b, s, nh, d)
        pm = fx == 0
        hx = jnp.where(pm, 0.0, fx @ fc1_w.T + fc1_b)
        hx = jax.nn.relu(hx)
        hx = jnp.where(pm, 0.0, hx @ fc2_w.T + fc2_b)
        hx = layernorm(hx + fx, fnorm_g, fnorm_b)
        fout = hx.reshape(b, s, h)
        fg = jax.nn.softmax(fout @ fgate_w.T, axis=-1)
        return (fout.reshape(b, s, nh, d) * fg[..., None]).reshape(b, s, h)

    def _L1_attn_ref(x, Wqkv, bqkv, W0, b0):
        import jax, jax.numpy as jnp
        import numpy as np
        B, N, D, H = (4, 256, 64, 8)
        b, n, d = x.shape
        h = Wqkv.shape[1] // (3 * d)
        qkv = x @ Wqkv + bqkv
        q, k, v = jnp.reshape(qkv, (3, b, n, d, h))
        score = jnp.einsum('bnqh,btqh->bnth', q, k) * d ** (-0.5)
        attn = jax.nn.softmax(score, axis=1)
        av = jnp.einsum('bnnh,bnqh->bnqh', attn, v)
        out = av.reshape(b, n, d * h) @ W0 + b0
        return out

    def _L1_ffn_ref(x, gate_w, gate_b, w1, b1, w2, b2, gamma, beta):
        import jax, jax.numpy as jnp
        import numpy as np
        B, S, H, F, E, K = (8, 1024, 64, 128, 16, 2)
        EPS = 1e-05
        gate_logits = x @ gate_w + gate_b
        topk_vals, topk_idx = jax.lax.top_k(gate_logits, K)
        topk_w = jax.nn.softmax(topk_vals, axis=-1)
        h = jax.nn.relu(jnp.einsum('bsh,ehf->bsef', x, w1) + b1)
        expert_out = jnp.einsum('bsef,efh->bseh', h, w2) + b2
        sel = jnp.take_along_axis(expert_out, topk_idx[:, :, :, None], axis=2)
        moe = jnp.sum(topk_w[..., None] * sel, axis=2)
        y = x + moe
        mu = jnp.mean(y, axis=-1, keepdims=True)
        var = jnp.var(y, axis=-1, keepdims=True)
        return (y - mu) / jnp.sqrt(var + EPS) * gamma + beta
    h = _L0_tok_ref(x, L0_tok_W_q, L0_tok_W_k, L0_tok_W_v, L0_tok_W_o1, L0_tok_b_o1, L0_tok_ln_g, L0_tok_ln_b, L0_tok_W_o2, L0_tok_b_o2)
    h = jnp.concatenate([h, _L0_txt_ref(x_txt, pos_S, L0_txt_emb_table, L0_txt_input_weight, L0_txt_position_weight, L0_txt_ln1_w, L0_txt_ln1_b, L0_txt_ln2_w, L0_txt_ln2_b, L0_txt_w1, L0_txt_b1, L0_txt_w2, L0_txt_b2, L0_txt_lnf_w, L0_txt_lnf_b)], axis=1)
    h = h + _L0_attn_ref(_layernorm(h, axis=-1), L0_attn_W_qkv, L0_attn_b_qkv, L0_attn_W_out, L0_attn_b_out)
    h = h + _L0_ffn_ref(_layernorm(h, axis=-1), L0_ffn_hl_w, L0_ffn_hl_b, L0_ffn_wq, L0_ffn_wk, L0_ffn_wv, L0_ffn_gate_w, L0_ffn_gate_b, L0_ffn_ln_g, L0_ffn_ln_b, L0_ffn_fc1_w, L0_ffn_fc1_b, L0_ffn_fc2_w, L0_ffn_fc2_b, L0_ffn_fnorm_g, L0_ffn_fnorm_b, L0_ffn_fgate_w)
    h = h + _L1_attn_ref(_layernorm(h, axis=-1), L1_attn_Wqkv, L1_attn_bqkv, L1_attn_W0, L1_attn_b0)
    h = h + _L1_ffn_ref(_layernorm(h, axis=-1), L1_ffn_gate_w, L1_ffn_gate_b, L1_ffn_w1, L1_ffn_b1, L1_ffn_w2, L1_ffn_b2, L1_ffn_gamma, L1_ffn_beta)
    return h

_drawn_inputs = setup_inputs


def setup_inputs(seed=0):
    import zlib

    import numpy as np

    out = dict(_drawn_inputs(seed))
    spreads = {'L0_tok_b_o1': (0.0, 0.1),
     'L0_tok_ln_g': (1.0, 0.2),
     'L0_tok_ln_b': (0.0, 0.1),
     'L0_tok_b_o2': (0.0, 0.1),
     'L0_txt_ln1_w': (1.0, 0.2),
     'L0_txt_ln1_b': (0.0, 0.276),
     'L0_txt_ln2_w': (1.0, 0.586),
     'L0_txt_ln2_b': (0.0, 0.575),
     'L0_txt_b1': (0.0, 0.529),
     'L0_txt_b2': (0.0, 0.316),
     'L0_txt_lnf_w': (1.0, 0.2),
     'L0_txt_lnf_b': (0.0, 0.1),
     'L0_attn_b_qkv': (0.0, 0.1),
     'L0_attn_b_out': (0.0, 0.1),
     'L0_ffn_ln_g': (1.0, 0.2),
     'L0_ffn_ln_b': (0.0, 0.1),
     'L0_ffn_fnorm_g': (1.0, 0.2),
     'L0_ffn_fnorm_b': (0.0, 0.1),
     'L1_attn_bqkv': (0.0, 0.8),
     'L1_attn_b0': (0.0, 0.1),
     'L1_ffn_gate_b': (0.0, 0.1),
     'L1_ffn_b1': (0.0, 0.8),
     'L1_ffn_b2': (0.0, 0.1),
     'L1_ffn_gamma': (1.0, 0.2),
     'L1_ffn_beta': (0.0, 0.1)}
    factors = {'L0_attn_W_qkv': 8.0,
     'L0_ffn_wq': 8.0,
     'L0_ffn_wk': 8.0,
     'L0_ffn_gate_w': 8.0,
     'L0_ffn_gate_b': 8.0,
     'L0_ffn_fc1_w': 2.779,
     'L0_ffn_fc1_b': 8.0,
     'L1_attn_Wqkv': 8.0,
     'L1_attn_W0': 8.0,
     'L1_ffn_w1': 5.121,
     'L1_ffn_w2': 3.685}
    for name, (base, spread) in spreads.items():
        noise = np.random.default_rng([zlib.crc32(name.encode()), seed]).standard_normal(out[name].shape)
        drawn = base * np.exp(spread * noise) if base else spread * noise
        out[name] = jnp.asarray(drawn.astype(out[name].dtype))
    for name, factor in factors.items():
        out[name] = (out[name] * factor).astype(out[name].dtype)
    return out
```

```python
import concourse.bass as bass
from concourse import mybir
from contextlib import ExitStack
import numpy as np

F32 = mybir.dt.float32
BF16 = mybir.dt.bfloat16
I32 = mybir.dt.int32
U32 = mybir.dt.uint32
ALU = mybir.AluOpType
ACT = mybir.ActivationFunctionType
AX = mybir.AxisListType.X

BATCH = 16
C = 64
GRID = 32
NIMG = GRID * GRID
NTXT = 32
SEQ = NIMG + NTXT
ROWS = BATCH * SEQ
NT = 9
TAIL = SEQ - 8 * 128
LN_EPS = 1e-5


class Space:

    def __init__(self, nc, ctx, stage):
        self.nc, self.ctx, self.stage, self.sems, self.gathers = nc, ctx, stage, [], []

    def sb(self, name, shape, dt=F32):
        return self.ctx.enter_context(self.nc.sbuf_tensor(f"{self.stage}s_{name}", shape, dt))

    def ps(self, name, shape, dt=F32):
        return self.ctx.enter_context(self.nc.psum_tensor(f"{self.stage}s_{name}", shape, dt))

    def sem(self, name):
        s = self.ctx.enter_context(self.nc.semaphore(f"{self.stage}s_{name}"))
        self.sems.append(s)
        return s

    def gather_sem(self, name):
        self.gathers.append(self.sem(name))
        return self.gathers[-1]

    def rewind(self):
        for s in self.gathers:
            self.nc.gpsimd.dma_reset(range(s.num, s.num + 1))
        for s in self.sems:
            self.nc.gpsimd.sem_clear(s)
        self.nc.all_engine_barrier()


class Chain:

    def __init__(self, eng, sem):
        self.eng, self.sem, self.n = eng, sem, 0

    def __call__(self, instruction):
        self.n += 1
        instruction.then_inc(self.sem, 1)
        self.eng.wait_ge(self.sem, self.n)


def spread(ap, shape):
    return ap.unsqueeze(len(shape) - 1).to_broadcast(shape)


def layer_norm(dve, chain, x, xc, sq, mu, var, std, s_var, s_std, eps, n_var=1, depth=C):
    shape = list(x.shape)
    chain(dve.reduce_sum(mu, x, axis=AX))
    chain(dve.tensor_scalar(mu, mu, -1.0 / depth, None, ALU.mult))
    chain(dve.tensor_tensor(xc, x, spread(mu, shape), ALU.add))
    chain(dve.tensor_tensor(sq, xc, xc, ALU.mult))
    chain(dve.reduce_sum(var, sq, axis=AX))
    dve.tensor_scalar(var, var, 1.0 / depth, eps, ALU.mult, ALU.add).then_inc(s_var, 1)
    dve.wait_ge(s_std, n_var)
    chain(dve.reciprocal(std, std))
    chain(dve.tensor_tensor(xc, xc, spread(std, shape), ALU.mult))



SIDE = 128
HEADS = 8
POINTS = HEADS
DH = C // HEADS
TILES = NIMG // 128
PIX = (SIDE - 1) * SIDE
OFFSET_SCALE = 4.0
CORNER = 4 * C


def sampling_points(nc, w, fmap, idx_out, wgt_out, q_out):
    with ExitStack() as ctx:
        k = Space(nc, ctx, "a")
        w1 = k.sb("w1", [C + 1, C + 16])
        w2 = k.sb("w2", [33, 16])
        lng = k.sb("lng", [128, 16])
        lnb = k.sb("lnb", [128, 16])
        eye = k.sb("eye", [128, 128])
        wq4 = k.sb("wq4", [128, TILES, 4])
        ref = k.sb("ref", [128, TILES, 2])
        qidx = k.sb("qidx", [128, TILES], U32)
        first = k.sb("first", [128, 1])
        g = k.sb("g", [128, TILES, 4, C])
        qf = k.sb("qf", [128, TILES, C])
        xt = k.sb("xt", [C + 1, TILES, 128])
        o1 = k.sb("o1", [128, TILES, 16])
        hn = k.sb("hn", [128, TILES, 16])
        sq = k.sb("sq", [128, TILES, 16])
        th = k.sb("th", [128, TILES, 16])
        mu = k.sb("mu", [128, TILES])
        var = k.sb("var", [128, TILES])
        std = k.sb("std", [128, TILES])
        hT = k.sb("hT", [33, TILES, 128])
        qs = k.sb("qs", [128, TILES, C])
        pos = k.sb("pos", [128, TILES * POINTS, 2])
        posi = k.sb("posi", [128, TILES * POINTS, 2], I32)
        low = k.sb("low", [128, TILES * POINTS, 2])
        over = k.sb("over", [128, TILES * POINTS, 2])
        frac = k.sb("frac", [128, TILES * POINTS, 2])
        comp = k.sb("comp", [128, TILES * POINTS, 2])
        wgt = k.sb("wgt", [128, TILES * POINTS, 4])
        at = k.sb("at", [128, TILES * POINTS])
        idx = k.sb("idx", [128, TILES * POINTS], U32)
        ps_x = k.ps("ps_x", [128, 2, 512])
        ps_o = k.ps("ps_o", [128, 2, 512])
        ps_h = k.ps("ps_h", [128, 2, 512])
        ps_p = k.ps("ps_p", [128, 512])
        s_w = k.sem("weights_in")
        s_chain = k.sem("dve_step")
        s_pchain = k.sem("pool_step")
        s_i = k.sem("indices_in")
        s_g = k.gather_sem("gathered")
        s_q = k.sem("query_features")
        s_x = k.sem("features_turned")
        s_xk = k.sem("features_turned_kept")
        s_o = k.sem("projected")
        s_var = k.sem("variance")
        s_std = k.sem("deviation")
        s_u = k.sem("gelu_argument")
        s_th = k.sem("tanh")
        s_h = k.sem("hidden")
        s_ht = k.sem("hidden_turned")
        s_hk = k.sem("hidden_turned_kept")
        s_p = k.sem("offsets")
        s_done = k.sem("points")
        s_out = k.sem("points_out")

        with nc.Block() as block:
            @block.sync
            def _(sp):
                for dst, name in ((w1, "a_w1"), (w2, "a_w2"), (eye, "eye"), (wq4, "a_wq4"), (ref, "a_ref")):
                    sp.dma_start(dst[:], w[name]).then_inc(s_w, 16)
                sp.dma_start(lng[:], w["a_lng"].partition_broadcast(128)).then_inc(s_w, 16)
                sp.dma_start(lnb[:], w["a_lnb"].partition_broadcast(128)).then_inc(s_w, 16)
                sp.wait_ge(s_w, 112)

            @block.gpsimd
            def _(pool):
                chain = Chain(pool, s_pchain)
                chain(pool.memset(xt[C:C + 1], 1.0))
                chain(pool.memset(hT[:], 0.0))
                chain(pool.memset(hT[32:33], 1.0))
        k.rewind()

        with nc.Fori(0, BATCH) as b:
            with nc.Block() as block:
                @block.sync
                def _(sp):
                    sp.dma_start(qidx[:], w["a_qidx"][bass.ds(b * 128, 128), :]).then_inc(s_i, 16)
                    sp.dma_start(first[:], w["a_first"][bass.ds(b * 128, 128), :]).then_inc(s_i, 16)
                    sp.wait_ge(s_done, 1)
                    sp.dma_start(idx_out[bass.ds(b * 128, 128), :], idx[:]).then_inc(s_out, 16)
                    sp.dma_start(wgt_out[bass.ds(b * 128, 128), :], wgt[:].rearrange("p a k -> p (a k)")).then_inc(s_out, 16)
                    sp.dma_start(q_out[bass.ds(b * 128, 128), :], qs[:].rearrange("p t c -> p (t c)")).then_inc(s_out, 16)
                    sp.wait_ge(s_out, 48)

                @block.gpsimd
                def _(pool):
                    pool.wait_ge(s_i, 32)
                    for t in range(TILES):
                        pool.indirect_dma_start(g[:, t].rearrange("p k c -> p (k c)"), None, fmap,
                                                bass.IndirectOffsetOnAxis(ap=qidx[:, t:t + 1], axis=0)).then_inc(s_g, 16)
                    pool.wait_ge(s_g, 16 * TILES)

                @block.tensor
                def _(pe):
                    pe.wait_ge(s_q, 1)
                    for t in range(TILES):
                        last = pe.transpose(ps_x[0:C, t // 4, 128 * (t % 4):128 * (t % 4) + 128], qf[:, t], eye[:])
                    last.then_inc(s_x, 1)
                    pe.wait_ge(s_xk, 1)
                    for t in range(TILES):
                        last = pe.matmul(ps_o[:, t // 4, 80 * (t % 4):80 * (t % 4) + 80], xt[:, t], w1[:], start=True, stop=True)
                    last.then_inc(s_o, 1)
                    pe.wait_ge(s_h, 1)
                    for t in range(TILES):
                        last = pe.transpose(ps_h[0:16, t // 4, 128 * (t % 4):128 * (t % 4) + 128], hn[:, t], eye[:])
                    last.then_inc(s_ht, 1)
                    pe.wait_ge(s_hk, 1)
                    for t in range(TILES):
                        last = pe.matmul(ps_p[:, 16 * t:16 * t + 16], hT[:, t], w2[:], start=True, stop=True)
                    last.then_inc(s_p, 1)

                @block.scalar
                def _(act):
                    act.wait_ge(s_var, 1)
                    act.activation(std[:], var[:], ACT.Sqrt).then_inc(s_std, 1)
                    act.wait_ge(s_u, 1)
                    act.activation(th[:], th[:], ACT.Tanh, scale=0.7978845608028654).then_inc(s_th, 1)

                @block.vector
                def _(dve):
                    chain = Chain(dve, s_chain)
                    dve.wait_ge(s_g, 16 * TILES)
                    chain(dve.tensor_tensor(g[:].rearrange("p t k c -> p (t k) c"), g[:].rearrange("p t k c -> p (t k) c"),
                                            spread(wq4[:].rearrange("p t k -> p (t k)"), [128, TILES * 4, C]), ALU.mult))
                    chain(dve.tensor_tensor(g[:, :, 0:2], g[:, :, 0:2], g[:, :, 2:4], ALU.add))
                    dve.tensor_tensor(qf[:], g[:, :, 0], g[:, :, 1], ALU.add).then_inc(s_q, 1)
                    dve.wait_ge(s_x, 1)
                    dve.tensor_copy(xt[0:C].rearrange("p t q -> p (t q)"), ps_x[0:C].rearrange("p a n -> p (a n)")).then_inc(s_xk, 1)
                    dve.wait_ge(s_o, 1)
                    po = ps_o[:, :, 0:320].rearrange("p a (t m) -> p a t m", t=4)
                    dve.tensor_scalar(qs[:].rearrange("p (a t) c -> p a t c", a=2), po[:, :, :, 0:C], float(DH) ** -0.5, None, ALU.mult)
                    chain(dve.tensor_copy(o1[:].rearrange("p (a t) c -> p a t c", a=2), po[:, :, :, C:C + 16]))
                    layer_norm(dve, chain, o1[:], hn[:], sq[:], mu[:], var[:], std[:], s_var, s_std, LN_EPS, depth=16)
                    every = lambda u: u[:].unsqueeze(1).to_broadcast([128, TILES, 16])
                    chain(dve.tensor_tensor(hn[:], hn[:], every(lng), ALU.mult))
                    chain(dve.tensor_tensor(hn[:], hn[:], every(lnb), ALU.add))
                    chain(dve.tensor_tensor(th[:], hn[:], hn[:], ALU.mult))
                    chain(dve.tensor_scalar(th[:], th[:], 0.044715, 1.0, ALU.mult, ALU.add))
                    dve.tensor_tensor(th[:], th[:], hn[:], ALU.mult).then_inc(s_u, 1)
                    dve.wait_ge(s_u, 1)
                    dve.wait_ge(s_th, 1)
                    dve.scalar_tensor_tensor(hn[:], th[:], 1.0, hn[:], ALU.add, ALU.mult).then_inc(s_h, 1)
                    dve.wait_ge(s_ht, 1)
                    dve.tensor_scalar(hT[0:16].rearrange("p t q -> p (t q)"), ps_h[0:16].rearrange("p a n -> p (a n)"), 0.5, None,
                                      ALU.mult).then_inc(s_hk, 1)
                    dve.wait_ge(s_p, 1)
                    p3 = pos[:]
                    chain(dve.tensor_scalar(p3, ps_p[:, 0:128].rearrange("p (a x) -> p a x", x=2), OFFSET_SCALE,
                                            float(np.float32(2.0 / (SIDE - 1))), ALU.mult, ALU.mult))
                    p4 = pos[:].rearrange("p (t a) x -> p t a x", t=TILES)
                    chain(dve.tensor_tensor(p4, p4, ref[:].unsqueeze(2).to_broadcast([128, TILES, POINTS, 2]), ALU.add))
                    chain(dve.tensor_scalar(p3, p3, 1.0, 0.5, ALU.add, ALU.mult))
                    chain(dve.tensor_scalar(p3, p3, float(SIDE - 1), -1.0, ALU.mult, ALU.max))
                    chain(dve.tensor_scalar(p3, p3, float(SIDE), None, ALU.min))
                    chain(dve.tensor_copy(posi[:], p3))
                    chain(dve.tensor_copy(low[:], posi[:]))
                    chain(dve.tensor_tensor(over[:], low[:], p3, ALU.is_gt))
                    chain(dve.tensor_tensor(low[:], low[:], over[:], ALU.subtract))
                    chain(dve.tensor_scalar(low[:], low[:], 0.0, float(SIDE - 2), ALU.max, ALU.min))
                    chain(dve.tensor_tensor(frac[:], p3, low[:], ALU.subtract))
                    chain(dve.tensor_scalar(frac[:], frac[:], 0.0, 1.0, ALU.max, ALU.min))
                    chain(dve.tensor_scalar(comp[:], frac[:], -1.0, 1.0, ALU.mult, ALU.add))
                    chain(dve.scalar_tensor_tensor(at[:], low[:, :, 1], float(SIDE), low[:, :, 0], ALU.mult, ALU.add))
                    chain(dve.tensor_scalar(at[:], at[:], first[:, 0:1], None, ALU.add))
                    chain(dve.tensor_copy(idx[:], at[:]))
                    for n, (wx, wy) in enumerate(((comp, comp), (comp, frac), (frac, comp), (frac, frac))):
                        last = dve.tensor_tensor(wgt[:, :, n], wx[:, :, 0], wy[:, :, 1], ALU.mult)
                    last.then_inc(s_done, 1)
            k.rewind()


def deformable_attention(nc, w, fmap, idx_in, wgt_in, q_in, h_out):
    with ExitStack() as ctx:
        k = Space(nc, ctx, "b")
        NG = 4
        wkv = k.sb("wkv", [128, 2 * 2 * C])
        eye = k.sb("eye", [128, 128])
        idx = k.sb("idx", [128, TILES * POINTS], U32)
        wgt = k.sb("wgt", [128, TILES, POINTS * 4])
        q = k.sb("q", [128, TILES, C])
        g = k.sb("g", [128, NG, POINTS * 4, C])
        m = k.sb("m", [128, 2, 4, POINTS, C])
        st = k.sb("st", [128, 2, 4, 128])
        prod = k.sb("prod", [128, POINTS, C])
        sc = k.sb("sc", [128, 2, POINTS, POINTS])
        mx = k.sb("mx", [128, POINTS])
        z = k.sb("z", [128, POINTS])
        pv = k.sb("pv", [128, POINTS, C])
        y = k.sb("y", [128, TILES, C])
        ps_t = k.ps("ps_t", [128, 2, 4, 128])
        ps_k = k.ps("ps_k", [128, 2, POINTS, 2 * C])
        s_w = k.sem("weights_in")
        s_chain = k.sem("dve_step")
        s_in = k.sem("points_in")
        s_g = [k.gather_sem(f"gathered_{i}") for i in range(NG)]
        s_m = k.sem("corners_weighted")
        s_t = k.sem("corners_summed")
        s_st = k.sem("samples_kept")
        s_k = k.sem("keys_values")
        s_s = k.sem("scores_shifted")
        s_e = k.sem("exponents")
        s_v = k.sem("tiles_done")
        s_out = k.sem("rows_out")

        with nc.Block() as block:
            @block.sync
            def _(sp):
                sp.dma_start(wkv[:], w["b_wkv"]).then_inc(s_w, 16)
                sp.dma_start(eye[:], w["eye"]).then_inc(s_w, 16)
                sp.wait_ge(s_w, 32)
        k.rewind()

        with nc.Fori(0, BATCH) as b:
            with nc.Block() as block:
                @block.sync
                def _(sp):
                    rows = bass.ds(b * 128, 128)
                    sp.dma_start(idx[:], idx_in[rows, :]).then_inc(s_in, 16)
                    sp.dma_start(wgt[:].rearrange("p t k -> p (t k)"), wgt_in[rows, :]).then_inc(s_in, 16)
                    sp.dma_start(q[:].rearrange("p t c -> p (t c)"), q_in[rows, :]).then_inc(s_in, 16)
                    sp.wait_ge(s_v, TILES)
                    sp.dma_start(h_out[bass.ds(b * SEQ, NIMG), :].rearrange("(t p) c -> p t c", p=128), y[:]).then_inc(s_out, 16)
                    sp.wait_ge(s_out, 16)

                @block.gpsimd
                def _(pool):
                    pool.wait_ge(s_in, 48)
                    for t in range(TILES):
                        if t >= NG:
                            pool.wait_ge(s_m, t - NG + 1)
                        for p in range(POINTS):
                            pool.indirect_dma_start(g[:, t % NG, 4 * p:4 * p + 4].rearrange("p k c -> p (k c)"), None, fmap,
                                                    bass.IndirectOffsetOnAxis(ap=idx[:, POINTS * t + p:POINTS * t + p + 1], axis=0))\
                                .then_inc(s_g[t % NG], 16)
                    for n in range(NG):
                        pool.wait_ge(s_g[n], 16 * POINTS * len(range(n, TILES, NG)))

                @block.tensor
                def _(pe):
                    def corners(t):
                        pe.wait_ge(s_m, t + 1)
                        if t >= 2:
                            pe.wait_ge(s_st, t - 1)
                        for i in range(4):
                            for n in range(4):
                                last = pe.matmul(ps_t[:, t % 2, i], m[:, t % 2, n, 2 * i:2 * i + 2, :].rearrange("p a c -> p (a c)"), eye[:], start=n == 0, stop=n == 3)
                        last.then_inc(s_t, 1)

                    def project(t):
                        pe.wait_ge(s_st, t + 1)
                        if t >= 2:
                            pe.wait_ge(s_v, t - 1)
                        for i in range(4):
                            last = pe.matmul(ps_k[:, t % 2, 2 * i:2 * i + 2].rearrange("p a c -> p (a c)"), st[:, t % 2, i], wkv[:], start=True, stop=True)
                        last.then_inc(s_k, 1)

                    for t in range(TILES + 1):
                        if t < TILES:
                            corners(t)
                        if t >= 1:
                            project(t - 1)

                @block.scalar
                def _(act):
                    for t in range(TILES + 2):
                        if t < TILES:
                            act.wait_ge(s_t, t + 1)
                            if t >= 2:
                                act.wait_ge(s_k, t - 1)
                            act.activation(st[:, t % 2], ps_t[:, t % 2], ACT.Copy).then_inc(s_st, 1)
                        if 1 <= t < TILES + 1:
                            act.wait_ge(s_s, t)
                            act.activation(sc[:, (t - 1) % 2], sc[:, (t - 1) % 2], ACT.Exp).then_inc(s_e, 1)

                @block.vector
                def _(dve):
                    chain = Chain(dve, s_chain)

                    def weight(t):
                        dve.wait_ge(s_g[t % NG], 16 * POINTS * (t // NG + 1))
                        if t >= 2:
                            dve.wait_ge(s_t, t - 1)
                        dve.tensor_tensor(m[:, t % 2].rearrange("p k a c -> p a k c"), g[:, t % NG].rearrange("p (a k) c -> p a k c", k=4),
                                          spread(wgt[:, t], [128, 4 * POINTS, C]).rearrange("p (a k) c -> p a k c", k=4), ALU.mult).then_inc(s_m, 1)

                    def score(t):
                        dve.wait_ge(s_k, t + 1)
                        keys = ps_k[:, t % 2, :, 0:C]
                        chain(dve.tensor_tensor(prod[:], keys, q[:, t].unsqueeze(1).to_broadcast([128, POINTS, C]), ALU.mult))
                        s = sc[:, t % 2]
                        chain(dve.reduce_sum(s.rearrange("p a h -> p (a h)"), prod[:].rearrange("p a (h d) -> p (a h) d", h=POINTS), axis=AX))
                        chain(dve.reduce_max(mx[:], s.rearrange("p a h -> p h a"), axis=AX))
                        dve.tensor_tensor(s, s, mx[:].unsqueeze(1).to_broadcast([128, POINTS, POINTS]), ALU.subtract).then_inc(s_s, 1)

                    def mix(t):
                        s = sc[:, t % 2]
                        dve.wait_ge(s_e, t + 1)
                        chain(dve.reduce_sum(z[:], s.rearrange("p a h -> p h a"), axis=AX))
                        chain(dve.reciprocal(z[:], z[:]))
                        values = ps_k[:, t % 2, :, C:2 * C].rearrange("p a (h d) -> p a h d", h=POINTS)
                        chain(dve.tensor_tensor(pv[:].rearrange("p a (h d) -> p a h d", h=POINTS), values,
                                                s.unsqueeze(3).to_broadcast([128, POINTS, POINTS, DH]), ALU.mult))
                        chain(dve.reduce_sum(y[:, t], pv[:].rearrange("p a c -> p c a"), axis=AX))
                        yt = y[:, t].rearrange("p (h d) -> p h d", h=POINTS)
                        dve.tensor_tensor(yt, yt, spread(z[:], [128, POINTS, DH]), ALU.mult).then_inc(s_v, 1)

                    dve.wait_ge(s_in, 48)
                    for t in range(TILES + 2):
                        if t < TILES:
                            weight(t)
                        if 1 <= t < TILES + 1:
                            score(t - 1)
                            mix(t - 1)
            k.rewind()



LAYERS = 6
TT = BATCH * NTXT // 128
PER = 128 // NTXT
HID = 256
NPOS = NIMG


def text_tokens(nc, w, h_out):
    with ExitStack() as ctx:
        k = Space(nc, ctx, "t")
        eye = k.sb("eye", [128, 128])
        heads = k.sb("heads", [C, HEADS])
        alibi = k.sb("alibi", [128, HEADS, NTXT])
        tok = k.sb("tok", [128, TT], I32)
        pos = k.sb("pos", [128, 1], I32)
        emb = k.sb("emb", [128, TT, C])
        table = k.sb("table", [128, C])
        iw = k.sb("iw", [128, 1])
        pw = k.sb("pw", [128, 1])
        lnf = k.sb("lnf", [128, 2, C])
        lnw = k.sb("lnw", [128, 4, C])
        w1 = k.sb("w1", [C + 1, HID])
        w2 = k.sb("w2", [128, 2, C])
        b2 = k.sb("b2", [128, C])
        x = k.sb("x", [128, TT, C])
        xc = k.sb("xc", [128, TT, C])
        xn = k.sb("xn", [128, TT, HEADS, DH + 1])
        sq = k.sb("sq", [128, TT, C])
        mu = k.sb("mu", [128, TT])
        var = k.sb("var", [128, TT])
        std = k.sb("std", [128, TT])
        xt = k.sb("xt", [C + 1, TT * 128])
        xm = k.sb("xm", [C, TT * PER, HEADS, NTXT])
        sc = k.sb("sc", [128, TT, HEADS, NTXT])
        mx = k.sb("mx", [128, TT, HEADS])
        pbd = k.sb("pbd", [128, TT, HEADS, 128])
        pt = k.sb("pt", [128, TT, HEADS, 128])
        z = k.sb("z", [128, TT, HEADS])
        av = k.sb("av", [128, TT, C])
        hid = k.sb("hid", [128, 2, TT * 128])
        ps_a = k.ps("ps_a", [128, 512])
        ps_s = k.ps("ps_s", [128, TT, HEADS * NTXT])
        ps_t = k.ps("ps_t", [128, 2, 512])
        ps_o = k.ps("ps_o", [128, TT, 128])
        ps_h = k.ps("ps_h", [128, 2, 512])
        s_w = k.sem("weights_in")
        s_chain = k.sem("dve_step")
        s_pchain = k.sem("pool_step")
        s_idx = k.sem("tokens_in")
        s_emb = k.gather_sem("embedded")
        s_lw = k.sem("layer_weights_in")
        s_var = k.sem("variance")
        s_std = k.sem("deviation")
        s_n = k.sem("normed")
        s_x = k.sem("normed_turned")
        s_xk = k.sem("normed_turned_kept")
        s_m = k.sem("heads_masked")
        s_s = k.sem("scores")
        s_sub = k.sem("scores_shifted")
        s_e = k.sem("exponents")
        s_pt = k.sem("exponents_turned")
        s_ptk = k.sem("exponents_turned_kept")
        s_o = k.sem("attended")
        s_h = k.sem("hidden")
        s_g = k.sem("gelu")
        s_y = k.sem("hidden_projected")
        s_done = k.sem("done")
        s_out = k.sem("rows_out")

        with nc.Block() as block:
            @block.sync
            def _(sp):
                sp.dma_start(tok[:], w["x_txt"]).then_inc(s_idx, 16)
                for n in range(PER):
                    sp.dma_start(pos[NTXT * n:NTXT * n + NTXT], w["pos_S"]).then_inc(s_idx, 16)
                sp.dma_start(eye[:], w["eye"]).then_inc(s_w, 16)
                sp.dma_start(heads[:], w["t_heads"]).then_inc(s_w, 16)
                sp.dma_start(alibi[:], w["t_alibi"]).then_inc(s_w, 16)
                sp.dma_start(iw[:], w["t_iw"].partition_broadcast(128)).then_inc(s_w, 16)
                sp.dma_start(pw[:], w["t_pw"].partition_broadcast(128)).then_inc(s_w, 16)
                sp.dma_start(lnf[:, 0], w["t_lnfw"].partition_broadcast(128)).then_inc(s_w, 16)
                sp.dma_start(lnf[:, 1], w["t_lnfb"].partition_broadcast(128)).then_inc(s_w, 16)
                sp.wait_ge(s_w, 112)

            @block.gpsimd
            def _(pool):
                chain = Chain(pool, s_pchain)
                chain(pool.memset(pbd[:], 0.0))
                chain(pool.memset(xt[C:C + 1], 1.0))
                chain(pool.memset(xn[:, :, :, DH:], 1.0))
                pool.wait_ge(s_idx, 16 * (1 + PER))
                for t in range(TT):
                    pool.indirect_dma_start(emb[:, t], None, w["t_emb"],
                                            bass.IndirectOffsetOnAxis(ap=tok[:, t:t + 1], axis=0)).then_inc(s_emb, 16)
                pool.indirect_dma_start(table[:], None, w["t_table"],
                                        bass.IndirectOffsetOnAxis(ap=pos[:, 0:1], axis=0)).then_inc(s_emb, 16)
                pool.wait_ge(s_emb, 16 * (TT + 1))

            @block.vector
            def _(dve):
                chain = Chain(dve, s_chain)
                dve.wait_ge(s_w, 112)
                dve.wait_ge(s_emb, 16 * (TT + 1))
                chain(dve.tensor_scalar(table[:], table[:], pw[:, 0:1], None, ALU.mult))
                chain(dve.tensor_scalar(emb[:], emb[:], iw[:, 0:1], None, ALU.mult))
                chain(dve.tensor_tensor(x[:], emb[:], table[:].unsqueeze(1).to_broadcast([128, TT, C]), ALU.add))
        k.rewind()

        with nc.Fori(0, LAYERS) as layer:
            with nc.Block() as block:
                @block.sync
                def _(sp):
                    one = bass.ds(layer, 1)
                    for m, name in enumerate(("t_ln1w", "t_ln1b", "t_ln2w", "t_ln2b")):
                        sp.dma_start(lnw[:, m], w[name][one, :].rearrange("a c -> (a c)").partition_broadcast(128)).then_inc(s_lw, 16)
                    sp.dma_start(w1[:], w["t_w1"][bass.ds(layer * (C + 1), C + 1), :]).then_inc(s_lw, 16)
                    sp.dma_start(w2[:], w["t_w2"][bass.ds(layer * HID, HID), :].rearrange("(a p) c -> p a c", a=2)).then_inc(s_lw, 16)
                    sp.dma_start(b2[:], w["t_b2"][one, :].rearrange("a c -> (a c)").partition_broadcast(128)).then_inc(s_lw, 16)
                    sp.wait_ge(s_lw, 112)

                @block.tensor
                def _(pe):
                    pe.wait_ge(s_n, 1)
                    for t in range(TT):
                        last = pe.transpose(ps_a[0:C, 128 * t:128 * t + 128], xc[:, t], eye[:])
                    last.then_inc(s_x, 1)
                    pe.wait_ge(s_m, HEADS)
                    for t in range(TT):
                        for n in range(PER):
                            j = PER * t + n
                            last = pe.matmul(ps_s[NTXT * n:NTXT * n + NTXT, t], xt[0:C, NTXT * j:NTXT * j + NTXT],
                                             xm[:, j].rearrange("p h s -> p (h s)"), start=True, stop=True,
                                             tile_position=(0, NTXT * n))
                    last.then_inc(s_s, 1)
                    pe.wait_ge(s_e, PER)
                    for i in range(2 * TT):
                        if i >= 2:
                            pe.wait_ge(s_ptk, i - 1)
                        for h in range(4):
                            last = pe.transpose(ps_t[:, i % 2, 128 * h:128 * h + 128], pbd[:, i // 2, 4 * (i % 2) + h], eye[:])
                        last.then_inc(s_pt, 1)
                    pe.wait_ge(s_ptk, 2 * TT)
                    for t in range(TT):
                        for h in range(HEADS):
                            last = pe.matmul(ps_o[:, t, (DH + 1) * h:(DH + 1) * h + DH + 1], pt[:, t, h], xn[:, t, h], start=True, stop=True)
                    last.then_inc(s_o, 1)
                    pe.wait_ge(s_n, 2)
                    for t in range(TT):
                        last = pe.transpose(ps_a[0:C, 128 * t:128 * t + 128], xc[:, t], eye[:])
                    last.then_inc(s_x, 1)
                    pe.wait_ge(s_xk, 2)
                    pe.wait_ge(s_lw, 112)
                    for a in range(2):
                        pe.matmul(ps_h[:, a], w1[:, 128 * a:128 * a + 128], xt[:], start=True, stop=True).then_inc(s_h, 1)
                    pe.wait_ge(s_g, 2)
                    for t in range(TT):
                        for a in range(2):
                            last = pe.matmul(ps_t[:, 0, C * t:C * t + C], hid[:, a, 128 * t:128 * t + 128], w2[:, a], start=a == 0, stop=a == 1)
                    last.then_inc(s_y, 1)

                @block.scalar
                def _(act):
                    act.wait_ge(s_var, 1)
                    act.activation(std[:], var[:], ACT.Sqrt).then_inc(s_std, 1)
                    act.wait_ge(s_sub, 1)
                    for n in range(PER):
                        rows = slice(NTXT * n, NTXT * n + NTXT)
                        act.activation(pbd[rows, :, :, rows], sc[rows], ACT.Exp).then_inc(s_e, 1)
                    act.wait_ge(s_var, 2)
                    act.activation(std[:], var[:], ACT.Sqrt).then_inc(s_std, 1)
                    for a in range(2):
                        act.wait_ge(s_h, a + 1)
                        act.activation(hid[:, a], ps_h[:, a], ACT.Gelu).then_inc(s_g, 1)

                @block.vector
                def _(dve):
                    chain = Chain(dve, s_chain)

                    def norm(m):
                        layer_norm(dve, chain, x[:], xc[:], sq[:], mu[:], var[:], std[:], s_var, s_std, LN_EPS, n_var=m + 1)
                        every = lambda u: lnw[:, u].unsqueeze(1).to_broadcast([128, TT, C])
                        chain(dve.tensor_tensor(xc[:], xc[:], every(2 * m), ALU.mult))
                        dve.tensor_tensor(xc[:], xc[:], every(2 * m + 1), ALU.add).then_inc(s_n, 1)

                    dve.wait_ge(s_lw, 112)
                    norm(0)
                    dve.wait_ge(s_n, 1)
                    chain(dve.tensor_copy(xn[:, :, :, 0:DH], xc[:].rearrange("p t (h d) -> p t h d", h=HEADS)))
                    dve.wait_ge(s_x, 1)
                    dve.tensor_copy(xt[0:C], ps_a[0:C]).then_inc(s_xk, 1)
                    dve.wait_ge(s_xk, 1)
                    rows = xt[0:C].rearrange("p (j s) -> p j s", s=NTXT)
                    for h in range(HEADS):
                        dve.tensor_scalar(xm[:, :, h], rows, heads[:, h:h + 1], None, ALU.mult).then_inc(s_m, 1)
                    dve.wait_ge(s_s, 1)
                    for t in range(TT):
                        last = dve.scalar_tensor_tensor(sc[:, t].rearrange("p h s -> p (h s)"), ps_s[:, t], float(DH) ** -0.5,
                                                        alibi[:].rearrange("p h s -> p (h s)"), ALU.mult, ALU.add)
                    chain(last)
                    chain(dve.reduce_max(mx[:], sc[:], axis=AX))
                    dve.tensor_tensor(sc[:], sc[:], spread(mx[:], [128, TT, HEADS, NTXT]), ALU.subtract).then_inc(s_sub, 1)
                    for i in range(2 * TT):
                        dve.wait_ge(s_pt, i + 1)
                        dve.tensor_copy(pt[:, i // 2, 4 * (i % 2):4 * (i % 2) + 4].rearrange("p h n -> p (h n)"), ps_t[:, i % 2]).then_inc(s_ptk, 1)
                    dve.wait_ge(s_o, 1)
                    for t in range(TT):
                        both = ps_o[:, t, 0:HEADS * (DH + 1)].rearrange("p (h d) -> p h d", h=HEADS)
                        last = dve.reciprocal(z[:, t], both[:, :, DH])
                    chain(last)
                    for t in range(TT):
                        both = ps_o[:, t, 0:HEADS * (DH + 1)].rearrange("p (h d) -> p h d", h=HEADS)
                        last = dve.tensor_tensor(av[:, t].rearrange("p (h d) -> p h d", h=HEADS), both[:, :, 0:DH],
                                                 spread(z[:, t], [128, HEADS, DH]), ALU.mult)
                    chain(last)
                    chain(dve.tensor_tensor(x[:], x[:], av[:], ALU.add))
                    norm(1)
                    dve.wait_ge(s_x, 2)
                    dve.tensor_copy(xt[0:C], ps_a[0:C]).then_inc(s_xk, 1)
                    chain(dve.tensor_tensor(x[:], x[:], b2[:].unsqueeze(1).to_broadcast([128, TT, C]), ALU.add))
                    dve.wait_ge(s_y, 1)
                    chain(dve.tensor_tensor(x[:].rearrange("p t c -> p (t c)"), x[:].rearrange("p t c -> p (t c)"), ps_t[:, 0, 0:TT * C], ALU.add))
            k.rewind()

        with nc.Block() as block:
            @block.scalar
            def _(act):
                act.wait_ge(s_var, 1)
                act.activation(std[:], var[:], ACT.Sqrt).then_inc(s_std, 1)

            @block.vector
            def _(dve):
                chain = Chain(dve, s_chain)
                layer_norm(dve, chain, x[:], xc[:], sq[:], mu[:], var[:], std[:], s_var, s_std, LN_EPS)
                chain(dve.tensor_tensor(xc[:], xc[:], lnf[:, 0].unsqueeze(1).to_broadcast([128, TT, C]), ALU.mult))
                dve.tensor_tensor(xc[:], xc[:], lnf[:, 1].unsqueeze(1).to_broadcast([128, TT, C]), ALU.add).then_inc(s_done, 1)

            @block.sync
            def _(sp):
                sp.wait_ge(s_done, 1)
                for j in range(TT * PER):
                    n = j % PER
                    sp.dma_start(h_out[SEQ * j + NIMG:SEQ * (j + 1), :], xc[NTXT * n:NTXT * n + NTXT, j // PER]).then_inc(s_out, 16)
                sp.wait_ge(s_out, 16 * TT * PER)
        k.rewind()



KEEP = SEQ // 2
ROUNDS = 26
PIECE = 352
DVE_TILES = (0, 1, 2, 3)
ACT_TILES = ((4, 5), (6, 7, 8))


def height(t):
    return TAIL if t == NT - 1 else 128


def l0_attention(nc, w, h_in, h_out):
    with ExitStack() as ctx:
        k = Space(nc, ctx, "c")
        wqk = k.sb("wqk", [C + 1, 2, 128])
        wvt = k.sb("wvt", [C, C + 1])
        wout = k.sb("wout", [C, C])
        wvo = k.sb("wvo", [C + 1, C])
        bout = k.sb("bout", [128, C])
        eye = k.sb("eye", [128, 128])
        x = k.sb("x", [128, NT, C])
        xn = k.sb("xn", [128, NT, C])
        sq = k.sb("sq", [128, NT, C])
        y = k.sb("y", [128, NT, C])
        mu = k.sb("mu", [128, NT])
        var = k.sb("var", [128, NT])
        std = k.sb("std", [128, NT])
        xt = k.sb("xt", [C + 1, SEQ])
        qt = k.sb("qt", [128, SEQ])
        kt = k.sb("kt", [128, SEQ])
        v = k.sb("v", [128, NT, C])
        s = k.sb("s", [128, NT, SEQ])
        top = k.sb("top", [128, NT])
        low = k.sb("low", [128, NT])
        rng = k.sb("rng", [128, NT])
        base = k.sb("base", [128, NT])
        cand = k.sb("cand", [128, NT])
        cnt = k.sb("cnt", [128, NT])
        hit = k.sb("hit", [128, NT])
        nshift = k.sb("nshift", [128, NT])
        z = k.sb("z", [128, NT])
        junk_d = k.sb("junk_d", [128, 4, SEQ], BF16)
        junk_a = k.sb("junk_a", [128, 5, SEQ], BF16)
        pt = k.sb("pt", [128, 2, NT, 128])
        ps_s = k.ps("ps_s", [128, 2, 3, 512])
        ps_m = k.ps("ps_m", [128, 2, 512])
        s_w = k.sem("weights_in")
        s_chain = k.sem("dve_step")
        s_pchain = k.sem("pool_step")
        s_wv = k.sem("value_weights_made")
        s_x = k.sem("rows_in")
        s_var = k.sem("variance")
        s_std = k.sem("deviation")
        s_tr = k.sem("transposed")
        s_xt = k.sem("transposes_kept")
        s_q = k.sem("queries")
        s_qt = k.sem("queries_kept")
        s_k = k.sem("keys")
        s_kt = k.sem("keys_kept")
        s_v = k.sem("values")
        s_vk = k.sem("values_kept")
        s_s = k.sem("scores")
        s_sk = k.sem("scores_kept")
        s_low = k.sem("lowest_scores")
        s_rng = k.sem("intervals")
        s_cd = k.sem("dve_counts")
        s_ca = [k.sem("act_counts_0"), k.sem("act_counts_1")]
        s_up = [k.sem("act_candidates_0"), k.sem("act_candidates_1")]
        s_mask = k.sem("scores_masked")
        s_ns = k.sem("shifts")
        s_p = k.sem("probabilities")
        s_pt = k.sem("probabilities_transposed")
        s_ptd = k.sem("transposes_kept_dve")
        s_pta = k.sem("transposes_kept_act")
        s_o = k.sem("outputs")
        s_y = k.sem("rows_done")
        s_out = k.sem("rows_out")

        with nc.Block() as block:
            @block.sync
            def _(sp):
                sp.dma_start(wqk[:, :, 0:C], w["c_wqk"]).then_inc(s_w, 16)
                sp.dma_start(wvt[:], w["c_wvt"]).then_inc(s_w, 16)
                sp.dma_start(wout[:], w["c_wout"]).then_inc(s_w, 16)
                sp.dma_start(bout[:], w["c_bout"].partition_broadcast(128)).then_inc(s_w, 16)
                sp.dma_start(eye[:], w["eye"]).then_inc(s_w, 16)
                sp.wait_ge(s_w, 80)

            @block.gpsimd
            def _(pool):
                chain = Chain(pool, s_pchain)
                chain(pool.memset(wqk[:, :, C:128], 0.0))
                chain(pool.memset(x[:], 0.0))
                chain(pool.memset(xt[C:C + 1], 1.0))
                chain(pool.memset(top[:], 0.0))
                chain(pool.memset(low[:], 0.0))
                chain(pool.memset(cnt[:], 0.0))
                chain(pool.memset(z[:], 1.0))

            @block.tensor
            def _(pe):
                pe.wait_ge(s_w, 80)
                pe.matmul(ps_m[0:C + 1, 0, 0:C], wvt[:], wout[:], start=True, stop=True).then_inc(s_wv, 1)

            @block.vector
            def _(dve):
                dve.wait_ge(s_wv, 1)
                dve.tensor_copy(wvo[:], ps_m[0:C + 1, 0, 0:C])
        k.rewind()

        with nc.Fori(0, BATCH) as b:
            with nc.Block() as block:
                @block.sync
                def _(sp):
                    sp.dma_start(x[:, 0:8], h_in[bass.ds(b * SEQ, NIMG), :].rearrange("(t p) c -> p t c", p=128)).then_inc(s_x, 16)
                    sp.dma_start(x[0:TAIL, 8], h_in[bass.ds(b * SEQ + NIMG, TAIL), :]).then_inc(s_x, 16)
                    sp.wait_ge(s_y, NT)
                    sp.dma_start(h_out[bass.ds(b * SEQ, NIMG), :].rearrange("(t p) c -> p t c", p=128), y[:, 0:8]).then_inc(s_out, 16)
                    sp.dma_start(h_out[bass.ds(b * SEQ + NIMG, TAIL), :], y[0:TAIL, 8]).then_inc(s_out, 16)
                    sp.wait_ge(s_out, 32)

                @block.tensor
                def _(pe):
                    pe.wait_ge(s_chain, 7)
                    for t in range(NT):
                        n = height(t)
                        last = pe.transpose(ps_s[0:C, 0, t // 4, 128 * (t % 4):128 * (t % 4) + n], xn[0:n, t, :], eye[0:n, 0:n])
                    last.then_inc(s_tr, 1)
                    pe.wait_ge(s_xt, 1)
                    for c in range(3):
                        last = pe.matmul(ps_s[:, 1, c, 0:PIECE], wqk[:, 0], xt[:, PIECE * c:PIECE * (c + 1)], start=True, stop=True)
                    last.then_inc(s_q, 1)
                    for c in range(3):
                        last = pe.matmul(ps_s[:, 0, c, 0:PIECE], wqk[:, 1], xt[:, PIECE * c:PIECE * (c + 1)], start=True, stop=True)
                    last.then_inc(s_k, 1)
                    for t in range(NT):
                        n = height(t)
                        last = pe.matmul(ps_m[0:n, t // 5, C * (t % 5):C * (t % 5) + C], xt[:, 128 * t:128 * t + n], wvo[:], start=True, stop=True)
                    last.then_inc(s_v, 1)
                    pe.wait_ge(s_qt, 1)
                    pe.wait_ge(s_kt, 1)
                    for t in range(NT):
                        n = height(t)
                        if t >= 2:
                            pe.wait_ge(s_sk, t - 1)
                        for c in range(3):
                            last = pe.matmul(ps_s[0:n, t % 2, c, 0:PIECE], qt[:, 128 * t:128 * t + n],
                                             kt[:, PIECE * c:PIECE * (c + 1)], start=True, stop=True)
                        last.then_inc(s_s, 1)
                    pe.wait_ge(s_sk, NT)

                    def transpose_probabilities(t):
                        n = height(t)
                        pe.wait_ge(s_p, t + 1)
                        if t >= 2:
                            pe.wait_ge(s_ptd, t - 1)
                            pe.wait_ge(s_pta, t - 1)
                        for c in range(NT):
                            m = height(c)
                            last = pe.transpose(ps_s[0:m, t % 2, c // 4, 128 * (c % 4):128 * (c % 4) + n],
                                                s[0:n, t, 128 * c:128 * c + m], eye[0:n, 0:n])
                        last.then_inc(s_pt, 1)

                    def mix(t):
                        n = height(t)
                        pe.wait_ge(s_ptd, t + 1)
                        pe.wait_ge(s_pta, t + 1)
                        if t == 0:
                            pe.wait_ge(s_vk, 1)
                        if t >= 2:
                            pe.wait_ge(s_y, t - 1)
                        for c in range(NT):
                            m = height(c)
                            last = pe.matmul(ps_m[0:n, t % 2, 0:C], pt[0:m, t % 2, c, 0:n], v[0:m, c], start=c == 0, stop=c == NT - 1)
                        last.then_inc(s_o, 1)

                    transpose_probabilities(0)
                    for t in range(NT):
                        if t + 1 < NT:
                            transpose_probabilities(t + 1)
                        mix(t)

                @block.vector
                def _(dve):
                    chain = Chain(dve, s_chain)
                    dve.wait_ge(s_x, 32)
                    layer_norm(dve, chain, x[:], xn[:], sq[:], mu[:], var[:], std[:], s_var, s_std, LN_EPS)
                    dve.wait_ge(s_tr, 1)
                    dve.tensor_copy(xt[0:C, 0:NIMG], ps_s[0:C, 0, 0:2, :])
                    dve.tensor_copy(xt[0:C, NIMG:SEQ], ps_s[0:C, 0, 2, 0:TAIL]).then_inc(s_xt, 1)
                    dve.wait_ge(s_k, 1)
                    dve.tensor_copy(kt[:], ps_s[:, 0, :, 0:PIECE]).then_inc(s_kt, 1)
                    dve.wait_ge(s_v, 1)
                    dve.tensor_copy(v[:, 0:5], ps_m[:, 0, 0:5 * C].rearrange("p (t c) -> p t c", c=C))
                    dve.tensor_copy(v[:, 5:8], ps_m[:, 1, 0:3 * C].rearrange("p (t c) -> p t c", c=C))
                    dve.tensor_copy(v[0:TAIL, 8], ps_m[0:TAIL, 1, 3 * C:4 * C]).then_inc(s_vk, 1)
                    for t in range(NT):
                        n = height(t)
                        dve.wait_ge(s_s, t + 1)
                        dve.tensor_scalar(s[0:n, t], ps_s[0:n, t % 2, :, 0:PIECE], 0.125, None, ALU.mult, ALU.max,
                                          accum_out=top[0:n, t:t + 1]).then_inc(s_sk, 1)
                        dve.wait_ge(s_sk, t + 1)
                        chain(dve.tensor_reduce(low[0:n, t:t + 1], s[0:n, t], axis=AX, op=ALU.min))
                    dve.tensor_scalar(nshift[:], top[:], 0.0, -1.0, ALU.max, ALU.mult).then_inc(s_ns, 1)
                    chain(dve.tensor_tensor(rng[:], top[:], low[:], ALU.subtract))
                    dve.scalar_tensor_tensor(cand[:], rng[:], 0.5, low[:], ALU.mult, ALU.add).then_inc(s_rng, 1)
                    dve.wait_ge(s_rng, 1)
                    d = slice(0, len(DVE_TILES))
                    for r in range(ROUNDS):
                        for t in DVE_TILES:
                            dve.tensor_scalar(junk_d[:, t], s[:, t], cand[:, t:t + 1], None, ALU.is_ge, ALU.add,
                                              accum_out=cnt[:, t:t + 1]).then_inc(s_cd, 1)
                        dve.wait_ge(s_cd, 4 * (r + 1))
                        chain(dve.scalar_tensor_tensor(hit[:, d], cnt[:, d], float(KEEP), rng[:, d], ALU.is_ge, ALU.mult))
                        chain(dve.scalar_tensor_tensor(low[:, d], hit[:, d], 0.5 ** (r + 1), low[:, d], ALU.mult, ALU.add))
                        if r + 1 < ROUNDS:
                            chain(dve.scalar_tensor_tensor(cand[:, d], rng[:, d], 0.5 ** (r + 2), low[:, d], ALU.mult, ALU.add))
                    for t in range(NT):
                        n = height(t)
                        for g, tiles in enumerate(ACT_TILES):
                            if t == tiles[0]:
                                dve.wait_ge(s_up[g], 4 * ROUNDS)
                        dve.scalar_tensor_tensor(s[0:n, t], s[0:n, t], low[0:n, t:t + 1], s[0:n, t], ALU.is_ge, ALU.mult).then_inc(s_mask, 1)

                    def finish(t):
                        n = height(t)
                        dve.wait_ge(s_p, t + 1)
                        chain(dve.reciprocal(z[0:n, t:t + 1], z[0:n, t:t + 1]))
                        dve.wait_ge(s_o, t + 1)
                        dve.scalar_tensor_tensor(y[0:n, t], ps_m[0:n, t % 2, 0:C], z[0:n, t:t + 1], y[0:n, t], ALU.mult, ALU.add).then_inc(s_y, 1)

                    for t in range(NT):
                        n = height(t)
                        if t == 0:
                            dve.wait_ge(s_x, 32)
                            chain(dve.tensor_tensor(y[:], x[:], bout[:].unsqueeze(1).to_broadcast([128, NT, C]), ALU.add))
                        dve.wait_ge(s_pt, t + 1)
                        if t >= 2:
                            dve.wait_ge(s_o, t - 1)
                        dve.tensor_copy(pt[:, t % 2, 0:4, 0:n], ps_s[:, t % 2, 0, :].rearrange("p (c s) -> p c s", c=4)[:, :, 0:n]).then_inc(s_ptd, 1)
                        if t >= 1:
                            finish(t - 1)
                    finish(NT - 1)

                @block.gpsimd
                def _(pool):
                    pool.wait_ge(s_rng, 1)
                    for r in range(ROUNDS):
                        for g, tiles in enumerate(ACT_TILES):
                            a = slice(tiles[0], tiles[-1] + 1)
                            n = 4 * r
                            pool.wait_ge(s_ca[g], len(tiles) * (r + 1))
                            pool.tensor_scalar(hit[:, a], cnt[:, a], 0.0, 0.5 ** (r + 1), ALU.is_le, ALU.mult).then_inc(s_up[g], 1)
                            pool.wait_ge(s_up[g], n + 1)
                            pool.tensor_tensor(hit[:, a], hit[:, a], rng[:, a], ALU.mult).then_inc(s_up[g], 1)
                            pool.wait_ge(s_up[g], n + 2)
                            pool.tensor_tensor(low[:, a], low[:, a], hit[:, a], ALU.add).then_inc(s_up[g], 1)
                            pool.tensor_scalar(base[:, a], rng[:, a], 0.5 ** (r + 2), None, ALU.mult).then_inc(s_pchain, 1)
                            pool.wait_ge(s_up[g], n + 3)
                            pool.wait_ge(s_pchain, 2 * r + g + 1)
                            pool.tensor_tensor(cand[:, a], base[:, a], low[:, a], ALU.add).then_inc(s_up[g], 1)

                @block.scalar
                def _(act):
                    act.wait_ge(s_var, 1)
                    act.activation(std[:], var[:], ACT.Sqrt).then_inc(s_std, 1)
                    act.wait_ge(s_q, 1)
                    act.activation(qt[:], ps_s[:, 1, :, 0:PIECE], ACT.Copy).then_inc(s_qt, 1)
                    act.wait_ge(s_rng, 1)
                    for r in range(ROUNDS):
                        for g, tiles in enumerate(ACT_TILES):
                            if r:
                                act.wait_ge(s_up[g], 4 * r)
                            for t in tiles:
                                n = height(t)
                                act.activation(junk_a[0:n, t - 4], s[0:n, t], ACT.Sign, bias=cand[0:n, t:t + 1], scale=-1.0,
                                               accum_out=cnt[0:n, t:t + 1]).then_inc(s_ca[g], 1)
                    act.wait_ge(s_ns, 1)

                    def keep_transposes(t):
                        n = height(t)
                        act.wait_ge(s_pt, t + 1)
                        if t >= 2:
                            act.wait_ge(s_o, t - 1)
                        act.activation(pt[:, t % 2, 4:8, 0:n], ps_s[:, t % 2, 1, :].rearrange("p (c s) -> p c s", c=4)[:, :, 0:n], ACT.Copy)
                        act.activation(pt[0:TAIL, t % 2, 8, 0:n], ps_s[0:TAIL, t % 2, 2, 0:n], ACT.Copy).then_inc(s_pta, 1)

                    for t in range(NT):
                        n = height(t)
                        act.wait_ge(s_mask, t + 1)
                        act.activation(s[0:n, t], s[0:n, t], ACT.Exp, bias=nshift[0:n, t:t + 1], accum_out=z[0:n, t:t + 1]).then_inc(s_p, 1)
                        if t >= 1:
                            keep_transposes(t - 1)
                    keep_transposes(NT - 1)
            k.rewind()



NH = 4
NE = 4
D = C // NH
QK = NE * D + D
VS = D + 1
NEG = -1e30
STACK_Q = (0, 0, 0, 1, 1, 2)
STACK_K = (0, 1, 2, 0, 1, 0)
DEPTH = len(STACK_Q) * D
SHIFT = 3
FFN_EPS = 1e-8


def ffn_project(nc, w, h_in, qk3, vals, sxn):
    with ExitStack() as ctx:
        k = Space(nc, ctx, "g")
        hlt = k.sb("hlt", [D, NH, C + 1])
        wqk = k.sb("wqk", [D, NH, QK])
        wv = k.sb("wv", [D, NH, D])
        a_qk = k.sb("a_qk", [C + 1, NH, QK])
        a_sv = k.sb("a_sv", [C + 1, 2, C])
        eye = k.sb("eye", [128, 128])
        x = k.sb("x", [128, NT, C])
        xn = k.sb("xn", [128, NT, C])
        sq = k.sb("sq", [128, NT, C])
        mu = k.sb("mu", [128, NT])
        var = k.sb("var", [128, NT])
        std = k.sb("std", [128, NT])
        xt = k.sb("xt", [C + 1, SEQ])
        sv = k.sb("sv", [128, NT, 2, C])
        hi = k.sb("hi", [QK, 2, SEQ], BF16)
        rest = k.sb("rest", [QK, 2, SEQ])
        mid = k.sb("mid", [QK, 2, SEQ], BF16)
        lo = k.sb("lo", [QK, 2, SEQ], BF16)
        ps_s = k.ps("ps_s", [128, 2, 3, 512])
        ps_m = k.ps("ps_m", [128, 2, 512])
        s_w = k.sem("weights_in")
        s_chain = k.sem("dve_step")
        s_pchain = k.sem("pool_step")
        s_mm = k.sem("weights_multiplied")
        s_x = k.sem("rows_in")
        s_var = k.sem("variance")
        s_std = k.sem("deviation")
        s_tr = k.sem("transposed")
        s_xt = k.sem("transposes_kept")
        s_sv = k.sem("values")
        s_svk = k.sem("values_kept")
        s_p = k.sem("projections")
        s_hi = k.sem("high_parts")
        s_rest = k.sem("remainders")
        s_mid = k.sem("middle_parts")
        s_lo = k.sem("low_parts")
        s_out = k.sem("values_out")
        s_o = [k.sem("parts_out_0"), k.sem("parts_out_1")]

        with nc.Block() as block:
            @block.sync
            def _(sp):
                for dst, name in ((hlt, "g_hlt"), (wqk, "g_wqk"), (wv, "g_wv"), (eye, "eye")):
                    sp.dma_start(dst[:], w[name]).then_inc(s_w, 16)
                sp.dma_start(a_sv[:, 0], w["g_hl"]).then_inc(s_w, 16)
                sp.wait_ge(s_w, 80)

            @block.gpsimd
            def _(pool):
                chain = Chain(pool, s_pchain)
                chain(pool.memset(x[:], 0.0))
                chain(pool.memset(xt[C:C + 1], 1.0))

            @block.tensor
            def _(pe):
                pe.wait_ge(s_w, 80)
                for n in range(NH):
                    pe.matmul(ps_s[0:C + 1, 0, 0, QK * n:QK * n + QK], hlt[:, n], wqk[:, n], start=True, stop=True)
                    last = pe.matmul(ps_s[0:C + 1, 0, 1, D * n:D * n + D], hlt[:, n], wv[:, n], start=True, stop=True)
                last.then_inc(s_mm, 1)

            @block.vector
            def _(dve):
                dve.wait_ge(s_mm, 1)
                p = ps_s[0:C + 1, 0, 0, 0:NH * QK].rearrange("p (n m) -> p n m", n=NH)
                dve.tensor_scalar(a_qk[:, :, 0:NE * D], p[:, :, 0:NE * D], float(D) ** 0.5, None, ALU.mult)
                dve.tensor_copy(a_qk[:, :, NE * D:QK], p[:, :, NE * D:QK])
                dve.tensor_copy(a_sv[:, 1], ps_s[0:C + 1, 0, 1, 0:C])
        k.rewind()

        with nc.Fori(0, BATCH) as b:
            with nc.Block() as block:
                @block.sync
                def _(sp):
                    sp.dma_start(x[:, 0:8], h_in[bass.ds(b * SEQ, NIMG), :].rearrange("(t p) c -> p t c", p=128)).then_inc(s_x, 16)
                    sp.dma_start(x[0:TAIL, 8], h_in[bass.ds(b * SEQ + NIMG, TAIL), :]).then_inc(s_x, 16)
                    sp.wait_ge(s_svk, 3)
                    for dst, which in ((sxn, 0), (vals, 1)):
                        sp.dma_start(dst[bass.ds(b * SEQ, NIMG), :].rearrange("(t p) c -> p t c", p=128), sv[:, 0:8, which]).then_inc(s_out, 16)
                        sp.dma_start(dst[bass.ds(b * SEQ + NIMG, TAIL), :], sv[0:TAIL, 8, which]).then_inc(s_out, 16)
                    for n in range(NH):
                        for part, src, done in ((0, hi, s_hi), (1, mid, s_mid), (2, lo, s_lo)):
                            sp.wait_ge(done, n + 1)
                            row = b * (NH * 3 * QK) + (n * 3 + part) * QK
                            sp.dma_start(qk3[bass.ds(row, QK), :], src[:, n % 2]).then_inc(s_o[n % 2], 16)
                    sp.wait_ge(s_out, 64)
                    for o in s_o:
                        sp.wait_ge(o, 96)

                @block.tensor
                def _(pe):
                    pe.wait_ge(s_chain, 7)
                    for t in range(NT):
                        n = height(t)
                        last = pe.transpose(ps_s[0:C, 0, t // 4, 128 * (t % 4):128 * (t % 4) + n], xn[0:n, t, :], eye[0:n, 0:n])
                    last.then_inc(s_tr, 1)
                    pe.wait_ge(s_xt, 1)
                    for n in range(NH):
                        if n >= 2:
                            pe.wait_ge(s_hi, n - 1)
                            pe.wait_ge(s_rest, n - 1)
                        for c in range(3):
                            last = pe.matmul(ps_s[0:QK, n % 2, c, 0:PIECE], a_qk[:, n], xt[:, PIECE * c:PIECE * (c + 1)], start=True, stop=True)
                        last.then_inc(s_p, 1)
                        if n == 1:
                            for t in range(NT):
                                m = height(t)
                                if t in (4, 8):
                                    pe.wait_ge(s_svk, t // 4)
                                last = pe.matmul(ps_m[0:m, (t // 4) % 2, 128 * (t % 4):128 * (t % 4) + 128], xt[:, 128 * t:128 * t + m],
                                                 a_sv[:].rearrange("p a c -> p (a c)"), start=True, stop=True)
                                if t % 4 == 3 or t == NT - 1:
                                    last.then_inc(s_sv, 1)

                @block.vector
                def _(dve):
                    chain = Chain(dve, s_chain)
                    dve.wait_ge(s_x, 32)
                    layer_norm(dve, chain, x[:], xn[:], sq[:], mu[:], var[:], std[:], s_var, s_std, LN_EPS)
                    dve.wait_ge(s_tr, 1)
                    dve.tensor_copy(xt[0:C, 0:NIMG], ps_s[0:C, 0, 0:2, :])
                    dve.tensor_copy(xt[0:C, NIMG:SEQ], ps_s[0:C, 0, 2, 0:TAIL]).then_inc(s_xt, 1)
                    for n in range(NH):
                        dve.wait_ge(s_hi, n + 1)
                        if n >= 2:
                            dve.wait_ge(s_lo, n - 1)
                        dve.tensor_tensor(rest[:, n % 2], ps_s[0:QK, n % 2, :, 0:PIECE], hi[:, n % 2].rearrange("p (c s) -> p c s", c=3),
                                          ALU.subtract).then_inc(s_rest, 1)
                        if n == 1:
                            for i in range(3):
                                dve.wait_ge(s_sv, i + 1)
                                m, hs = (4, 128) if i < 2 else (1, TAIL)
                                src = ps_m[0:hs, i % 2, 0:128 * m].rearrange("p (t a c) -> p t a c", t=m, a=2)
                                dve.tensor_copy(sv[0:hs, 4 * i:4 * i + m], src).then_inc(s_svk, 1)

                @block.scalar
                def _(act):
                    act.wait_ge(s_var, 1)
                    act.activation(std[:], var[:], ACT.Sqrt).then_inc(s_std, 1)
                    for n in range(NH):
                        act.wait_ge(s_p, n + 1)
                        if n >= 2:
                            act.wait_ge(s_o[n % 2], 48)
                            act.wait_ge(s_rest, n - 1)
                        act.activation(hi[:, n % 2].rearrange("p (c s) -> p c s", c=3), ps_s[0:QK, n % 2, :, 0:PIECE], ACT.Copy).then_inc(s_hi, 1)

                @block.gpsimd
                def _(pool):
                    for n in range(NH):
                        pool.wait_ge(s_rest, n + 1)
                        if n >= 2:
                            pool.wait_ge(s_o[n % 2], 48)
                        pool.tensor_copy(mid[:, n % 2], rest[:, n % 2]).then_inc(s_mid, 1)
                        pool.wait_ge(s_mid, n + 1)
                        pool.tensor_tensor(lo[:, n % 2], rest[:, n % 2], mid[:, n % 2], ALU.subtract).then_inc(s_lo, 1)
            k.rewind()


def max_units():
    units = []
    for i in range(8):
        for c in range(i // 4 + 1):
            for pair in range(2):
                units.append((i, c, pair, min(512, 128 * (i + 1) - 512 * c)))
    return units + [(8, 0, 0, 1024), (8, 1, 0, TAIL)]


def exp_units():
    units = []
    for c in range(2):
        for j in range(4 * (c + 1)):
            s0 = max(512 * c, 128 * j)
            wide = 512 * (c + 1) - s0
            per = 1 if wide > 256 else 2 if wide > 128 else 4
            for e0 in range(0, NE, per):
                units.append((c, [(e0 + i, j, wide * i, s0, wide) for i in range(per)]))
    for j0, j1 in ((0, 4), (4, 8), (8, 9)):
        units.append((2, [(e, j, TAIL * (NE * (j - j0) + e), NIMG, TAIL) for j in range(j0, j1) for e in range(NE)]))
    return units


def ffn_attend(nc, w, qk3, vals, mrow, att):
    with ExitStack() as ctx:
        k = Space(nc, ctx, "d")
        q = k.sb("q", [DEPTH + SHIFT, 2, NE, SEQ], BF16)
        ky = k.sb("ky", [DEPTH + SHIFT, 2, SEQ], BF16)
        v = k.sb("v", [128, 2, NT, 32])
        eyeb = k.sb("eyeb", [128, 128], BF16)
        eye4 = k.sb("eye4", [128, TAIL], BF16)
        consts = k.sb("consts", [128, 3 * 128 + TAIL])
        hide = k.sb("hide", [128, 128], BF16)
        hide_t = k.sb("hide_t", [128, 128], BF16)
        mx = k.sb("mx", [128, 8, 2, NE])
        mx8 = k.sb("mx8", [128, 2])
        m_ = k.sb("m_", [128, NT, NE])
        mr = k.sb("mr", [128, NT, NE])
        parts = k.sb("parts", [128, NT, 3, NE], BF16)
        p8 = k.sb("p8", [128, 3], BF16)
        mt = k.sb("mt", [12, SEQ], BF16)
        NP = 4
        pt = k.sb("pt", [128, NP, 512])
        ot = k.sb("ot", [128, 2, SEQ])
        ps1 = k.ps("ps1", [128, 2, 2, 512])
        ps2 = k.ps("ps2", [128, 2, 512])
        pso = k.ps("pso", [128, 2, 512])
        s_w = k.sem("constants_in")
        s_pchain = k.sem("pool_step")
        s_q = [k.sem("queries_in_0"), k.sem("queries_in_1")]
        s_p1 = k.sem("first_scores")
        s_p1k = k.sem("first_scores_read")
        s_mm = k.sem("maxima")
        s_m3 = k.sem("maxima_parts")
        s_mo = k.sem("maxima_out")
        s_row = k.sem("maxima_rows")
        s_p2 = k.sem("second_scores")
        s_e = k.sem("exponents")
        s_pv = k.sem("values_mixed")
        s_ok = k.sem("outputs_kept")
        s_out = [k.sem("outputs_out_0"), k.sem("outputs_out_1")]

        firsts = max_units()
        seconds = exp_units()
        N1 = len(firsts) + 2
        N2 = len(seconds)
        ends = [max(i for i, (c, _) in enumerate(seconds) if c == chunk) for chunk in range(3)]
        LOADS = 2 * len(STACK_Q) + 2

        with nc.Block() as block:
            @block.sync
            def _(sp):
                sp.dma_start(consts[:], w["d_consts"]).then_inc(s_w, 16)

            @block.vector
            def _(dve):
                dve.wait_ge(s_w, 16)
                for n, dst in enumerate((eyeb, hide, hide_t, eye4)):
                    dve.tensor_copy(dst[:], consts[:, 128 * n:min(128 * (n + 1), 3 * 128 + TAIL)])

            @block.gpsimd
            def _(pool):
                chain = Chain(pool, s_pchain)
                chain(pool.memset(v[:], 0.0))
                chain(pool.memset(v[:, :, :, D:VS], 1.0))
                chain(pool.memset(ky[DEPTH:DEPTH + SHIFT], 1.0))
                chain(pool.memset(mx[:], NEG))
                chain(pool.memset(parts[:], 0.0))
                chain(pool.memset(m_[:], 0.0))
        k.rewind()

        with nc.Fori(0, BATCH) as b:
            with nc.Block() as block:
                @block.sync
                def _(sp):
                    def load(n):
                        if n >= 2:
                            sp.wait_ge(s_pv, N2 * (n - 1))
                        for g in range(len(STACK_Q)):
                            row = b * (NH * 3 * QK) + (3 * n + STACK_Q[g]) * QK
                            sp.dma_start(q[D * g:D * g + D, n % 2], qk3[bass.ds(row, NE * D), :].rearrange("(e o) s -> o e s", e=NE)).then_inc(s_q[n % 2], 16)
                            row = b * (NH * 3 * QK) + (3 * n + STACK_K[g]) * QK + NE * D
                            sp.dma_start(ky[D * g:D * g + D, n % 2], qk3[bass.ds(row, D), :]).then_inc(s_q[n % 2], 16)
                        sp.dma_start(v[:, n % 2, 0:8, 0:D], vals[bass.ds(b * SEQ, NIMG), D * n:D * n + D].rearrange("(t p) c -> p t c", p=128)).then_inc(s_q[n % 2], 16)
                        sp.dma_start(v[0:TAIL, n % 2, 8, 0:D], vals[bass.ds(b * SEQ + NIMG, TAIL), D * n:D * n + D]).then_inc(s_q[n % 2], 16)

                    def maxima_rows(n):
                        sp.wait_ge(s_p1k, N1 * (n + 1))
                        rows = slice(SHIFT * NE * n, SHIFT * NE * (n + 1))
                        sp.dma_start(mrow[rows, :], mt[:]).then_inc(s_mo, 16)
                        sp.wait_ge(s_mo, 16 * (n + 1))
                        sp.dma_start(q[DEPTH:DEPTH + SHIFT, n % 2], mrow[rows, :].rearrange("(j e) s -> j e s", e=NE)).then_inc(s_row, 16)

                    def store(n):
                        sp.wait_ge(s_ok, 3 * (n + 1))
                        for e in range(NE):
                            row = b * (NH * NE * VS) + (NE * n + e) * VS
                            sp.dma_start(att[bass.ds(row, VS), :], ot[32 * e:32 * e + VS, n % 2]).then_inc(s_out[n % 2], 16)

                    load(0)
                    load(1)
                    for n in range(NH):
                        maxima_rows(n)
                        if n >= 1:
                            store(n - 1)
                        if 1 <= n < NH - 1:
                            load(n + 1)
                    store(NH - 1)
                    for o in s_out:
                        sp.wait_ge(o, 2 * NE * 16)

                @block.tensor
                def _(pe):
                    def first(n, i):
                        u = N1 * n + i
                        if i == 0:
                            pe.wait_ge(s_q[n % 2], 16 * LOADS * (n // 2 + 1))
                        if u >= 2:
                            pe.wait_ge(s_p1k, u - 1)
                        p = ps1[:, u % 2]
                        qn, kn = q[0:DEPTH, n % 2], ky[0:DEPTH, n % 2]
                        t, c, pair, wide = firsts[i]
                        if t < 8:
                            for a in range(2):
                                edge = c == t // 4
                                last = pe.matmul(p[:, a, 0:wide], qn[:, 2 * pair + a, 128 * t:128 * t + 128],
                                                 kn[:, 512 * c:512 * c + wide], start=True, stop=not edge)
                                if edge:
                                    last = pe.matmul(p[:, a, wide - 128:wide], eyeb[:], hide[:], start=False, stop=True)
                        else:
                            for e in range(NE):
                                for a in range(2 - c):
                                    at = 1024 if c else 512 * a
                                    m = TAIL if c else 512
                                    last = pe.matmul(p[32 * e:32 * e + 32, a, 0:m], qn[:, e, NIMG:SEQ], kn[:, at:at + m],
                                                     start=True, stop=not c)
                                if c:
                                    last = pe.matmul(p[32 * e:32 * e + 32, 0, 0:m], eyeb[:, 0:TAIL], hide[:, 0:TAIL], start=False, stop=True)
                        last.then_inc(s_p1, 1)

                    def turn_maxima(n):
                        for half in range(2):
                            u = N1 * (n + 1) - 2 + half
                            pe.wait_ge(s_p1k, u - 1)
                            if half == 0:
                                pe.wait_ge(s_m3, n + 1)
                                for t in range(8):
                                    last = pe.matmul(ps1[0:12, u % 2, t // 4, 128 * (t % 4):128 * (t % 4) + 128],
                                                     parts[:, t].rearrange("p j e -> p (j e)"), eyeb[:], start=True, stop=True)
                            else:
                                last = pe.matmul(ps1[0:12, u % 2, 0, 0:TAIL], parts[:, 8].rearrange("p j e -> p (j e)"), eye4[:], start=True, stop=True)
                            last.then_inc(s_p1, 1)

                    def second(n, i):
                        u = N2 * n + i
                        if i == 0:
                            pe.wait_ge(s_row, 16 * (n + 1))
                        if u >= 2:
                            pe.wait_ge(s_e, u - 1)
                        for e, j, col, s0, wide in seconds[i][1]:
                            m = height(j)
                            edge = s0 == 128 * j
                            last = pe.matmul(ps2[0:m, u % 2, col:col + wide], ky[:, n % 2, 128 * j:128 * j + m],
                                             q[:, n % 2, e, s0:s0 + wide], start=True, stop=not edge)
                            if edge:
                                d = min(128, wide)
                                last = pe.matmul(ps2[0:m, u % 2, col:col + d], eyeb[:, 0:m], hide_t[:, 0:d], start=False, stop=True)
                        last.then_inc(s_p2, 1)

                    def mix(n, i):
                        u = N2 * n + i
                        c, parts_ = seconds[i]
                        o = 3 * n + c
                        if i == 0 or seconds[i - 1][0] != c:
                            if o >= 2:
                                pe.wait_ge(s_ok, o - 1)
                        pe.wait_ge(s_e, u + 1)
                        for e, j, col, s0, wide in parts_:
                            m = height(j)
                            at = s0 - 512 * c
                            lastj = (3, 7, 8)[c]
                            last = pe.matmul(pso[32 * e:32 * e + 32, o % 2, at:at + wide], v[0:m, n % 2, j, :], pt[0:m, u % NP, col:col + wide],
                                             start=j == 0, stop=j == lastj)
                        last.then_inc(s_pv, 1)

                    for i in range(len(firsts)):
                        first(0, i)
                    turn_maxima(0)
                    LAG = 2
                    for n in range(NH):
                        ahead = 0
                        for i in range(N2 + LAG):
                            if i < N2:
                                second(n, i)
                            if i >= LAG:
                                mix(n, i - LAG)
                            if n + 1 < NH:
                                while ahead < len(firsts) and ahead * 33 <= i * len(firsts):
                                    first(n + 1, ahead)
                                    ahead += 1
                        if n + 1 < NH:
                            turn_maxima(n + 1)

                @block.vector
                def _(dve):
                    def read(n, i):
                        u = N1 * n + i
                        t, c, pair, wide = firsts[i]
                        if n and i == 0:
                            dve.wait_ge(s_m3, n)
                        dve.wait_ge(s_p1, u + 1)
                        if t < 8:
                            dve.reduce_max(mx[:, t, c, 2 * pair:2 * pair + 2], ps1[:, u % 2, :, 0:wide], axis=AX).then_inc(s_p1k, 1)
                        elif c == 0:
                            dve.tensor_reduce(mx8[:, 0:1], ps1[:, u % 2].rearrange("p a n -> p (a n)"), axis=AX, op=ALU.max).then_inc(s_p1k, 1)
                        else:
                            dve.reduce_max(mx8[:, 1:2], ps1[:, u % 2, 0, 0:TAIL], axis=AX).then_inc(s_p1k, 1)

                    def join_maxima(n):
                        dve.wait_ge(s_p1k, N1 * n + len(firsts))
                        dve.tensor_tensor(m_[:, 0:8], mx[:, :, 0], mx[:, :, 1], ALU.max)
                        dve.tensor_tensor(m_[:, 8, 0:1], mx8[:, 0:1], mx8[:, 1:2], ALU.max).then_inc(s_mm, 1)

                    def keep_maxima(n):
                        u = N1 * (n + 1) - 2
                        if n:
                            dve.wait_ge(s_mo, 16 * n)
                        dve.wait_ge(s_p1, u + 1)
                        dve.tensor_copy(mt[:, 0:NIMG], ps1[0:12, u % 2].rearrange("p a n -> p (a n)")).then_inc(s_p1k, 1)
                        dve.wait_ge(s_p1, u + 2)
                        dve.tensor_copy(mt[:, NIMG:SEQ], ps1[0:12, (u + 1) % 2, 0, 0:TAIL]).then_inc(s_p1k, 1)

                    def keep_outputs(n, c):
                        if n >= 2 and c == 0:
                            dve.wait_ge(s_out[n % 2], NE * 16 * (n // 2))
                        dve.wait_ge(s_pv, N2 * n + ends[c] + 1)
                        wide = (512, 512, TAIL)[c]
                        dve.tensor_copy(ot[:, n % 2, 512 * c:512 * c + wide], pso[:, (3 * n + c) % 2, 0:wide]).then_inc(s_ok, 1)

                    for i in range(len(firsts)):
                        read(0, i)
                    join_maxima(0)
                    keep_maxima(0)
                    LAG = 2
                    for n in range(NH):
                        ahead = 0
                        for i in range(N2 + LAG):
                            if n + 1 < NH:
                                while ahead < len(firsts) and ahead * 33 <= i * len(firsts):
                                    read(n + 1, ahead)
                                    ahead += 1
                                    if ahead == len(firsts):
                                        join_maxima(n + 1)
                            if i - LAG in ends:
                                keep_outputs(n, ends.index(i - LAG))
                        if n + 1 < NH:
                            keep_maxima(n + 1)

                @block.gpsimd
                def _(pool):
                    chain = Chain(pool, s_pchain)
                    for n in range(NH):
                        pool.wait_ge(s_mm, n + 1)
                        chain(pool.tensor_scalar(m_[:], m_[:], -1.0, 1.0, ALU.mult, ALU.mult))
                        for part in range(SHIFT):
                            dst = parts[:, 0:8, part]
                            chain(pool.tensor_copy(dst, m_[:, 0:8]))
                            chain(pool.tensor_copy(p8[:, part:part + 1], m_[:, 8, 0:1]))
                            if part < 2:
                                chain(pool.tensor_tensor(m_[:, 0:8], m_[:, 0:8], dst, ALU.subtract))
                                chain(pool.tensor_tensor(m_[:, 8, 0:1], m_[:, 8, 0:1], p8[:, part:part + 1], ALU.subtract))
                        for e in range(NE):
                            r = slice(32 * e, 32 * e + 32)
                            chain(pool.tensor_copy(parts[r, 8, :, e], p8[r, :]))
                        pool.tensor_copy(mr[0:1, 0, 0:1], m_[0:1, 0, 0:1]).then_inc(s_m3, 1)
                        pool.wait_ge(s_m3, n + 1)

                @block.scalar
                def _(act):
                    for n in range(NH):
                        for i, (c, parts_) in enumerate(seconds):
                            u = N2 * n + i
                            m = height(parts_[0][1])
                            wide = parts_[-1][2] + parts_[-1][4]
                            act.wait_ge(s_p2, u + 1)
                            if u >= NP:
                                act.wait_ge(s_pv, u - NP + 1)
                            act.activation(pt[0:m, u % NP, 0:wide], ps2[0:m, u % 2, 0:wide], ACT.Exp).then_inc(s_e, 1)
            k.rewind()



G = NH * NE


def ffn_finish(nc, w, h_in, att, sxn, h_out):
    with ExitStack() as ctx:
        k = Space(nc, ctx, "h")
        eye = k.sb("eye", [128, 128])
        gw = k.sb("gw", [128, 2, 2 * NE])
        gbias = k.sb("gbias", [128, G])
        fc1 = k.sb("fc1", [C + 1, C])
        fc2 = k.sb("fc2", [C + 1, C])
        fgate = k.sb("fgate", [C, NH])
        lng = k.sb("lng", [128, D])
        lnb = k.sb("lnb", [128, D])
        fng = k.sb("fng", [128, D])
        fnb = k.sb("fnb", [128, D])
        resid = k.sb("resid", [128, NT, C])
        x = k.sb("x", [128, NT, C])
        sx = k.sb("sx", [128, NT, C])
        ot = k.sb("ot", [NE * VS, NH, SEQ])
        rz = k.sb("rz", [128, 2, G])
        a = k.sb("a", [128, NT, G * D])
        at = k.sb("at", [128, 2, 2, 128])
        lg = k.sb("lg", [128, NT * NH, NE])
        gm = k.sb("gm", [128, NT * NH])
        y = k.sb("y", [128, NT, C])
        sq = k.sb("sq", [128, NT, C])
        fx = k.sb("fx", [128, NT, C])
        nz = k.sb("nz", [128, NT, C])
        hx = k.sb("hx", [128, NT, C])
        mu = k.sb("mu", [128, NT * NH])
        var = k.sb("var", [128, NT * NH])
        std = k.sb("std", [128, NT * NH])
        ft = k.sb("ft", [C + 1, SEQ])
        fg = k.sb("fg", [128, NT, NH])
        ps_t = k.ps("ps_t", [128, 2, 512])
        ps_a = k.ps("ps_a", [128, 2, 512])
        ps_g = k.ps("ps_g", [128, 512])
        ps_x = k.ps("ps_x", [128, 3, 512])
        s_w = k.sem("weights_in")
        s_x = k.sem("rows_in")
        s_ot = k.sem("attention_in")
        s_chain = k.sem("dve_step")
        s_pchain = k.sem("pool_step")
        s_t = k.sem("attention_transposed")
        s_a = k.sem("attention_divided")
        s_am = k.sem("attention_masked")
        s_at = k.sem("attention_turned")
        s_atk = k.sem("attention_turned_kept")
        s_g = k.sem("gate_logits")
        s_gx = k.sem("gate_shifted")
        s_ge = k.sem("gate_exponents")
        s_mix = k.sem("experts_mixed")
        s_var = k.sem("variance")
        s_std = k.sem("deviation")
        s_f = k.sem("layer_inputs")
        s_ft = k.sem("layer_inputs_turned")
        s_ftk = k.sem("layer_inputs_turned_kept")
        s_l = k.sem("layer_outputs")
        s_y = k.sem("results")
        s_out = k.sem("rows_out")

        with nc.Block() as block:
            @block.sync
            def _(sp):
                for dst, name in ((eye, "eye"), (gw, "h_gw"), (fc1, "h_fc1"), (fc2, "h_fc2"), (fgate, "h_fgate")):
                    sp.dma_start(dst[:], w[name]).then_inc(s_w, 16)
                for dst, name in ((gbias, "h_gbias"), (lng, "h_lng"), (lnb, "h_lnb"), (fng, "h_fng"), (fnb, "h_fnb")):
                    sp.dma_start(dst[:], w[name].partition_broadcast(128)).then_inc(s_w, 16)
                sp.wait_ge(s_pchain, 1)
                for n in range(NH):
                    cols = slice(D * n, D * n + D)
                    sp.dma_start(resid[:, 0:8, cols], sxn[SEQ * n:SEQ * n + NIMG, cols].rearrange("(t p) c -> p t c", p=128)).then_inc(s_w, 16)
                    sp.dma_start(resid[0:TAIL, 8, cols], sxn[SEQ * n + NIMG:SEQ * n + SEQ, cols]).then_inc(s_w, 16)
                sp.wait_ge(s_w, 18 * 16)

            @block.gpsimd
            def _(pool):
                chain = Chain(pool, s_pchain)
                chain(pool.memset(resid[:, 8], 0.0))
                chain(pool.memset(x[:], 0.0))
                chain(pool.memset(a[:], 0.0))
                chain(pool.memset(sx[:], 1.0))
                chain(pool.memset(lg[:], 0.0))
                chain(pool.memset(hx[:], 0.0))
                chain(pool.memset(fg[:], 0.0))
                chain(pool.memset(ft[C:C + 1], 1.0))
        k.rewind()

        with nc.Fori(0, BATCH) as b:
            with nc.Block() as block:
                @block.sync
                def _(sp):
                    for n in range(NH):
                        row = b * (G * VS) + n * (NE * VS)
                        sp.dma_start(ot[:, n], att[bass.ds(row, NE * VS), :]).then_inc(s_ot, 16)
                    for dst, src in ((x, h_in), (sx, sxn)):
                        sp.dma_start(dst[:, 0:8], src[bass.ds(b * SEQ, NIMG), :].rearrange("(t p) c -> p t c", p=128)).then_inc(s_x, 16)
                        sp.dma_start(dst[0:TAIL, 8], src[bass.ds(b * SEQ + NIMG, TAIL), :]).then_inc(s_x, 16)
                    sp.wait_ge(s_y, 1)
                    sp.dma_start(h_out[bass.ds(b * SEQ, NIMG), :].rearrange("(t p) c -> p t c", p=128), y[:, 0:8]).then_inc(s_out, 16)
                    sp.dma_start(h_out[bass.ds(b * SEQ + NIMG, TAIL), :], y[0:TAIL, 8]).then_inc(s_out, 16)
                    sp.wait_ge(s_out, 32)

                @block.tensor
                def _(pe):
                    pe.wait_ge(s_ot, 64)

                    def turn_back(t):
                        m = height(t)
                        if t >= 2:
                            pe.wait_ge(s_a, t - 1)
                        for n in range(NH):
                            last = pe.transpose(ps_t[0:m, t % 2, NE * VS * n:NE * VS * (n + 1)], ot[:, n, 128 * t:128 * t + m],
                                                eye[0:NE * VS, 0:NE * VS])
                        last.then_inc(s_t, 1)

                    def turn(t):
                        m = height(t)
                        pe.wait_ge(s_am, t + 1)
                        if t >= 2:
                            pe.wait_ge(s_atk, t - 1)
                        for i in range(2):
                            last = pe.transpose(ps_a[:, t % 2, 128 * i:128 * i + m], a[0:m, t, 128 * i:128 * i + 128], eye[0:m, 0:m])
                        last.then_inc(s_at, 1)

                    def gate(t):
                        m = height(t)
                        pe.wait_ge(s_atk, t + 1)
                        for i in range(2):
                            last = pe.matmul(ps_g[0:m, G * t + 8 * i:G * t + 8 * i + 8], at[:, t % 2, i, 0:m], gw[:, i], start=True, stop=True)
                        last.then_inc(s_g, 1)

                    for t in range(NT + 2):
                        if t < NT:
                            turn_back(t)
                        if 1 <= t < NT + 1:
                            turn(t - 1)
                        if t >= 2:
                            gate(t - 2)
                    for layer, src in enumerate((fx, hx, hx)):
                        pe.wait_ge(s_f, layer + 1)
                        for t in range(NT):
                            m = height(t)
                            last = pe.transpose(ps_x[0:C, t // 4, 128 * (t % 4):128 * (t % 4) + m], src[0:m, t, :], eye[0:m, 0:m])
                        last.then_inc(s_ft, 1)
                        pe.wait_ge(s_ftk, layer + 1)
                        for t in range(NT):
                            m = height(t)
                            if layer < 2:
                                wl = (fc1, fc2)[layer]
                                last = pe.matmul(ps_t[0:m, t // 5, C * (t % 5):C * (t % 5) + C], ft[:, 128 * t:128 * t + m], wl[:], start=True, stop=True)
                            else:
                                last = pe.matmul(ps_g[0:m, NH * t:NH * t + NH], ft[0:C, 128 * t:128 * t + m], fgate[:], start=True, stop=True)
                        last.then_inc(s_l, 1)

                @block.scalar
                def _(act):
                    for t in range(NT):
                        m = height(t)
                        act.wait_ge(s_at, t + 1)
                        if t >= 2:
                            act.wait_ge(s_g, t - 1)
                        act.activation(at[:, t % 2, :, 0:m], ps_a[:, t % 2, 0:256].rearrange("p (i s) -> p i s", i=2)[:, :, 0:m], ACT.Copy).then_inc(s_atk, 1)
                    act.wait_ge(s_gx, 1)
                    act.activation(lg[:], lg[:], ACT.Exp).then_inc(s_ge, 1)
                    for i in range(2):
                        act.wait_ge(s_var, i + 1)
                        act.activation(std[:], var[:], ACT.Sqrt).then_inc(s_std, 1)
                    act.wait_ge(s_gx, 2)
                    act.activation(fg[:], fg[:], ACT.Exp).then_inc(s_ge, 1)

                @block.gpsimd
                def _(pool):
                    for t in range(NT):
                        m = height(t)
                        pool.wait_ge(s_a, t + 1)
                        av = a[0:m, t].rearrange("p (n e d) -> p n e d", n=NH, e=NE)
                        mask = nz[0:m, t].rearrange("p (n d) -> p n d", n=NH).unsqueeze(2).to_broadcast([m, NH, NE, D])
                        pool.tensor_tensor(av, av, mask, ALU.mult).then_inc(s_am, 1)

                @block.vector
                def _(dve):
                    chain = Chain(dve, s_chain)
                    dve.wait_ge(s_x, 64)
                    chain(dve.tensor_scalar(nz[:], sx[:], 0.0, None, ALU.not_equal))
                    for t in range(NT):
                        m = height(t)
                        dve.wait_ge(s_t, t + 1)
                        p = ps_t[0:m, t % 2, 0:G * VS].rearrange("p (g v) -> p g v", g=G)
                        chain(dve.reciprocal(rz[0:m, t % 2], p[:, :, D]))
                        dve.tensor_tensor(a[0:m, t].rearrange("p (g d) -> p g d", g=G), p[:, :, 0:D],
                                          spread(rz[0:m, t % 2], [m, G, D]), ALU.mult).then_inc(s_a, 1)
                    dve.wait_ge(s_g, NT)
                    lgt = lg[:].rearrange("p (t n) e -> p t (n e)", t=NT)
                    gp = ps_g[:, 0:NT * G].rearrange("p (t g) -> p t g", t=NT)
                    dve.tensor_tensor(lgt[:, 0:8], gp[:, 0:8], gbias[:].unsqueeze(1).to_broadcast([128, 8, G]), ALU.add)
                    chain(dve.tensor_tensor(lgt[0:TAIL, 8], gp[0:TAIL, 8], gbias[0:TAIL], ALU.add))
                    softmax(chain, dve, lg[:], gm[:], s_gx, s_ge, 1)
                    dve.wait_ge(s_am, NT)
                    a4 = a[:].rearrange("p t (n e d) -> p (t n) e d", n=NH, e=NE)
                    chain(dve.tensor_tensor(a4, a4, lg[:].unsqueeze(3).to_broadcast([128, NT * NH, NE, D]), ALU.mult))
                    yh = y[:].rearrange("p t (n d) -> p (t n) d", n=NH)
                    chain(dve.reduce_sum(yh, a4.rearrange("p m e d -> p m d e"), axis=AX))
                    chain(dve.tensor_tensor(y[:], y[:], resid[:], ALU.add))
                    heads = lambda u: u[:].rearrange("p t (n d) -> p (t n) d", n=NH)
                    rows = lambda u: u[:].unsqueeze(1).to_broadcast([128, NT * NH, D])
                    layer_norm(dve, chain, heads(y), heads(fx), heads(sq), mu[:], var[:], std[:], s_var, s_std, FFN_EPS, n_var=1, depth=D)
                    chain(dve.tensor_tensor(heads(fx), heads(fx), rows(lng), ALU.mult))
                    dve.tensor_tensor(heads(fx), heads(fx), rows(lnb), ALU.add).then_inc(s_f, 1)
                    dve.wait_ge(s_f, 1)
                    chain(dve.tensor_scalar(nz[:], fx[:], 0.0, None, ALU.not_equal))

                    def keep_turned(i):
                        dve.wait_ge(s_ft, i)
                        dve.tensor_copy(ft[0:C, 0:NIMG], ps_x[0:C, 0:2, :].rearrange("p a n -> p (a n)"))
                        dve.tensor_copy(ft[0:C, NIMG:SEQ], ps_x[0:C, 2, 0:TAIL]).then_inc(s_ftk, 1)
                        dve.wait_ge(s_l, i)

                    blocks = ((0, 5, 128, 0, 0), (5, 8, 128, 1, 0), (8, 9, TAIL, 1, 3))
                    keep_turned(1)
                    for t0, t1, m, bank, at0 in blocks:
                        p = ps_t[0:m, bank, C * at0:C * (at0 + t1 - t0)].rearrange("p (t c) -> p t c", c=C)
                        last = dve.scalar_tensor_tensor(hx[0:m, t0:t1], p, 0.0, nz[0:m, t0:t1], ALU.max, ALU.mult)
                    last.then_inc(s_f, 1)
                    keep_turned(2)
                    for t0, t1, m, bank, at0 in blocks:
                        p = ps_t[0:m, bank, C * at0:C * (at0 + t1 - t0)].rearrange("p (t c) -> p t c", c=C)
                        last = dve.tensor_tensor(hx[0:m, t0:t1], p, nz[0:m, t0:t1], ALU.mult)
                    chain(last)
                    chain(dve.tensor_tensor(y[:], hx[:], fx[:], ALU.add))
                    layer_norm(dve, chain, heads(y), heads(hx), heads(sq), mu[:], var[:], std[:], s_var, s_std, FFN_EPS, n_var=2, depth=D)
                    chain(dve.tensor_tensor(heads(hx), heads(hx), rows(fng), ALU.mult))
                    dve.tensor_tensor(heads(hx), heads(hx), rows(fnb), ALU.add).then_inc(s_f, 1)
                    keep_turned(3)
                    gp = ps_g[:, 0:NT * NH].rearrange("p (t g) -> p t g", t=NT)
                    dve.tensor_copy(fg[:, 0:8], gp[:, 0:8])
                    chain(dve.tensor_copy(fg[0:TAIL, 8], gp[0:TAIL, 8]))
                    softmax(chain, dve, fg[:], gm[:, 0:NT], s_gx, s_ge, 2)
                    chain(dve.tensor_tensor(heads(y), heads(hx), spread(fg[:].rearrange("p t n -> p (t n)"), [128, NT * NH, D]), ALU.mult))
                    dve.tensor_tensor(y[:], y[:], x[:], ALU.add).then_inc(s_y, 1)
            k.rewind()


def softmax(chain, dve, x, m, s_shifted, s_exp, count):
    shape = list(x.shape)
    chain(dve.reduce_max(m, x, axis=AX))
    dve.tensor_tensor(x, x, spread(m, shape), ALU.subtract).then_inc(s_shifted, 1)
    dve.wait_ge(s_exp, count)
    chain(dve.reduce_sum(m, x, axis=AX))
    chain(dve.reciprocal(m, m))
    chain(dve.tensor_tensor(x, x, spread(m, shape), ALU.mult))



THIRD = ROWS // 3
PART = SEQ // 3
WID = (128, 128, 96)


def l1_attention(nc, w, h_in, h_out):
    with ExitStack() as ctx:
        k = Space(nc, ctx, "e")
        w_qk = k.sb("w_qk", [C + 1, 3, HEADS * C])
        w_vt = k.sb("w_vt", [C, 3, HEADS, C + 1])
        w_0 = k.sb("w_0", [C, HEADS, C])
        w_v0 = k.sb("w_v0", [C + 1, 3, HEADS * C])
        bias0 = k.sb("bias0", [128, C])
        eye = k.sb("eye", [128, 128])
        half = k.sb("half", [128, 2])
        x = k.sb("x", [128, NT, C])
        xn = k.sb("xn", [128, NT, C])
        sq = k.sb("sq", [128, NT, C])
        mu = k.sb("mu", [128, NT])
        var = k.sb("var", [128, NT])
        std = k.sb("std", [128, NT])
        xt = k.sb("xt", [C + 1, 3, PART])
        qt = k.sb("qt", [128, 2, 3, PART])
        kz = k.sb("kz", [128, 2, 2, 3, PART])
        prod = k.sb("prod", [128, 2, 3 * PART])
        NB = 4
        sc = k.sb("sc", [128, NB, 3, PART])
        ex = k.sb("ex", [128, 2, 3, PART], BF16)
        nmax = k.sb("nmax", [128, NT, HEADS])
        z = k.sb("z", [128, NT, HEADS])
        dz = k.sb("dz", [128, NT, HEADS])
        attn = k.sb("attn", [128, NT, HEADS])
        ya = k.sb("ya", [128, 2, HEADS, C])
        res = k.sb("res", [128, 3, 3, C])
        out = k.sb("out", [128, 3, 3, C])
        ps_s = k.ps("ps_s", [128, 2, 3, 512])
        ps_p = k.ps("ps_p", [128, 2, 512])
        s_w = k.sem("weights_in")
        s_chain = k.sem("dve_step")
        s_pchain = k.sem("pool_step")
        s_mv = k.sem("value_weights_made")
        s_mvc = k.sem("value_weights_kept")
        s_x = k.sem("rows_in")
        s_res = k.sem("residual_in")
        s_var = k.sem("variance")
        s_std = k.sem("deviation")
        s_xn = k.sem("normed")
        s_tr = k.sem("transposed")
        s_xt = k.sem("transposes_kept")
        s_pq = k.sem("queries_projected")
        s_pk = k.sem("keys_projected")
        s_qt = k.sem("queries_kept")
        s_kt = k.sem("keys_kept")
        s_s = k.sem("scores")
        s_sc = k.sem("scores_kept")
        s_ex = k.sem("exponents_summed")
        s_prod = k.sem("query_key_products")
        s_dg = k.sem("diagonals")
        s_dsub = k.sem("diagonal_shifted")
        s_dexp = k.sem("diagonal_exponents")
        s_y = k.sem("values_projected")
        s_ya = k.sem("values_weighted")
        s_sum = k.sem("heads_summed")
        s_out = k.sem("rows_out")

        with nc.Block() as block:
            @block.sync
            def _(sp):
                sp.dma_start(w_qk[:], w["e_wqk"].rearrange("r j n -> r j n")).then_inc(s_w, 16)
                sp.dma_start(w_vt[:], w["e_wvt"]).then_inc(s_w, 16)
                sp.dma_start(w_0[:], w["e_w0"]).then_inc(s_w, 16)
                sp.dma_start(bias0[:], w["e_b0"].partition_broadcast(128)).then_inc(s_w, 16)
                sp.dma_start(eye[:], w["eye"]).then_inc(s_w, 16)
                sp.wait_ge(s_w, 80)

            @block.gpsimd
            def _(pool):
                chain = Chain(pool, s_pchain)
                chain(pool.memset(half[0:64, 0:1], 1.0))
                chain(pool.memset(half[0:64, 1:2], 0.0))
                chain(pool.memset(half[64:128, 0:1], 0.0))
                chain(pool.memset(half[64:128, 1:2], 1.0))
                chain(pool.memset(kz[64:128, :, 0], 0.0))
                chain(pool.memset(kz[0:64, :, 1], 0.0))
                chain(pool.memset(x[:], 0.0))
                chain(pool.memset(xt[64:65], 1.0))
                chain(pool.memset(nmax[:], 0.0))
                chain(pool.memset(z[:], 1.0))
                chain(pool.memset(dz[:], 0.0))

            @block.tensor
            def _(pe):
                pe.wait_ge(s_w, 80)
                for j in range(3):
                    if j >= 2:
                        pe.wait_ge(s_mvc, j - 1)
                    for h in range(HEADS):
                        last = pe.matmul(ps_p[0:C + 1, j % 2, h * C:(h + 1) * C], w_vt[:, j, h, :],
                                         w_0[:, h, :], start=True, stop=True)
                    last.then_inc(s_mv, 1)

            @block.vector
            def _(dve):
                for j in range(3):
                    dve.wait_ge(s_mv, j + 1)
                    dve.tensor_copy(w_v0[:, j, :], ps_p[0:C + 1, j % 2, :]).then_inc(s_mvc, 1)
        k.rewind()

        units = [(p, hh, t) for p in range(4) for hh in range(2) for t in range(NT)]
        PER = 2 * NT
        PROJECT_AT = (5, 8, 11)
        KEEP_AT = (7, 10, 13)

        with nc.Fori(0, BATCH) as b:
            with nc.Block() as block:
                @block.sync
                def _(sp):
                    for g in range(3):
                        first = h_in[bass.ds(b * PART + g * THIRD, 256), :]
                        sp.dma_start(x[:, 3 * g:3 * g + 2, :], first.rearrange("(t p) c -> p t c", p=128)).then_inc(s_x, 16)
                        sp.dma_start(x[0:96, 3 * g + 2, :], h_in[bass.ds(b * PART + g * THIRD + 256, 96), :]).then_inc(s_x, 16)
                    sp.dma_start(res[:, 0:2], h_in[bass.ds(b * SEQ, 768), :].rearrange("(t p j) c -> p t j c", p=128, j=3)).then_inc(s_res, 16)
                    sp.dma_start(res[0:96, 2], h_in[bass.ds(b * SEQ + 768, 288), :].rearrange("(p j) c -> p j c", j=3)).then_inc(s_res, 16)
                    sp.wait_ge(s_sum, NT)
                    sp.dma_start(h_out[bass.ds(b * SEQ, 768), :].rearrange("(t p j) c -> p t j c", p=128, j=3), out[:, 0:2]).then_inc(s_out, 16)
                    sp.dma_start(h_out[bass.ds(b * SEQ + 768, 288), :].rearrange("(p j) c -> p j c", j=3), out[0:96, 2]).then_inc(s_out, 16)
                    sp.wait_ge(s_out, 32)

                @block.scalar
                def _(act):
                    act.wait_ge(s_var, 1)
                    act.activation(std[:], var[:], ACT.Sqrt).then_inc(s_std, 1)

                    def keep_queries(p, j):
                        if p >= 2 and j == 0:
                            act.wait_ge(s_s, PER * (p - 1))
                            act.wait_ge(s_prod, p - 1)
                        act.wait_ge(s_pq, 3 * p + j + 1)
                        act.activation(qt[:, p % 2, j, :], ps_p[:, 0, 0:PART], ACT.Copy).then_inc(s_qt, 1)

                    for j in range(3):
                        keep_queries(0, j)
                    for u, (p, hh, t) in enumerate(units):
                        n = 128 if t % 3 < 2 else 96
                        h = 2 * p + hh
                        if u % PER in KEEP_AT and p < 3:
                            keep_queries(p + 1, KEEP_AT.index(u % PER))
                        act.wait_ge(s_sc, u + 1)
                        if u >= 2:
                            act.wait_ge(s_ex, u - 1)
                        act.activation(ex[0:n, u % 2], sc[0:n, u % NB], ACT.Exp, bias=nmax[0:n, t, h:h + 1],
                                       scale=-1.0, accum_out=z[0:n, t, h:h + 1]).then_inc(s_ex, 1)
                    act.wait_ge(s_dsub, 1)
                    act.activation(attn[:], dz[:], ACT.Exp).then_inc(s_dexp, 1)

                @block.vector
                def _(dve):
                    chain = Chain(dve, s_chain)
                    dve.wait_ge(s_x, 96)
                    layer_norm(dve, chain, x[:], xn[:], sq[:], mu[:], var[:], std[:], s_var, s_std, LN_EPS)
                    for g in range(3):
                        dve.wait_ge(s_tr, g + 1)
                        dve.tensor_copy(xt[0:C, g, :], ps_s[0:C, 0, g, 0:PART]).then_inc(s_xt, 1)

                    def keep_keys(p, j):
                        if p >= 2 and j == 0:
                            dve.wait_ge(s_s, PER * (p - 1))
                            dve.wait_ge(s_prod, p - 1)
                        dve.wait_ge(s_pk, 3 * p + j + 1)
                        dve.tensor_copy(kz[0:64, p % 2, 0, j, :], ps_p[0:64, 1, 0:PART])
                        dve.tensor_copy(kz[64:128, p % 2, 1, j, :], ps_p[64:128, 1, 0:PART]).then_inc(s_kt, 1)

                    for j in range(3):
                        keep_keys(0, j)
                    for u, (p, hh, t) in enumerate(units):
                        n = 128 if t % 3 < 2 else 96
                        h = 2 * p + hh
                        if u % PER in KEEP_AT and p < 3:
                            keep_keys(p + 1, KEEP_AT.index(u % PER))
                        dve.wait_ge(s_s, u + 1)
                        if u >= NB:
                            dve.wait_ge(s_ex, u - NB + 1)
                        dve.tensor_scalar(sc[0:n, u % NB], ps_s[0:n, u % 2, :, 0:PART], -0.125, None, ALU.mult,
                                          ALU.min, accum_out=nmax[0:n, t, h:h + 1]).then_inc(s_sc, 1)
                    dve.wait_ge(s_dg, 4)
                    dg = ps_p[:, 0, 352:352 + NT * HEADS].rearrange("p (j t h) -> p j t h", j=3, t=3)
                    dz4 = dz[:].rearrange("p (j t) h -> p j t h", j=3)
                    nm4 = nmax[:].rearrange("p (j t) h -> p j t h", j=3)
                    dve.wait_ge(s_sc, len(units))
                    for t, n in enumerate(WID):
                        last = dve.scalar_tensor_tensor(dz4[0:n, :, t], dg[0:n, :, t], 0.125, nm4[0:n, :, t], ALU.mult, ALU.add)
                    last.then_inc(s_dsub, 1)
                    dve.wait_ge(s_ex, len(units))
                    chain(dve.reciprocal(z[:], z[:]))
                    dve.wait_ge(s_dexp, 1)
                    chain(dve.tensor_tensor(attn[:], attn[:], z[:], ALU.mult))
                    for t in range(NT):
                        n = WID[t % 3]
                        dve.wait_ge(s_y, t + 1)
                        if t >= 2:
                            dve.wait_ge(s_sum, t - 1)
                        dve.tensor_tensor(ya[0:n, t % 2], ps_p[0:n, t % 2, :].rearrange("p (h c) -> p h c", h=HEADS),
                                          spread(attn[0:n, t], [n, HEADS, C]), ALU.mult).then_inc(s_ya, 1)

                @block.gpsimd
                def _(pool):
                    chain = Chain(pool, s_pchain)
                    for p in range(4):
                        pool.wait_ge(s_qt, 3 * (p + 1))
                        pool.wait_ge(s_kt, 3 * (p + 1))
                        if p >= 2:
                            pool.wait_ge(s_dg, p - 1)
                        q2 = qt[:].rearrange("p a j n -> p a (j n)")
                        k2 = kz[:].rearrange("p a z j n -> p a z (j n)")
                        chain(pool.tensor_tensor(prod[0:64, p % 2], q2[0:64, p % 2], k2[0:64, p % 2, 0], ALU.mult))
                        pool.tensor_tensor(prod[64:128, p % 2], q2[64:128, p % 2], k2[64:128, p % 2, 1], ALU.mult).then_inc(s_prod, 1)
                        pool.wait_ge(s_prod, p + 1)
                    pool.wait_ge(s_res, 32)
                    chain(pool.tensor_tensor(res[:, 0:2], res[:, 0:2], spread_b(bias0[:], 2), ALU.add))
                    chain(pool.tensor_tensor(res[0:96, 2], res[0:96, 2], bias0[0:96].unsqueeze(1).to_broadcast([96, 3, C]), ALU.add))
                    for t in range(NT):
                        j, ti, n = t // 3, t % 3, WID[t % 3]
                        pool.wait_ge(s_ya, t + 1)
                        y = ya[0:n, t % 2]
                        for m in (4, 2, 1):
                            chain(pool.tensor_tensor(y[:, 0:m], y[:, 0:m], y[:, m:2 * m], ALU.add))
                        pool.tensor_tensor(out[0:n, ti, j], y[:, 0], res[0:n, ti, j], ALU.add).then_inc(s_sum, 1)

                @block.tensor
                def _(pe):
                    pe.wait_ge(s_chain, 7)
                    for g in range(3):
                        for t, n in enumerate(WID):
                            last = pe.transpose(ps_s[0:C, 0, g, 128 * t:128 * t + n], xn[0:n, 3 * g + t, :], eye[0:n, 0:n])
                        last.then_inc(s_tr, 1)
                    pe.wait_ge(s_xt, 3)

                    def project(p, j):
                        if 3 * p + j >= 1:
                            pe.wait_ge(s_qt, 3 * p + j)
                        pe.matmul(ps_p[:, 0, 0:PART], w_qk[:, j, 128 * p:128 * p + 128], xt[:, 0, :],
                                  start=True, stop=True).then_inc(s_pq, 1)
                        if 3 * p + j >= 1:
                            pe.wait_ge(s_kt, 3 * p + j)
                        pe.matmul(ps_p[:, 1, 0:PART], w_qk[:, j, 128 * p:128 * p + 128], xt[:, 1, :],
                                  start=True, stop=True).then_inc(s_pk, 1)

                    def diagonal(p):
                        pe.wait_ge(s_prod, p + 1)
                        pe.wait_ge(s_qt, 3 * min(p + 2, 4))
                        for t in range(NT):
                            n = WID[t % 3]
                            at = PART * (t // 3) + 128 * (t % 3)
                            col = 352 + HEADS * t + 2 * p
                            last = pe.matmul(ps_p[0:n, 0, col:col + 2], prod[:, p % 2, at:at + n], half[:], start=True, stop=True)
                        last.then_inc(s_dg, 1)

                    for j in range(3):
                        project(0, j)
                    for u, (p, hh, t) in enumerate(units):
                        n = WID[t % 3]
                        if u % PER in PROJECT_AT and p < 3:
                            project(p + 1, PROJECT_AT.index(u % PER))
                        if u % PER == 16:
                            diagonal(p)
                        if u % PER == 0:
                            pe.wait_ge(s_qt, 3 * (p + 1))
                            pe.wait_ge(s_kt, 3 * (p + 1))
                        if u >= 2:
                            pe.wait_ge(s_sc, u - 1)
                        for j in range(3):
                            last = pe.matmul(ps_s[0:n, u % 2, j, 0:PART],
                                             kz[:, p % 2, hh, t // 3, 128 * (t % 3):128 * (t % 3) + n],
                                             qt[:, p % 2, j, :], start=True, stop=True)
                        last.then_inc(s_s, 1)
                    for t in range(NT):
                        n = WID[t % 3]
                        if t == 0:
                            pe.wait_ge(s_dsub, 1)
                        if t >= 2:
                            pe.wait_ge(s_ya, t - 1)
                        pe.matmul(ps_p[0:n, t % 2, :], xt[:, 2, 128 * (t % 3):128 * (t % 3) + n], w_v0[:, t // 3, :],
                                  start=True, stop=True).then_inc(s_y, 1)
            k.rewind()


def spread_b(bias, n):
    return bias.unsqueeze(1).unsqueeze(1).to_broadcast([128, n, 3, C])



EXPERTS = 16
FF = 128
CHUNK = 352
WIDTHS = (128, 128, 96)


def l1_experts(nc, w, h_in, h_out):
    with ExitStack() as ctx:
        k = Space(nc, ctx, "f")
        w1 = k.sb("w1", [C + 1, EXPERTS, FF])
        w2 = k.sb("w2", [FF, EXPERTS, C])
        wg = k.sb("wg", [C + 1, EXPERTS])
        b2 = k.sb("b2", [EXPERTS, C])
        gamma = k.sb("gamma", [128, C])
        beta = k.sb("beta", [128, C])
        eye = k.sb("eye", [128, 128])
        iota = k.sb("iota", [128, EXPERTS])
        x = k.sb("x", [128, NT, C])
        xn = k.sb("xn", [128, NT, C])
        sq = k.sb("sq", [128, NT, C])
        mu = k.sb("mu", [128, NT])
        var = k.sb("var", [128, NT])
        std = k.sb("std", [128, NT])
        xt = k.sb("xt", [C + 1, 3, CHUNK])
        lg = k.sb("lg", [128, NT, EXPERTS])
        top = k.sb("top", [128, NT, 8])
        who = k.sb("who", [128, NT, 8], U32)
        whof = k.sb("whof", [128, NT, 2])
        e2 = k.sb("e2", [128, NT])
        den = k.sb("den", [128, NT])
        w1st = k.sb("w1st", [128, NT])
        w2nd = k.sb("w2nd", [128, NT])
        ga = k.sb("ga", [128, NT, EXPERTS])
        gb = k.sb("gb", [128, NT, EXPERTS])
        gt = k.sb("gt", [EXPERTS, 3, CHUNK])
        ht = k.sb("ht", [FF, 2, EXPERTS, CHUNK])
        wo = k.sb("wo", [128, 2, EXPERTS, C])
        moe = k.sb("moe", [128, NT, C])
        y = k.sb("y", [128, NT, C])
        ps_a = k.ps("ps_a", [128, 2, 512])
        ps_h = k.ps("ps_h", [128, 2, 512])
        ps_o = k.ps("ps_o", [128, 2, 2, 512])
        s_w = k.sem("weights_in")
        s_chain = k.sem("dve_step")
        s_pchain = k.sem("pool_step")
        s_x = k.sem("rows_in")
        s_var = k.sem("variance")
        s_std = k.sem("deviation")
        s_xn = k.sem("normed")
        s_tr = k.sem("transposed")
        s_xt = k.sem("transposes_kept")
        s_lg = k.sem("logits")
        s_lgk = k.sem("logits_kept")
        s_d2 = k.sem("second_less_first")
        s_e2 = k.sem("second_exponent")
        s_g = k.sem("gates")
        s_gt = k.sem("gates_transposed")
        s_gtk = k.sem("gates_transposed_kept")
        s_h = k.sem("hidden")
        s_ht = k.sem("hidden_kept")
        s_o = k.sem("expert_outputs")
        s_wo = k.sem("outputs_weighted")
        s_b2 = k.sem("output_biases")
        s_y = k.sem("results")
        s_out = k.sem("rows_out")

        with nc.Block() as block:
            @block.sync
            def _(sp):
                for dst, name in ((w1, "f_w1"), (w2, "f_w2"), (wg, "f_wg"), (b2, "f_b2"), (eye, "eye"), (iota, "f_iota")):
                    sp.dma_start(dst[:], w[name]).then_inc(s_w, 16)
                sp.dma_start(gamma[:], w["f_gamma"].partition_broadcast(128)).then_inc(s_w, 16)
                sp.dma_start(beta[:], w["f_beta"].partition_broadcast(128)).then_inc(s_w, 16)
                sp.wait_ge(s_w, 128)

            @block.gpsimd
            def _(pool):
                chain = Chain(pool, s_pchain)
                chain(pool.memset(x[:], 0.0))
                chain(pool.memset(lg[:], 0.0))
                chain(pool.memset(top[:], 0.0))
                chain(pool.memset(who[:], 0))
                chain(pool.memset(moe[:], 0.0))
                chain(pool.memset(xt[C:C + 1], 1.0))
        k.rewind()

        with nc.Fori(0, BATCH) as b:
            with nc.Block() as block:
                @block.sync
                def _(sp):
                    for c in range(3):
                        at = b * SEQ + c * CHUNK
                        sp.dma_start(x[:, 3 * c:3 * c + 2], h_in[bass.ds(at, 256), :].rearrange("(t p) c -> p t c", p=128)).then_inc(s_x, 16)
                        sp.dma_start(x[0:96, 3 * c + 2], h_in[bass.ds(at + 256, 96), :]).then_inc(s_x, 16)
                    sp.wait_ge(s_y, 1)
                    for c in range(3):
                        at = b * SEQ + c * CHUNK
                        sp.dma_start(h_out[bass.ds(at, 256), :].rearrange("(t p) c -> p t c", p=128), y[:, 3 * c:3 * c + 2]).then_inc(s_out, 16)
                        sp.dma_start(h_out[bass.ds(at + 256, 96), :], y[0:96, 3 * c + 2]).then_inc(s_out, 16)
                    sp.wait_ge(s_out, 96)

                @block.scalar
                def _(act):
                    act.wait_ge(s_var, 1)
                    act.activation(std[:], var[:], ACT.Sqrt).then_inc(s_std, 1)
                    act.wait_ge(s_d2, 1)
                    act.activation(e2[:], e2[:], ACT.Exp).then_inc(s_e2, 1)
                    for c in range(3):
                        for e in range(EXPERTS):
                            n = c * EXPERTS + e
                            act.wait_ge(s_h, n + 1)
                            if c == 2 and e == 0:
                                act.wait_ge(s_o, 3)
                            act.activation(ht[:, c % 2, e], ps_h[:, n % 2, 0:CHUNK], ACT.Relu).then_inc(s_ht, 1)
                    act.wait_ge(s_var, 2)
                    act.activation(std[:], var[:], ACT.Sqrt).then_inc(s_std, 1)

                @block.vector
                def _(dve):
                    chain = Chain(dve, s_chain)
                    dve.wait_ge(s_x, 96)
                    layer_norm(dve, chain, x[:], xn[:], sq[:], mu[:], var[:], std[:], s_var, s_std, LN_EPS)
                    for c in range(3):
                        dve.wait_ge(s_tr, c + 1)
                        dve.tensor_copy(xt[0:C, c], ps_a[0:C, c % 2, 0:CHUNK]).then_inc(s_xt, 1)
                    dve.wait_ge(s_lg, 1)
                    lgp = ps_a[:, 1, 352:352 + NT * EXPERTS].rearrange("p (c t e) -> p c t e", c=3, t=3)
                    lg4 = lg[:].rearrange("p (c t) e -> p c t e", c=3)
                    dve.tensor_copy(lg4[:, :, 0:2], lgp[:, :, 0:2])
                    dve.tensor_copy(lg4[0:96, :, 2], lgp[0:96, :, 2]).then_inc(s_lgk, 1)
                    dve.wait_ge(s_lgk, 1)
                    for t in range(NT):
                        last = dve.max(top[:, t], lg[:, t])
                    chain(last)
                    for t in range(NT):
                        last = dve.max_index(who[:, t], top[:, t], lg[:, t])
                    dve.tensor_tensor(e2[:], top[:, :, 1], top[:, :, 0], ALU.subtract).then_inc(s_d2, 1)
                    chain(last)
                    chain(dve.tensor_copy(whof[:], who[:, :, 0:2]))
                    shape = [128, NT, EXPERTS]
                    every = iota[:].unsqueeze(1).to_broadcast(shape)
                    chain(dve.tensor_tensor(ga[:], every, spread(whof[:, :, 0], shape), ALU.is_equal))
                    chain(dve.tensor_tensor(gb[:], every, spread(whof[:, :, 1], shape), ALU.is_equal))
                    dve.wait_ge(s_e2, 1)
                    chain(dve.tensor_scalar(den[:], e2[:], 1.0, None, ALU.add))
                    chain(dve.reciprocal(w1st[:], den[:]))
                    chain(dve.tensor_tensor(w2nd[:], e2[:], w1st[:], ALU.mult))
                    chain(dve.tensor_tensor(ga[:], ga[:], spread(w1st[:], shape), ALU.mult))
                    chain(dve.tensor_tensor(gb[:], gb[:], spread(w2nd[:], shape), ALU.mult))
                    dve.tensor_tensor(ga[:], ga[:], gb[:], ALU.add).then_inc(s_g, 1)
                    for c in range(3):
                        dve.wait_ge(s_gt, c + 1)
                        dve.tensor_copy(gt[:, c], ps_a[0:EXPERTS, 0, 0:CHUNK]).then_inc(s_gtk, 1)
                    dve.wait_ge(s_g, 1)
                    for t in range(NT):
                        n = WIDTHS[t % 3]
                        dve.wait_ge(s_o, t + 1)
                        dve.tensor_tensor(wo[0:n, t % 2], ps_o[0:n, t % 2].rearrange("p a (e c) -> p (a e) c", c=C),
                                          spread(ga[0:n, t], [n, EXPERTS, C]), ALU.mult).then_inc(s_wo, 1)
                        dve.wait_ge(s_wo, t + 1)
                        last = dve.reduce_sum(moe[0:n, t], wo[0:n, t % 2].rearrange("p e c -> p c e"), axis=AX)
                        chain(last)
                    chain(dve.tensor_tensor(moe[:], moe[:], xn[:], ALU.add))
                    dve.wait_ge(s_b2, 1)
                    for c in range(3):
                        for ti, n in enumerate(WIDTHS):
                            col = 64 * (3 * c + ti)
                            at = ps_b(ps_a, ps_h, 3 * c + ti)
                            last = dve.tensor_tensor(moe[0:n, 3 * c + ti], moe[0:n, 3 * c + ti], at[0:n], ALU.add)
                    chain(last)
                    layer_norm(dve, chain, moe[:], y[:], sq[:], mu[:], var[:], std[:], s_var, s_std, LN_EPS, n_var=2)
                    chain(dve.tensor_tensor(y[:], y[:], gamma[:].unsqueeze(1).to_broadcast([128, NT, C]), ALU.mult))
                    chain(dve.tensor_tensor(y[:], y[:], beta[:].unsqueeze(1).to_broadcast([128, NT, C]), ALU.add))
                    dve.tensor_tensor(y[:], y[:], x[:], ALU.add).then_inc(s_y, 1)

                @block.tensor
                def _(pe):
                    pe.wait_ge(s_chain, 7)
                    for c in range(3):
                        if c == 2:
                            pe.wait_ge(s_xt, 1)
                        for t, n in enumerate(WIDTHS):
                            last = pe.transpose(ps_a[0:C, c % 2, 128 * t:128 * t + n], xn[0:n, 3 * c + t, :], eye[0:n, 0:n])
                        last.then_inc(s_tr, 1)
                    pe.wait_ge(s_xt, 3)
                    for t in range(NT):
                        n = WIDTHS[t % 3]
                        col = 352 + EXPERTS * t
                        last = pe.matmul(ps_a[0:n, 1, col:col + EXPERTS], xt[:, t // 3, 128 * (t % 3):128 * (t % 3) + n], wg[:],
                                         start=True, stop=True)
                    last.then_inc(s_lg, 1)

                    def hidden(c, lo, hi):
                        for e in range(lo, hi):
                            n = c * EXPERTS + e
                            if n >= 2:
                                pe.wait_ge(s_ht, n - 1)
                            pe.matmul(ps_h[:, n % 2, 0:CHUNK], w1[:, e], xt[:, c], start=True, stop=True).then_inc(s_h, 1)

                    def transpose_gates():
                        pe.wait_ge(s_g, 1)
                        for c in range(3):
                            if c >= 1:
                                pe.wait_ge(s_gtk, c)
                            for t, n in enumerate(WIDTHS):
                                last = pe.transpose(ps_a[0:EXPERTS, 0, 128 * t:128 * t + n], ga[0:n, 3 * c + t, :], eye[0:n, 0:n])
                            last.then_inc(s_gt, 1)

                    def outputs(c):
                        pe.wait_ge(s_ht, EXPERTS * (c + 1))
                        for ti, n in enumerate(WIDTHS):
                            t = 3 * c + ti
                            if t >= 2:
                                pe.wait_ge(s_wo, t - 1)
                            for e in range(EXPERTS):
                                last = pe.matmul(ps_o[0:n, t % 2, e // 8, C * (e % 8):C * (e % 8) + C],
                                                 ht[:, c % 2, e, 128 * ti:128 * ti + n], w2[:, e], start=True, stop=True)
                            last.then_inc(s_o, 1)

                    hidden(0, 0, EXPERTS)
                    transpose_gates()
                    hidden(1, 0, EXPERTS)
                    outputs(0)
                    hidden(2, 0, EXPERTS)
                    outputs(1)
                    outputs(2)
                    pe.wait_ge(s_gtk, 3)
                    for t in range(NT):
                        n = WIDTHS[t % 3]
                        last = pe.matmul(ps_b(ps_a, ps_h, t)[0:n], gt[:, t // 3, 128 * (t % 3):128 * (t % 3) + n], b2[:],
                                         start=True, stop=True)
                    last.then_inc(s_b2, 1)
            k.rewind()


def ps_b(ps_a, ps_h, t):
    return ps_h[:, t // 7, C * (t % 7):C * (t % 7) + C]


def early_fusion(nc, w, out):
    def dram(name, shape, dt=F32):
        return nc.dram_tensor(name, shape, dt).ap()

    tokens, h1, h2, h3 = (dram(name, (ROWS, C)) for name in ("tokens", "h1", "h2", "h3"))
    index = dram("index", (BATCH * 128, TILES * POINTS), U32)
    corner = dram("corner", (BATCH * 128, TILES * POINTS * 4))
    query = dram("query", (BATCH * 128, TILES * C))
    sampling_points(nc, w, w["fmap"], index, corner, query)
    deformable_attention(nc, w, w["fmap"], index, corner, query, tokens)
    text_tokens(nc, w, tokens)
    l0_attention(nc, w, tokens, h1)
    qk3 = dram("qk3", (BATCH * NH * 3 * QK, SEQ), BF16)
    vals = dram("vals", (ROWS, C))
    split = dram("split", (ROWS, C))
    maxima = dram("maxima", (3 * NH * NE, SEQ), BF16)
    attended = dram("attended", (BATCH * NH * NE * VS, SEQ))
    ffn_project(nc, w, h1, qk3, vals, split)
    ffn_attend(nc, w, qk3, vals, maxima, attended)
    ffn_finish(nc, w, h1, attended, split, h2)
    l1_attention(nc, w, h2, h3)
    l1_experts(nc, w, h3, out)


def layout(i):
    a = {}
    a["eye"] = np.eye(128, dtype=np.float32)
    wb = np.concatenate([i["L1_attn_Wqkv"], i["L1_attn_bqkv"][None]], 0).reshape(65, 3, 64, 8)
    a["e_wqk"] = wb.transpose(0, 1, 3, 2).reshape(65, 3, 512)
    a["e_wvt"] = wb.transpose(2, 1, 3, 0)
    a["e_w0"] = i["L1_attn_W0"].reshape(64, 8, 64)
    a["e_b0"] = i["L1_attn_b0"]
    a["f_w1"] = np.concatenate([i["L1_ffn_w1"].transpose(1, 0, 2), i["L1_ffn_b1"][None]], 0)
    a["f_w2"] = i["L1_ffn_w2"].transpose(1, 0, 2)
    a["f_wg"] = np.concatenate([i["L1_ffn_gate_w"], i["L1_ffn_gate_b"][None]], 0)
    a["f_b2"] = i["L1_ffn_b2"]
    a["f_gamma"] = i["L1_ffn_gamma"]
    a["f_beta"] = i["L1_ffn_beta"]
    a["f_iota"] = np.tile(np.arange(16, dtype=np.float32), (128, 1))
    wb = np.concatenate([i["L0_attn_W_qkv"], i["L0_attn_b_qkv"][None]], 0).reshape(65, 3, 64)
    a["c_wqk"] = wb[:, 0:2]
    a["c_wvt"] = wb[:, 2].T
    a["c_wout"] = i["L0_attn_W_out"]
    a["c_bout"] = i["L0_attn_b_out"]
    hl = np.concatenate([i["L0_ffn_hl_w"].reshape(64, 64).T, i["L0_ffn_hl_b"].reshape(1, 64)], 0)
    a["g_hl"] = hl
    a["g_hlt"] = hl.T.reshape(4, 16, 65).transpose(1, 0, 2)
    wq = i["L0_ffn_wq"].transpose(3, 0, 1, 2).reshape(16, 4, 64)
    wk = i["L0_ffn_wk"].transpose(2, 0, 1)
    a["g_wqk"] = np.concatenate([wq, wk], 2)
    a["g_wv"] = i["L0_ffn_wv"].transpose(2, 0, 1)
    gw = np.zeros((2, 64, 2, 2, 4), np.float32)
    g4 = i["L0_ffn_gate_w"].reshape(2, 2, 4, 64)
    for n in range(2):
        gw[n, :, :, n, :] = g4[:, n].transpose(2, 0, 1)
    a["h_gw"] = gw.reshape(128, 2, 8)
    a["h_gbias"] = i["L0_ffn_gate_b"].reshape(16)
    for m in (1, 2):
        fc = np.zeros((65, 64), np.float32)
        for n in range(4):
            fc[16 * n:16 * n + 16, 16 * n:16 * n + 16] = i[f"L0_ffn_fc{m}_w"].T
            fc[64, 16 * n:16 * n + 16] = i[f"L0_ffn_fc{m}_b"]
        a[f"h_fc{m}"] = fc
    a["h_fgate"] = i["L0_ffn_fgate_w"].T
    a["h_lng"], a["h_lnb"], a["h_fng"], a["h_fnb"] = (i["L0_ffn_" + x] for x in ("ln_g", "ln_b", "fnorm_g", "fnorm_b"))
    x = i["x"].transpose(0, 2, 3, 1)
    a["fmap"] = np.concatenate([x[:, :-1], x[:, 1:]], 3).reshape(-1, 2 * C)
    lin = np.linspace(-1.0, 1.0, 32).astype(np.float32)
    px = (lin + np.float32(1)) * np.float32(0.5) * np.float32(127)
    p0 = np.clip(np.floor(px), 0, 126).astype(np.float32)
    fr = np.clip(px - p0, 0, 1).astype(np.float32)
    tok = np.arange(1024)
    yi, xi = tok // 32, tok % 32
    by_tile = lambda u: u.reshape((8, 128) + u.shape[1:]).swapaxes(0, 1)
    fx, fy = fr[xi], fr[yi]
    a["a_wq4"] = by_tile(np.stack([(1 - fx) * (1 - fy), (1 - fx) * fy, fx * (1 - fy), fx * fy], 1).astype(np.float32))
    a["a_ref"] = by_tile(np.stack([lin[xi], lin[yi]], 1))
    q0 = by_tile((p0[yi] * 128 + p0[xi]).astype(np.uint32))
    off = (np.arange(16) * (127 * 128)).astype(np.uint32)
    a["a_qidx"] = (off[:, None, None] + q0[None]).reshape(16 * 128, 8)
    a["a_first"] = np.repeat(off.astype(np.float32), 128)[:, None]
    w1 = np.zeros((65, 80), np.float32)
    w1[:64, :64] = i["L0_tok_W_q"].T
    w1[:64, 64:] = i["L0_tok_W_o1"]
    w1[64, 64:] = i["L0_tok_b_o1"]
    a["a_w1"] = w1
    w2 = np.zeros((33, 16), np.float32)
    w2[:16] = i["L0_tok_W_o2"]
    w2[32] = i["L0_tok_b_o2"]
    a["a_w2"] = w2
    a["a_lng"], a["a_lnb"] = i["L0_tok_ln_g"], i["L0_tok_ln_b"]
    kv = np.zeros((2, 64, 2, 2, 64), np.float32)
    for p in range(2):
        kv[p, :, p, 0] = i["L0_tok_W_k"].T
        kv[p, :, p, 1] = i["L0_tok_W_v"].T
    a["b_wkv"] = kv.reshape(128, 256)
    a["x_txt"] = i["x_txt"].reshape(4, 128).T
    a["pos_S"] = i["pos_S"][:, None]
    a["t_heads"] = np.kron(np.eye(8), np.ones((8, 1))).astype(np.float32)
    s = np.arange(32, dtype=np.float32)
    h = np.arange(8, dtype=np.float32)[None, :, None]
    dist = np.abs(s[:, None, None] - s[None, None, :])
    upper = s[:, None, None] < s[None, None, :]
    slope = np.where(upper, -np.float32(2) ** -(np.float32(0.5) + h), -np.float32(2) ** -(np.float32(1) + h))
    a["t_alibi"] = np.tile((slope * dist).astype(np.float32), (4, 1, 1))
    freq = np.float32(1) / np.float32(10000) ** (np.arange(0, 64, 2, dtype=np.float32) / np.float32(64))
    angle = (np.arange(1024, dtype=np.float32)[:, None] * freq[None]).astype(np.float32)
    a["t_table"] = np.concatenate([np.sin(angle), np.cos(angle)], 1).astype(np.float32)
    a["t_emb"] = i["L0_txt_emb_table"]
    a["t_iw"], a["t_pw"] = i["L0_txt_input_weight"], i["L0_txt_position_weight"]
    a["t_lnfw"], a["t_lnfb"] = i["L0_txt_lnf_w"], i["L0_txt_lnf_b"]
    for n in ("ln1_w", "ln1_b", "ln2_w", "ln2_b"):
        a["t_" + n.replace("_", "")] = i["L0_txt_" + n]
    a["t_w1"] = np.concatenate([i["L0_txt_w1"], i["L0_txt_b1"][:, None]], 1).reshape(6 * 65, 256)
    a["t_w2"] = i["L0_txt_w2"].reshape(6 * 256, 64)
    a["t_b2"] = i["L0_txt_b2"]
    n = np.arange(128)
    later = np.where(n[None, :] > n[:, None], -1e30, 0)
    a["d_consts"] = np.concatenate([np.eye(128), later, later.T, np.tile(np.eye(32), (4, 1))], 1).astype(np.float32)
    return {k: np.ascontiguousarray(v) for k, v in a.items()}


def kernel(**inputs):
    from concourse import bacc
    from concourse.bass_utils import run_bass_kernel_spmd

    nc = bacc.Bacc("TRN2", target_bir_lowering=False, num_devices=1)
    arrays = {f"in_{name}": array for name, array in layout(inputs).items()}
    w = {name[3:]: nc.dram_tensor(name, array.shape, mybir.dt.from_np(array.dtype), kind="ExternalInput").ap()
         for name, array in arrays.items()}
    out = nc.dram_tensor("out_0_dram", (ROWS, C), F32, kind="ExternalOutput").ap()
    early_fusion(nc, w, out)
    r = run_bass_kernel_spmd(nc, [arrays], core_ids=[0])
    return r.results[0]["out_0_dram"].reshape(BATCH, SEQ, C)
```

```python
import concourse.bass as bass
from concourse import mybir
from contextlib import ExitStack
import numpy as np

F32 = mybir.dt.float32
BF16 = mybir.dt.bfloat16
I32 = mybir.dt.int32
U32 = mybir.dt.uint32
ALU = mybir.AluOpType
ACT = mybir.ActivationFunctionType
AX = mybir.AxisListType.X

BATCH = 16
C = 64
GRID = 32
NIMG = GRID * GRID
NTXT = 32
SEQ = NIMG + NTXT
ROWS = BATCH * SEQ
NT = 9
TAIL = SEQ - 8 * 128
LN_EPS = 1e-5


class Space:

    def __init__(self, nc, ctx, stage):
        self.nc, self.ctx, self.stage, self.sems, self.gathers = nc, ctx, stage, [], []

    def sb(self, name, shape, dt=F32):
        return self.ctx.enter_context(self.nc.sbuf_tensor(f"{self.stage}s_{name}", shape, dt))

    def ps(self, name, shape, dt=F32):
        return self.ctx.enter_context(self.nc.psum_tensor(f"{self.stage}s_{name}", shape, dt))

    def sem(self, name):
        s = self.ctx.enter_context(self.nc.semaphore(f"{self.stage}s_{name}"))
        self.sems.append(s)
        return s

    def gather_sem(self, name):
        self.gathers.append(self.sem(name))
        return self.gathers[-1]

    def rewind(self):
        for run in runs(self.gathers):
            self.nc.gpsimd.dma_reset(run)
        for run in runs(self.sems):
            self.nc.gpsimd.sem_clear(run)
        self.nc.all_engine_barrier()


def runs(sems):
    numbers = sorted(s.num for s in sems)
    starts = [n for n in numbers if n - 1 not in numbers]
    ends = [n + 1 for n in numbers if n + 1 not in numbers]
    return [range(a, b) for a, b in zip(starts, ends)]


class Chain:

    def __init__(self, eng, sem):
        self.eng, self.sem, self.n = eng, sem, 0

    def __call__(self, instruction):
        self.n += 1
        instruction.then_inc(self.sem, 1)
        self.eng.wait_ge(self.sem, self.n)


def spread(ap, shape):
    return ap.unsqueeze(len(shape) - 1).to_broadcast(shape)




def split_moving(dve, chain, src, parts, rest, done):
    chain(dve.tensor_copy(parts[:, 0], src))
    chain(dve.tensor_tensor(rest, src, parts[:, 0], ALU.subtract))
    chain(dve.tensor_copy(parts[:, 1], rest))
    dve.tensor_copy(parts[0:C, 2], parts[0:C, 0])
    dve.tensor_tensor(parts[C:2 * C, 2], rest[C:2 * C], parts[C:2 * C, 1], ALU.subtract).then_inc(done, 1)


def split_weights(dve, chain, w, mid, parts):
    chain(dve.tensor_copy(parts[0:C, 0], w[0:C]))
    chain(dve.tensor_copy(parts[C:2 * C, 1], w[C:2 * C]))
    chain(dve.tensor_tensor(w[0:C], w[0:C], parts[0:C, 0], ALU.subtract))
    chain(dve.tensor_tensor(w[C:2 * C], w[C:2 * C], parts[C:2 * C, 1], ALU.subtract))
    chain(dve.tensor_copy(mid, w))
    chain(dve.tensor_copy(parts[C:2 * C, 0], mid[C:2 * C]))
    chain(dve.tensor_tensor(parts[0:C, 1], w[0:C], mid[0:C], ALU.subtract))


PASSES = ((0, 0), (1, 0), (2, 1))


def layer_norm(dve, chain, x, xc, sq, mu, var, std, s_var, s_std, eps, n_var=1, depth=C, done=None, twice=None):
    shape = list(x.shape)
    chain(dve.reduce_sum(mu, x, axis=AX))
    chain(dve.tensor_scalar(mu, mu, -1.0 / depth, None, ALU.mult))
    chain(dve.tensor_tensor(xc, x, spread(mu, shape), ALU.add))
    chain(dve.tensor_tensor(sq, xc, xc, ALU.mult))
    chain(dve.reduce_sum(var, sq, axis=AX))
    dve.tensor_scalar(var, var, 1.0 / depth, eps, ALU.mult, ALU.add).then_inc(s_var, 1)
    dve.wait_ge(s_std, n_var)
    chain(dve.reciprocal(std, std))
    if twice is None:
        last = dve.tensor_tensor(xc, xc, spread(std, shape), ALU.mult)
    else:
        pair = [shape[0], shape[1], 2, shape[2]]
        last = dve.tensor_tensor(twice, xc.unsqueeze(2).to_broadcast(pair), std.unsqueeze(2).unsqueeze(3).to_broadcast(pair), ALU.mult)
    if done is None:
        chain(last)
    else:
        last.then_inc(done, 1)



SIDE = 128
HEADS = 8
POINTS = HEADS
DH = C // HEADS
TILES = NIMG // 128
PIX = (SIDE - 1) * SIDE
OFFSET_SCALE = 4.0
CORNER = 4 * C


def image_tokens(nc, w, h_out):
    with ExitStack() as ctx:
        k = Space(nc, ctx, "a")
        fmap = w["fmap"]
        GB = 4
        w1 = k.sb("w1", [C + 1, C + 16])
        w2 = k.sb("w2", [33, 16])
        lng = k.sb("lng", [128, 16])
        lnb = k.sb("lnb", [128, 16])
        eye = k.sb("eye", [128, 128])
        wq4 = k.sb("wq4", [128, TILES, 4])
        ref = k.sb("ref", [128, TILES, 2])
        qidx = k.sb("qidx", [128, TILES], U32)
        first = k.sb("first", [128, 1])
        gq = k.sb("gq", [128, TILES, 4, C])
        qf = k.sb("qf", [128, TILES, C])
        xt = k.sb("xt", [C + 1, TILES, 128])
        o1 = k.sb("o1", [128, TILES, 16])
        hn = k.sb("hn", [128, TILES, 16])
        sq = k.sb("sq", [128, TILES, 16])
        th = k.sb("th", [128, TILES, 16])
        mu = k.sb("mu", [128, TILES])
        var = k.sb("var", [128, TILES])
        std = k.sb("std", [128, TILES])
        hT = k.sb("hT", [33, TILES, 128])
        pos = k.sb("pos", [128, TILES * POINTS, 2])
        posi = k.sb("posi", [128, TILES * POINTS, 2], I32)
        low = k.sb("low", [128, TILES * POINTS, 2])
        over = k.sb("over", [128, TILES * POINTS, 2])
        frac = k.sb("frac", [128, TILES * POINTS, 2])
        comp = k.sb("comp", [128, TILES * POINTS, 2])
        at = k.sb("at", [128, TILES * POINTS])
        next_wgt = k.sb("next_wgt", [128, TILES, POINTS * 4])
        next_idx = k.sb("next_idx", [128, TILES * POINTS], U32)
        next_q = k.sb("next_q", [128, TILES, C])
        wkv = k.sb("wkv", [128, 2 * 2 * C])
        idx = k.sb("idx", [128, TILES * POINTS], U32)
        wgt = k.sb("wgt", [128, TILES, POINTS * 4])
        q = k.sb("q", [128, TILES, C])
        g = k.sb("g", [128, GB, POINTS * 4, C])
        m = k.sb("m", [128, 2, 4, POINTS, C])
        st = k.sb("st", [128, 2, 4, 128])
        prod = k.sb("prod", [128, POINTS, C])
        sc = k.sb("sc", [128, 2, POINTS, POINTS])
        mx = k.sb("mx", [128, POINTS])
        z = k.sb("z", [128, POINTS])
        pv = k.sb("pv", [128, POINTS, C])
        y = k.sb("y", [128, TILES, C])
        ps_a = k.ps("ps_a", [128, 2, 512])
        ps_t = k.ps("ps_t", [128, 2, 4, 128])
        ps_k = k.ps("ps_k", [128, 2, POINTS, 2 * C])
        s_w = k.sem("weights_in")
        s_chain = k.sem("dve_step")
        s_pchain = k.sem("pool_step")
        s_i = k.sem("indices_in")
        s_gq = k.gather_sem("features_gathered")
        s_q = k.sem("query_features")
        s_x = k.sem("features_turned")
        s_xk = k.sem("features_turned_kept")
        s_o = k.sem("projected")
        s_var = k.sem("variance")
        s_std = k.sem("deviation")
        s_u = k.sem("gelu_argument")
        s_th = k.sem("tanh")
        s_h = k.sem("hidden")
        s_ht = k.sem("hidden_turned")
        s_hk = k.sem("hidden_turned_kept")
        s_p = k.sem("offsets")
        s_pt = k.sem("points")
        s_g = [k.gather_sem(f"gathered_{i}") for i in range(GB)]
        s_m = k.sem("corners_weighted")
        s_t = k.sem("corners_summed")
        s_st = k.sem("samples_kept")
        s_k = k.sem("keys_values")
        s_s = k.sem("scores_shifted")
        s_e = k.sem("exponents")
        s_v = k.sem("tiles_done")
        s_out = k.sem("rows_out")
        s_late = k.sem("rows_of_last_batch_out")

        with nc.Block() as block:
            @block.sync
            def _(sp):
                for dst, name in ((w1, "a_w1"), (w2, "a_w2"), (eye, "eye"), (wq4, "a_wq4"), (ref, "a_ref"), (wkv, "b_wkv")):
                    sp.dma_start(dst[:], w[name]).then_inc(s_w, 16)
                sp.dma_start(lng[:], w["a_lng"].partition_broadcast(128)).then_inc(s_w, 16)
                sp.dma_start(lnb[:], w["a_lnb"].partition_broadcast(128)).then_inc(s_w, 16)
                sp.wait_ge(s_w, 128)

            @block.gpsimd
            def _(pool):
                chain = Chain(pool, s_pchain)
                chain(pool.memset(xt[C:C + 1], 1.0))
                chain(pool.memset(hT[:], 0.0))
                chain(pool.memset(hT[32:33], 1.0))
        k.rewind()

        class Points:

            @staticmethod
            def load(sp, b):
                sp.dma_start(qidx[:], w["a_qidx"][bass.ds(b * 128, 128), :]).then_inc(s_i, 16)
                sp.dma_start(first[:], w["a_first"][bass.ds(b * 128, 128), :]).then_inc(s_i, 16)

            @staticmethod
            def gather(pool):
                pool.wait_ge(s_i, 32)
                for t in range(TILES):
                    pool.indirect_dma_start(gq[:, t].rearrange("p k c -> p (k c)"), None, fmap,
                                            bass.IndirectOffsetOnAxis(ap=qidx[:, t:t + 1], axis=0)).then_inc(s_gq, 16)

            @staticmethod
            def turn_features(pe):
                pe.wait_ge(s_q, 1)
                for t in range(TILES):
                    last = pe.transpose(ps_a[0:C, t // 4, 128 * (t % 4):128 * (t % 4) + 128], qf[:, t], eye[:])
                last.then_inc(s_x, 1)

            @staticmethod
            def project(pe):
                pe.wait_ge(s_xk, 1)
                for t in range(TILES):
                    last = pe.matmul(ps_a[:, t // 4, 80 * (t % 4):80 * (t % 4) + 80], xt[:, t], w1[:], start=True, stop=True)
                last.then_inc(s_o, 1)

            @staticmethod
            def turn_hidden(pe):
                pe.wait_ge(s_h, 1)
                for t in range(TILES):
                    last = pe.transpose(ps_a[0:16, t // 4, 128 * (t % 4):128 * (t % 4) + 128], hn[:, t], eye[:])
                last.then_inc(s_ht, 1)

            @staticmethod
            def offsets(pe):
                pe.wait_ge(s_hk, 1)
                for t in range(TILES):
                    last = pe.matmul(ps_a[:, 0, 16 * t:16 * t + 16], hT[:, t], w2[:], start=True, stop=True)
                last.then_inc(s_p, 1)

            @staticmethod
            def roots(act):
                act.wait_ge(s_var, 1)
                act.activation(std[:], var[:], ACT.Sqrt).then_inc(s_std, 1)
                act.wait_ge(s_u, 1)
                act.activation(th[:], th[:], ACT.Tanh, scale=0.7978845608028654).then_inc(s_th, 1)

            @staticmethod
            def mix_features(dve, chain):
                dve.wait_ge(s_gq, 16 * TILES)
                chain(dve.tensor_tensor(gq[:].rearrange("p t k c -> p (t k) c"), gq[:].rearrange("p t k c -> p (t k) c"),
                                        spread(wq4[:].rearrange("p t k -> p (t k)"), [128, TILES * 4, C]), ALU.mult))
                chain(dve.tensor_tensor(gq[:, :, 0:2], gq[:, :, 0:2], gq[:, :, 2:4], ALU.add))
                dve.tensor_tensor(qf[:], gq[:, :, 0], gq[:, :, 1], ALU.add).then_inc(s_q, 1)

            @staticmethod
            def keep_features(dve, chain):
                dve.wait_ge(s_x, 1)
                dve.tensor_copy(xt[0:C].rearrange("p t q -> p (t q)"), ps_a[0:C].rearrange("p a n -> p (a n)")).then_inc(s_xk, 1)

            @staticmethod
            def hidden(dve, chain):
                dve.wait_ge(s_o, 1)
                po = ps_a[:, :, 0:320].rearrange("p a (t m) -> p a t m", t=4)
                dve.tensor_scalar(next_q[:].rearrange("p (a t) c -> p a t c", a=2), po[:, :, :, 0:C], float(DH) ** -0.5, None, ALU.mult)
                chain(dve.tensor_copy(o1[:].rearrange("p (a t) c -> p a t c", a=2), po[:, :, :, C:C + 16]))
                layer_norm(dve, chain, o1[:], hn[:], sq[:], mu[:], var[:], std[:], s_var, s_std, LN_EPS, depth=16)
                every = lambda u: u[:].unsqueeze(1).to_broadcast([128, TILES, 16])
                chain(dve.tensor_tensor(hn[:], hn[:], every(lng), ALU.mult))
                chain(dve.tensor_tensor(hn[:], hn[:], every(lnb), ALU.add))
                chain(dve.tensor_tensor(th[:], hn[:], hn[:], ALU.mult))
                chain(dve.tensor_scalar(th[:], th[:], 0.044715, 1.0, ALU.mult, ALU.add))
                dve.tensor_tensor(th[:], th[:], hn[:], ALU.mult).then_inc(s_u, 1)
                dve.wait_ge(s_u, 1)

            @staticmethod
            def gelu(dve, chain):
                dve.wait_ge(s_th, 1)
                dve.scalar_tensor_tensor(hn[:], th[:], 1.0, hn[:], ALU.add, ALU.mult).then_inc(s_h, 1)

            @staticmethod
            def keep_hidden(dve, chain):
                dve.wait_ge(s_ht, 1)
                dve.tensor_scalar(hT[0:16].rearrange("p t q -> p (t q)"), ps_a[0:16].rearrange("p a n -> p (a n)"), 0.5, None,
                                  ALU.mult).then_inc(s_hk, 1)

            @staticmethod
            def corners(dve, chain):
                dve.wait_ge(s_p, 1)
                p3 = pos[:]
                chain(dve.tensor_scalar(p3, ps_a[:, 0, 0:128].rearrange("p (a x) -> p a x", x=2), OFFSET_SCALE,
                                        float(np.float32(2.0 / (SIDE - 1))), ALU.mult, ALU.mult))
                p4 = pos[:].rearrange("p (t a) x -> p t a x", t=TILES)
                chain(dve.tensor_tensor(p4, p4, ref[:].unsqueeze(2).to_broadcast([128, TILES, POINTS, 2]), ALU.add))
                chain(dve.tensor_scalar(p3, p3, 1.0, 0.5, ALU.add, ALU.mult))
                chain(dve.tensor_scalar(p3, p3, float(SIDE - 1), -1.0, ALU.mult, ALU.max))
                chain(dve.tensor_scalar(p3, p3, float(SIDE), None, ALU.min))
                chain(dve.tensor_copy(posi[:], p3))
                chain(dve.tensor_copy(low[:], posi[:]))
                chain(dve.tensor_tensor(over[:], low[:], p3, ALU.is_gt))
                chain(dve.tensor_tensor(low[:], low[:], over[:], ALU.subtract))
                chain(dve.tensor_scalar(low[:], low[:], 0.0, float(SIDE - 2), ALU.max, ALU.min))
                chain(dve.tensor_tensor(frac[:], p3, low[:], ALU.subtract))
                chain(dve.tensor_scalar(frac[:], frac[:], 0.0, 1.0, ALU.max, ALU.min))
                chain(dve.tensor_scalar(comp[:], frac[:], -1.0, 1.0, ALU.mult, ALU.add))
                chain(dve.scalar_tensor_tensor(at[:], low[:, :, 1], float(SIDE), low[:, :, 0], ALU.mult, ALU.add))
                chain(dve.tensor_scalar(at[:], at[:], first[:, 0:1], None, ALU.add))
                chain(dve.tensor_copy(next_idx[:], at[:]))
                corner_weights = next_wgt[:].rearrange("p t (a k) -> p (t a) k", k=4)
                for n, (wx, wy) in enumerate(((comp, comp), (comp, frac), (frac, comp), (frac, frac))):
                    last = dve.tensor_tensor(corner_weights[:, :, n], wx[:, :, 0], wy[:, :, 1], ALU.mult)
                last.then_inc(s_pt, 1)

        def gather(pool, t, index):
            for p in range(POINTS):
                pool.indirect_dma_start(g[:, t % GB, 4 * p:4 * p + 4].rearrange("p k c -> p (k c)"), None, fmap,
                                        bass.IndirectOffsetOnAxis(ap=index[:, POINTS * t + p:POINTS * t + p + 1], axis=0))\
                    .then_inc(s_g[t % GB], 16)

        def take_over(dve, what):
            for dst, src in what:
                dve.tensor_copy(dst[:], src[:])

        with nc.Block() as block:
            @block.sync
            def _(sp):
                Points.load(sp, 0)

            @block.gpsimd
            def _(pool):
                Points.gather(pool)
                pool.wait_ge(s_gq, 16 * TILES)
                pool.wait_ge(s_pt, 1)
                for t in range(GB):
                    gather(pool, t, next_idx)
                for t in range(GB):
                    pool.wait_ge(s_g[t], 16 * POINTS)

            @block.tensor
            def _(pe):
                Points.turn_features(pe)
                Points.project(pe)
                Points.turn_hidden(pe)
                Points.offsets(pe)

            @block.scalar
            def _(act):
                Points.roots(act)

            @block.vector
            def _(dve):
                chain = Chain(dve, s_chain)
                for step in (Points.mix_features, Points.keep_features, Points.hidden, Points.gelu, Points.keep_hidden, Points.corners):
                    step(dve, chain)
                dve.wait_ge(s_pt, 1)
                take_over(dve, ((idx, next_idx), (wgt, next_wgt), (q, next_q)))
        k.rewind()

        HALF = TILES // 2

        def store(sp, b, half, done):
            rows = bass.ds(b * SEQ + half * (NIMG // 2), NIMG // 2)
            sp.dma_start(h_out[rows, :].rearrange("(t p) c -> p t c", p=128), y[:, HALF * half:HALF * (half + 1)]).then_inc(done, 16)

        def batch(b, before, more):
            with nc.Block() as block:
                @block.sync
                def _(sp):
                    if more:
                        Points.load(sp, b + 1)
                    if before:
                        store(sp, b - 1, 1, s_late)
                    sp.wait_ge(s_v, HALF)
                    store(sp, b, 0, s_out)
                    sp.wait_ge(s_out, 16)
                    if before:
                        sp.wait_ge(s_late, 16)

                @block.gpsimd
                def _(pool):
                    if more:
                        Points.gather(pool)
                    for t in range(GB, TILES):
                        pool.wait_ge(s_m, t - GB + 1)
                        gather(pool, t, idx)
                    if more:
                        pool.wait_ge(s_pt, 1)
                        for t in range(GB):
                            pool.wait_ge(s_m, t + TILES - GB + 1)
                            gather(pool, t, next_idx)
                        pool.wait_ge(s_gq, 16 * TILES)
                    for n in range(GB):
                        pool.wait_ge(s_g[n], 16 * POINTS * (2 if more else 1))

                @block.tensor
                def _(pe):
                    def corners(t):
                        pe.wait_ge(s_m, t + 1)
                        if t >= 2:
                            pe.wait_ge(s_st, t - 1)
                        for i in range(4):
                            for n in range(4):
                                last = pe.matmul(ps_t[:, t % 2, i], m[:, t % 2, n, 2 * i:2 * i + 2, :].rearrange("p a c -> p (a c)"), eye[:], start=n == 0, stop=n == 3)
                        last.then_inc(s_t, 1)

                    def project(t):
                        pe.wait_ge(s_st, t + 1)
                        if t >= 2:
                            pe.wait_ge(s_v, t - 1)
                        for i in range(4):
                            last = pe.matmul(ps_k[:, t % 2, 2 * i:2 * i + 2].rearrange("p a c -> p (a c)"), st[:, t % 2, i], wkv[:], start=True, stop=True)
                        last.then_inc(s_k, 1)

                    for t in range(TILES + 1):
                        if t >= 1:
                            project(t - 1)
                        if more and t == 2:
                            Points.project(pe)
                        if more and t == 4:
                            Points.offsets(pe)
                        if t < TILES:
                            corners(t)
                        if more and t == 1:
                            Points.turn_features(pe)
                        if more and t == 3:
                            Points.turn_hidden(pe)

                @block.scalar
                def _(act):
                    for t in range(TILES + 1):
                        if t >= 1:
                            act.wait_ge(s_s, t)
                            act.activation(sc[:, (t - 1) % 2], sc[:, (t - 1) % 2], ACT.Exp).then_inc(s_e, 1)
                        if t < TILES:
                            act.wait_ge(s_t, t + 1)
                            if t >= 2:
                                act.wait_ge(s_k, t - 1)
                            act.activation(st[:, t % 2], ps_t[:, t % 2], ACT.Copy).then_inc(s_st, 1)
                        if more and t == 2:
                            Points.roots(act)

                @block.vector
                def _(dve):
                    chain = Chain(dve, s_chain)

                    def weight(t):
                        if t >= GB:
                            dve.wait_ge(s_g[t % GB], 16 * POINTS)
                        if t >= 2:
                            dve.wait_ge(s_t, t - 1)
                        dve.tensor_tensor(m[:, t % 2].rearrange("p k a c -> p a k c"), g[:, t % GB].rearrange("p (a k) c -> p a k c", k=4),
                                          spread(wgt[:, t], [128, 4 * POINTS, C]).rearrange("p (a k) c -> p a k c", k=4), ALU.mult).then_inc(s_m, 1)

                    def score(t):
                        dve.wait_ge(s_k, t + 1)
                        keys = ps_k[:, t % 2, :, 0:C]
                        chain(dve.tensor_tensor(prod[:], keys, q[:, t].unsqueeze(1).to_broadcast([128, POINTS, C]), ALU.mult))
                        s = sc[:, t % 2]
                        chain(dve.reduce_sum(s.rearrange("p a h -> p (a h)"), prod[:].rearrange("p a (h d) -> p (a h) d", h=POINTS), axis=AX))
                        chain(dve.reduce_max(mx[:], s.rearrange("p a h -> p h a"), axis=AX))
                        dve.tensor_tensor(s, s, mx[:].unsqueeze(1).to_broadcast([128, POINTS, POINTS]), ALU.subtract).then_inc(s_s, 1)

                    def mix(t):
                        s = sc[:, t % 2]
                        dve.wait_ge(s_e, t + 1)
                        chain(dve.reduce_sum(z[:], s.rearrange("p a h -> p h a"), axis=AX))
                        chain(dve.reciprocal(z[:], z[:]))
                        values = ps_k[:, t % 2, :, C:2 * C].rearrange("p a (h d) -> p a h d", h=POINTS)
                        chain(dve.tensor_tensor(pv[:].rearrange("p a (h d) -> p a h d", h=POINTS), values,
                                                s.unsqueeze(3).to_broadcast([128, POINTS, POINTS, DH]), ALU.mult))
                        if before and t == HALF:
                            dve.wait_ge(s_late, 16)
                        chain(dve.reduce_sum(y[:, t], pv[:].rearrange("p a c -> p c a"), axis=AX))
                        yt = y[:, t].rearrange("p (h d) -> p h d", h=POINTS)
                        dve.tensor_tensor(yt, yt, spread(z[:], [128, POINTS, DH]), ALU.mult).then_inc(s_v, 1)

                    for t in range(TILES + 1):
                        if t < TILES:
                            weight(t)
                        if more:
                            if t == 2:
                                Points.keep_features(dve, chain)
                            elif t == 3:
                                Points.gelu(dve, chain)
                            elif t == 4:
                                Points.corners(dve, chain)
                            elif t == TILES:
                                dve.wait_ge(s_pt, 1)
                                take_over(dve, ((idx, next_idx), (wgt, next_wgt)))
                        if t >= 1:
                            score(t - 1)
                            if more and t == TILES:
                                take_over(dve, ((q, next_q),))
                            mix(t - 1)
                        if more and t == 1:
                            Points.mix_features(dve, chain)
                        if more and t == 2:
                            Points.hidden(dve, chain)
                        if more and t == 3:
                            Points.keep_hidden(dve, chain)
            k.rewind()

        batch(0, False, True)
        with nc.Fori(1, BATCH - 1) as b:
            batch(b, True, True)
        batch(BATCH - 1, True, False)
        with nc.Block() as block:
            @block.sync
            def _(sp):
                store(sp, BATCH - 1, 1, s_late)
                sp.wait_ge(s_late, 16)
        k.rewind()



LAYERS = 6
TT = BATCH * NTXT // 128
PER = 128 // NTXT
HID = 256
NPOS = NIMG


def text_tokens(nc, w, h_out):
    with ExitStack() as ctx:
        k = Space(nc, ctx, "t")
        eye = k.sb("eye", [128, 128])
        heads = k.sb("heads", [C, HEADS])
        alibi = k.sb("alibi", [128, HEADS, NTXT])
        tok = k.sb("tok", [128, TT], I32)
        pos = k.sb("pos", [128, 1], I32)
        emb = k.sb("emb", [128, TT, C])
        table = k.sb("table", [128, C])
        iw = k.sb("iw", [128, 1])
        pw = k.sb("pw", [128, 1])
        lnf = k.sb("lnf", [128, 2, C])
        lnw = k.sb("lnw", [128, 4, C])
        w1 = k.sb("w1", [C + 1, HID])
        w2 = k.sb("w2", [128, 2, C])
        b2 = k.sb("b2", [128, C])
        x = k.sb("x", [128, TT, C])
        xc = k.sb("xc", [128, TT, C])
        xn = k.sb("xn", [128, TT, HEADS, DH + 1])
        sq = k.sb("sq", [128, TT, C])
        mu = k.sb("mu", [128, TT])
        var = k.sb("var", [128, TT])
        std = k.sb("std", [128, TT])
        xt = k.sb("xt", [C + 1, TT * 128])
        xm = k.sb("xm", [C, TT * PER, HEADS, NTXT])
        sc = k.sb("sc", [128, TT, HEADS, NTXT])
        mx = k.sb("mx", [128, TT, HEADS])
        pbd = k.sb("pbd", [128, TT, HEADS, 128])
        pt = k.sb("pt", [128, TT, HEADS, 128])
        z = k.sb("z", [128, TT, HEADS])
        av = k.sb("av", [128, TT, C])
        hid = k.sb("hid", [128, 2, TT * 128])
        ps_a = k.ps("ps_a", [128, 512])
        ps_s = k.ps("ps_s", [128, TT, HEADS * NTXT])
        ps_t = k.ps("ps_t", [128, 2, 512])
        ps_o = k.ps("ps_o", [128, TT, 128])
        ps_h = k.ps("ps_h", [128, 2, 512])
        s_w = k.sem("weights_in")
        s_chain = k.sem("dve_step")
        s_pchain = k.sem("pool_step")
        s_idx = k.sem("tokens_in")
        s_emb = k.gather_sem("embedded")
        s_lw = k.sem("layer_weights_in")
        s_var = k.sem("variance")
        s_std = k.sem("deviation")
        s_n = k.sem("normed")
        s_x = k.sem("normed_turned")
        s_xk = k.sem("normed_turned_kept")
        s_m = k.sem("heads_masked")
        s_s = k.sem("scores")
        s_sub = k.sem("scores_shifted")
        s_e = k.sem("exponents")
        s_pt = k.sem("exponents_turned")
        s_ptk = k.sem("exponents_turned_kept")
        s_o = k.sem("attended")
        s_h = k.sem("hidden")
        s_g = k.sem("gelu")
        s_y = k.sem("hidden_projected")
        s_done = k.sem("done")
        s_out = k.sem("rows_out")

        with nc.Block() as block:
            @block.sync
            def _(sp):
                sp.dma_start(tok[:], w["x_txt"]).then_inc(s_idx, 16)
                for n in range(PER):
                    sp.dma_start(pos[NTXT * n:NTXT * n + NTXT], w["pos_S"]).then_inc(s_idx, 16)
                sp.dma_start(eye[:], w["eye"]).then_inc(s_w, 16)
                sp.dma_start(heads[:], w["t_heads"]).then_inc(s_w, 16)
                sp.dma_start(alibi[:], w["t_alibi"]).then_inc(s_w, 16)
                sp.dma_start(iw[:], w["t_iw"].partition_broadcast(128)).then_inc(s_w, 16)
                sp.dma_start(pw[:], w["t_pw"].partition_broadcast(128)).then_inc(s_w, 16)
                sp.dma_start(lnf[:, 0], w["t_lnfw"].partition_broadcast(128)).then_inc(s_w, 16)
                sp.dma_start(lnf[:, 1], w["t_lnfb"].partition_broadcast(128)).then_inc(s_w, 16)
                sp.wait_ge(s_w, 112)

            @block.gpsimd
            def _(pool):
                chain = Chain(pool, s_pchain)
                chain(pool.memset(pbd[:], 0.0))
                chain(pool.memset(xt[C:C + 1], 1.0))
                chain(pool.memset(xn[:, :, :, DH:], 1.0))
                pool.wait_ge(s_idx, 16 * (1 + PER))
                for t in range(TT):
                    pool.indirect_dma_start(emb[:, t], None, w["t_emb"],
                                            bass.IndirectOffsetOnAxis(ap=tok[:, t:t + 1], axis=0)).then_inc(s_emb, 16)
                pool.indirect_dma_start(table[:], None, w["t_table"],
                                        bass.IndirectOffsetOnAxis(ap=pos[:, 0:1], axis=0)).then_inc(s_emb, 16)
                pool.wait_ge(s_emb, 16 * (TT + 1))

            @block.vector
            def _(dve):
                chain = Chain(dve, s_chain)
                dve.wait_ge(s_w, 112)
                dve.wait_ge(s_emb, 16 * (TT + 1))
                chain(dve.tensor_scalar(table[:], table[:], pw[:, 0:1], None, ALU.mult))
                chain(dve.tensor_scalar(emb[:], emb[:], iw[:, 0:1], None, ALU.mult))
                chain(dve.tensor_tensor(x[:], emb[:], table[:].unsqueeze(1).to_broadcast([128, TT, C]), ALU.add))
        k.rewind()

        with nc.Fori(0, LAYERS) as layer:
            with nc.Block() as block:
                @block.sync
                def _(sp):
                    one = bass.ds(layer, 1)
                    for m, name in enumerate(("t_ln1w", "t_ln1b", "t_ln2w", "t_ln2b")):
                        sp.dma_start(lnw[:, m], w[name][one, :].rearrange("a c -> (a c)").partition_broadcast(128)).then_inc(s_lw, 16)
                    sp.dma_start(w1[:], w["t_w1"][bass.ds(layer * (C + 1), C + 1), :]).then_inc(s_lw, 16)
                    sp.dma_start(w2[:], w["t_w2"][bass.ds(layer * HID, HID), :].rearrange("(a p) c -> p a c", a=2)).then_inc(s_lw, 16)
                    sp.dma_start(b2[:], w["t_b2"][one, :].rearrange("a c -> (a c)").partition_broadcast(128)).then_inc(s_lw, 16)
                    sp.wait_ge(s_lw, 112)

                @block.tensor
                def _(pe):
                    pe.wait_ge(s_n, 1)
                    for t in range(TT):
                        last = pe.transpose(ps_a[0:C, 128 * t:128 * t + 128], xc[:, t], eye[:])
                    last.then_inc(s_x, 1)
                    pe.wait_ge(s_m, HEADS)
                    for t in range(TT):
                        for n in range(PER):
                            j = PER * t + n
                            last = pe.matmul(ps_s[NTXT * n:NTXT * n + NTXT, t], xt[0:C, NTXT * j:NTXT * j + NTXT],
                                             xm[:, j].rearrange("p h s -> p (h s)"), start=True, stop=True,
                                             tile_position=(0, NTXT * n))
                    last.then_inc(s_s, 1)
                    pe.wait_ge(s_e, PER)
                    for i in range(2 * TT):
                        if i >= 2:
                            pe.wait_ge(s_ptk, i - 1)
                        for h in range(4):
                            last = pe.transpose(ps_t[:, i % 2, 128 * h:128 * h + 128], pbd[:, i // 2, 4 * (i % 2) + h], eye[:])
                        last.then_inc(s_pt, 1)
                    pe.wait_ge(s_ptk, 2 * TT)
                    for t in range(TT):
                        for h in range(HEADS):
                            last = pe.matmul(ps_o[:, t, (DH + 1) * h:(DH + 1) * h + DH + 1], pt[:, t, h], xn[:, t, h], start=True, stop=True)
                    last.then_inc(s_o, 1)
                    pe.wait_ge(s_n, 2)
                    for t in range(TT):
                        last = pe.transpose(ps_a[0:C, 128 * t:128 * t + 128], xc[:, t], eye[:])
                    last.then_inc(s_x, 1)
                    pe.wait_ge(s_xk, 2)
                    pe.wait_ge(s_lw, 112)
                    for a in range(2):
                        pe.matmul(ps_h[:, a], w1[:, 128 * a:128 * a + 128], xt[:], start=True, stop=True).then_inc(s_h, 1)
                    pe.wait_ge(s_g, 2)
                    for t in range(TT):
                        for a in range(2):
                            last = pe.matmul(ps_t[:, 0, C * t:C * t + C], hid[:, a, 128 * t:128 * t + 128], w2[:, a], start=a == 0, stop=a == 1)
                    last.then_inc(s_y, 1)

                @block.scalar
                def _(act):
                    act.wait_ge(s_var, 1)
                    act.activation(std[:], var[:], ACT.Sqrt).then_inc(s_std, 1)
                    act.wait_ge(s_sub, 1)
                    for n in range(PER):
                        rows = slice(NTXT * n, NTXT * n + NTXT)
                        act.activation(pbd[rows, :, :, rows], sc[rows], ACT.Exp).then_inc(s_e, 1)
                    act.wait_ge(s_var, 2)
                    act.activation(std[:], var[:], ACT.Sqrt).then_inc(s_std, 1)
                    for a in range(2):
                        act.wait_ge(s_h, a + 1)
                        act.activation(hid[:, a], ps_h[:, a], ACT.Gelu).then_inc(s_g, 1)

                @block.vector
                def _(dve):
                    chain = Chain(dve, s_chain)

                    def norm(m):
                        layer_norm(dve, chain, x[:], xc[:], sq[:], mu[:], var[:], std[:], s_var, s_std, LN_EPS, n_var=m + 1)
                        every = lambda u: lnw[:, u].unsqueeze(1).to_broadcast([128, TT, C])
                        chain(dve.tensor_tensor(xc[:], xc[:], every(2 * m), ALU.mult))
                        dve.tensor_tensor(xc[:], xc[:], every(2 * m + 1), ALU.add).then_inc(s_n, 1)

                    dve.wait_ge(s_lw, 112)
                    norm(0)
                    dve.wait_ge(s_n, 1)
                    chain(dve.tensor_copy(xn[:, :, :, 0:DH], xc[:].rearrange("p t (h d) -> p t h d", h=HEADS)))
                    dve.wait_ge(s_x, 1)
                    dve.tensor_copy(xt[0:C], ps_a[0:C]).then_inc(s_xk, 1)
                    dve.wait_ge(s_xk, 1)
                    rows = xt[0:C].rearrange("p (j s) -> p j s", s=NTXT)
                    for h in range(HEADS):
                        dve.tensor_scalar(xm[:, :, h], rows, heads[:, h:h + 1], None, ALU.mult).then_inc(s_m, 1)
                    dve.wait_ge(s_s, 1)
                    for t in range(TT):
                        last = dve.scalar_tensor_tensor(sc[:, t].rearrange("p h s -> p (h s)"), ps_s[:, t], float(DH) ** -0.5,
                                                        alibi[:].rearrange("p h s -> p (h s)"), ALU.mult, ALU.add)
                    chain(last)
                    chain(dve.reduce_max(mx[:], sc[:], axis=AX))
                    dve.tensor_tensor(sc[:], sc[:], spread(mx[:], [128, TT, HEADS, NTXT]), ALU.subtract).then_inc(s_sub, 1)
                    for i in range(2 * TT):
                        dve.wait_ge(s_pt, i + 1)
                        dve.tensor_copy(pt[:, i // 2, 4 * (i % 2):4 * (i % 2) + 4].rearrange("p h n -> p (h n)"), ps_t[:, i % 2]).then_inc(s_ptk, 1)
                    dve.wait_ge(s_o, 1)
                    for t in range(TT):
                        both = ps_o[:, t, 0:HEADS * (DH + 1)].rearrange("p (h d) -> p h d", h=HEADS)
                        last = dve.reciprocal(z[:, t], both[:, :, DH])
                    chain(last)
                    for t in range(TT):
                        both = ps_o[:, t, 0:HEADS * (DH + 1)].rearrange("p (h d) -> p h d", h=HEADS)
                        last = dve.tensor_tensor(av[:, t].rearrange("p (h d) -> p h d", h=HEADS), both[:, :, 0:DH],
                                                 spread(z[:, t], [128, HEADS, DH]), ALU.mult)
                    chain(last)
                    chain(dve.tensor_tensor(x[:], x[:], av[:], ALU.add))
                    norm(1)
                    dve.wait_ge(s_x, 2)
                    dve.tensor_copy(xt[0:C], ps_a[0:C]).then_inc(s_xk, 1)
                    chain(dve.tensor_tensor(x[:], x[:], b2[:].unsqueeze(1).to_broadcast([128, TT, C]), ALU.add))
                    dve.wait_ge(s_y, 1)
                    chain(dve.tensor_tensor(x[:].rearrange("p t c -> p (t c)"), x[:].rearrange("p t c -> p (t c)"), ps_t[:, 0, 0:TT * C], ALU.add))
            k.rewind()

        with nc.Block() as block:
            @block.scalar
            def _(act):
                act.wait_ge(s_var, 1)
                act.activation(std[:], var[:], ACT.Sqrt).then_inc(s_std, 1)

            @block.vector
            def _(dve):
                chain = Chain(dve, s_chain)
                layer_norm(dve, chain, x[:], xc[:], sq[:], mu[:], var[:], std[:], s_var, s_std, LN_EPS)
                chain(dve.tensor_tensor(xc[:], xc[:], lnf[:, 0].unsqueeze(1).to_broadcast([128, TT, C]), ALU.mult))
                dve.tensor_tensor(xc[:], xc[:], lnf[:, 1].unsqueeze(1).to_broadcast([128, TT, C]), ALU.add).then_inc(s_done, 1)

            @block.sync
            def _(sp):
                sp.wait_ge(s_done, 1)
                for j in range(TT * PER):
                    n = j % PER
                    sp.dma_start(h_out[SEQ * j + NIMG:SEQ * (j + 1), :], xc[NTXT * n:NTXT * n + NTXT, j // PER]).then_inc(s_out, 16)
                sp.wait_ge(s_out, 16 * TT * PER)
        k.rewind()



KEEP = SEQ // 2
ROUNDS = 26
PIECE = 352
DVE_TILES = (0, 1, 2, 3)
ACT_TILES = ((4, 5), (6, 7, 8))


def height(t):
    return TAIL if t == NT - 1 else 128


def l0_attention(nc, w, h_in, h_out):
    with ExitStack() as ctx:
        k = Space(nc, ctx, "c")
        wqk = k.sb("wqk", [C + 1, 2, 128])
        wvt = k.sb("wvt", [C, C + 1])
        wout = k.sb("wout", [C, C])
        wvo = k.sb("wvo", [C + 1, C])
        bout = k.sb("bout", [128, C])
        eye = k.sb("eye", [128, 128])
        x = k.sb("x", [128, NT, C])
        xn = k.sb("xn", [128, NT, C])
        sq = k.sb("sq", [128, NT, C])
        y = k.sb("y", [128, 2, NT, C])
        mu = k.sb("mu", [128, NT])
        var = k.sb("var", [128, NT])
        std = k.sb("std", [128, NT])
        xt = k.sb("xt", [C + 1, SEQ])
        qt = k.sb("qt", [128, SEQ])
        kt = k.sb("kt", [128, SEQ])
        v = k.sb("v", [128, 2, NT, C])
        s = k.sb("s", [128, 2, NT, SEQ])
        top = k.sb("top", [128, 2, NT])
        low = k.sb("low", [128, 2, NT])
        rng = k.sb("rng", [128, 2, NT])
        base = k.sb("base", [128, NT])
        cand = k.sb("cand", [128, 2, NT])
        cnt = k.sb("cnt", [128, 2, NT])
        hit = k.sb("hit", [128, 2, NT])
        nshift = k.sb("nshift", [128, 2, NT])
        z = k.sb("z", [128, 2, NT])
        junk_d = k.sb("junk_d", [128, 4, SEQ], BF16)
        junk_a = k.sb("junk_a", [128, 5, SEQ], BF16)
        pt = k.sb("pt", [128, 2, NT, 128])
        ps_s = k.ps("ps_s", [128, 2, 3, 512])
        ps_m = k.ps("ps_m", [128, 2, 512])
        s_w = k.sem("weights_in")
        s_chain = k.sem("dve_step")
        s_pchain = k.sem("pool_step")
        s_wv = k.sem("value_weights_made")
        s_x = k.sem("rows_in")
        s_xn = k.sem("normed")
        s_res = k.sem("residual_kept")
        s_var = k.sem("variance")
        s_std = k.sem("deviation")
        s_tr = k.sem("transposed")
        s_xt = k.sem("transposes_kept")
        s_q = k.sem("queries")
        s_qt = k.sem("queries_kept")
        s_k = k.sem("keys")
        s_kt = k.sem("keys_kept")
        s_v = k.sem("values")
        s_vk = k.sem("values_kept")
        s_s = k.sem("scores")
        s_sk = k.sem("scores_kept")
        s_low = k.sem("lowest_scores")
        s_rng = k.sem("intervals")
        s_cd = k.sem("dve_counts")
        s_ca = [k.sem("act_counts_0"), k.sem("act_counts_1")]
        s_up = [k.sem("act_candidates_0"), k.sem("act_candidates_1")]
        s_mask = k.sem("scores_masked")
        s_ns = k.sem("shifts")
        s_p = k.sem("probabilities")
        s_pt = k.sem("probabilities_transposed")
        s_ptk = k.sem("probabilities_kept")
        s_o = k.sem("outputs")
        s_y = k.sem("rows_done")
        s_out = k.sem("rows_out")

        with nc.Block() as block:
            @block.sync
            def _(sp):
                sp.dma_start(wqk[:, :, 0:C], w["c_wqk"]).then_inc(s_w, 16)
                sp.dma_start(wvt[:], w["c_wvt"]).then_inc(s_w, 16)
                sp.dma_start(wout[:], w["c_wout"]).then_inc(s_w, 16)
                sp.dma_start(bout[:], w["c_bout"].partition_broadcast(128)).then_inc(s_w, 16)
                sp.dma_start(eye[:], w["eye"]).then_inc(s_w, 16)
                sp.wait_ge(s_w, 80)

            @block.gpsimd
            def _(pool):
                chain = Chain(pool, s_pchain)
                chain(pool.memset(wqk[:, :, C:128], 0.0))
                chain(pool.memset(x[:], 0.0))
                chain(pool.memset(xt[C:C + 1], 1.0))
                chain(pool.memset(top[:], 0.0))
                chain(pool.memset(low[:], 0.0))
                chain(pool.memset(cnt[:], 0.0))
                chain(pool.memset(hit[:], 0.0))
                chain(pool.memset(z[:], 1.0))

            @block.tensor
            def _(pe):
                pe.wait_ge(s_w, 80)
                pe.matmul(ps_m[0:C + 1, 0, 0:C], wvt[:], wout[:], start=True, stop=True).then_inc(s_wv, 1)

            @block.vector
            def _(dve):
                dve.wait_ge(s_wv, 1)
                dve.tensor_copy(wvo[:], ps_m[0:C + 1, 0, 0:C])
        k.rewind()


        def load(sp, b):
            sp.dma_start(x[:, 0:8], h_in[bass.ds(b * SEQ, NIMG), :].rearrange("(t p) c -> p t c", p=128)).then_inc(s_x, 16)
            sp.dma_start(x[0:TAIL, 8], h_in[bass.ds(b * SEQ + NIMG, TAIL), :]).then_inc(s_x, 16)

        def keep_residual(pool, to):
            pool.wait_ge(s_x, 32)
            pool.tensor_tensor(y[:, to], x[:], bout[:].unsqueeze(1).to_broadcast([128, NT, C]), ALU.add).then_inc(s_res, 1)
            pool.wait_ge(s_res, 1)

        def norm(dve, chain):
            dve.wait_ge(s_x, 32)
            layer_norm(dve, chain, x[:], xn[:], sq[:], mu[:], var[:], std[:], s_var, s_std, LN_EPS, done=s_xn)

        def keep_turned(dve):
            dve.wait_ge(s_tr, 1)
            dve.tensor_copy(xt[0:C, 0:NIMG], ps_s[0:C, 0, 0:2, :])
            dve.tensor_copy(xt[0:C, NIMG:SEQ], ps_s[0:C, 0, 2, 0:TAIL]).then_inc(s_xt, 1)

        def keep_keys(act):
            act.wait_ge(s_k, 1)
            act.activation(kt[:], ps_s[:, 0, :, 0:PIECE], ACT.Copy).then_inc(s_kt, 1)

        def keep_values(act, to):
            act.wait_ge(s_v, 1)
            act.activation(v[:, to, 0:5], ps_m[:, 0, 0:5 * C].rearrange("p (t c) -> p t c", c=C), ACT.Copy)
            act.activation(v[:, to, 5:8], ps_m[:, 1, 0:3 * C].rearrange("p (t c) -> p t c", c=C), ACT.Copy)
            act.activation(v[0:TAIL, to, 8], ps_m[0:TAIL, 1, 3 * C:4 * C], ACT.Copy).then_inc(s_vk, 1)

        def keep_scores(dve, chain, to, t):
            n = height(t)
            dve.wait_ge(s_s, t + 1)
            dve.tensor_scalar(s[0:n, to, t], ps_s[0:n, t % 2, :, 0:PIECE], 0.125, None, ALU.mult, ALU.max,
                              accum_out=top[0:n, to, t:t + 1]).then_inc(s_sk, 1)
            dve.wait_ge(s_sk, t + 1)
            chain(dve.tensor_reduce(low[0:n, to, t:t + 1], s[0:n, to, t], axis=AX, op=ALU.min))

        def intervals(dve, chain, to):
            chain(dve.tensor_scalar(nshift[:, to], top[:, to], 0.0, -1.0, ALU.max, ALU.mult))
            chain(dve.tensor_tensor(rng[:, to], top[:, to], low[:, to], ALU.subtract))
            chain(dve.scalar_tensor_tensor(cand[:, to], rng[:, to], 0.5, low[:, to], ALU.mult, ALU.add))

        def queries(act):
            act.wait_ge(s_q, 1)
            act.activation(qt[:], ps_s[:, 1, :, 0:PIECE], ACT.Copy).then_inc(s_qt, 1)

        def head_products(pe, after_tail):
            if after_tail:
                pe.wait_ge(s_ptk, NT)
                pe.wait_ge(s_y, NT)
            pe.wait_ge(s_xn, 1)
            for t in range(NT):
                n = height(t)
                last = pe.transpose(ps_s[0:C, 0, t // 4, 128 * (t % 4):128 * (t % 4) + n], xn[0:n, t, :], eye[0:n, 0:n])
            last.then_inc(s_tr, 1)
            pe.wait_ge(s_xt, 1)
            for c in range(3):
                last = pe.matmul(ps_s[:, 1, c, 0:PIECE], wqk[:, 0], xt[:, PIECE * c:PIECE * (c + 1)], start=True, stop=True)
            last.then_inc(s_q, 1)
            for c in range(3):
                last = pe.matmul(ps_s[:, 0, c, 0:PIECE], wqk[:, 1], xt[:, PIECE * c:PIECE * (c + 1)], start=True, stop=True)
            last.then_inc(s_k, 1)
            for t in range(NT):
                n = height(t)
                last = pe.matmul(ps_m[0:n, t // 5, C * (t % 5):C * (t % 5) + C], xt[:, 128 * t:128 * t + n], wvo[:], start=True, stop=True)
            last.then_inc(s_v, 1)
            pe.wait_ge(s_qt, 1)
            pe.wait_ge(s_kt, 1)
            for t in range(NT):
                n = height(t)
                if t >= 2:
                    pe.wait_ge(s_sk, t - 1)
                for c in range(3):
                    last = pe.matmul(ps_s[0:n, t % 2, c, 0:PIECE], qt[:, 128 * t:128 * t + n],
                                     kt[:, PIECE * c:PIECE * (c + 1)], start=True, stop=True)
                last.then_inc(s_s, 1)


        def mask(dve, of, t):
            n = height(t)
            dve.scalar_tensor_tensor(s[0:n, of, t], s[0:n, of, t], low[0:n, of, t:t + 1], s[0:n, of, t], ALU.is_ge, ALU.mult).then_inc(s_mask, 1)

        def exponents(act, of, t):
            n = height(t)
            act.wait_ge(s_mask, t + 1)
            act.activation(s[0:n, of, t], s[0:n, of, t], ACT.Exp, bias=nshift[0:n, of, t:t + 1], accum_out=z[0:n, of, t:t + 1]).then_inc(s_p, 1)

        def transpose_probabilities(pe, of, t):
            n = height(t)
            pe.wait_ge(s_p, t + 1)
            if t >= 2:
                pe.wait_ge(s_ptk, t - 1)
            for c in range(NT):
                m = height(c)
                last = pe.transpose(ps_s[0:m, t % 2, c // 4, 128 * (c % 4):128 * (c % 4) + n],
                                    s[0:n, of, t, 128 * c:128 * c + m], eye[0:n, 0:n])
            last.then_inc(s_pt, 1)

        def keep_transposes(act, t):
            n = height(t)
            act.wait_ge(s_pt, t + 1)
            if t >= 2:
                act.wait_ge(s_o, t - 1)
            act.activation(pt[:, t % 2, 0:8, 0:n], ps_s[:, t % 2, 0:2].rearrange("p a (c s) -> p (a c) s", c=4)[:, :, 0:n], ACT.Copy)
            act.activation(pt[0:TAIL, t % 2, 8, 0:n], ps_s[0:TAIL, t % 2, 2, 0:n], ACT.Copy).then_inc(s_ptk, 1)

        def mix(pe, of, t):
            n = height(t)
            pe.wait_ge(s_ptk, t + 1)
            if t >= 2:
                pe.wait_ge(s_y, t - 1)
            for c in range(NT):
                m = height(c)
                last = pe.matmul(ps_m[0:n, t % 2, 0:C], pt[0:m, t % 2, c, 0:n], v[0:m, of, c], start=c == 0, stop=c == NT - 1)
            last.then_inc(s_o, 1)

        def tail_products(pe, of):
            transpose_probabilities(pe, of, 0)
            for t in range(NT):
                if t + 1 < NT:
                    transpose_probabilities(pe, of, t + 1)
                mix(pe, of, t)

        def finish(dve, chain, of, t):
            n = height(t)
            dve.wait_ge(s_p, t + 1)
            chain(dve.reciprocal(z[0:n, of, t:t + 1], z[0:n, of, t:t + 1]))
            dve.wait_ge(s_o, t + 1)
            dve.scalar_tensor_tensor(y[0:n, of, t], ps_m[0:n, t % 2, 0:C], z[0:n, of, t:t + 1], y[0:n, of, t], ALU.mult, ALU.add).then_inc(s_y, 1)

        def store(sp, b, of):
            sp.wait_ge(s_y, NT)
            sp.dma_start(h_out[bass.ds(b * SEQ, NIMG), :].rearrange("(t p) c -> p t c", p=128), y[:, of, 0:8]).then_inc(s_out, 16)
            sp.dma_start(h_out[bass.ds(b * SEQ + NIMG, TAIL), :], y[0:TAIL, of, 8]).then_inc(s_out, 16)
            sp.wait_ge(s_out, 32)

        with nc.Block() as block:
            @block.sync
            def _(sp):
                load(sp, 0)

            @block.gpsimd
            def _(pool):
                keep_residual(pool, 0)

            @block.tensor
            def _(pe):
                head_products(pe, False)

            @block.scalar
            def _(act):
                act.wait_ge(s_var, 1)
                act.activation(std[:], var[:], ACT.Sqrt).then_inc(s_std, 1)
                queries(act)
                keep_keys(act)
                keep_values(act, 0)

            @block.vector
            def _(dve):
                chain = Chain(dve, s_chain)
                norm(dve, chain)
                keep_turned(dve)
                for t in range(NT):
                    keep_scores(dve, chain, 0, t)
                intervals(dve, chain, 0)
        k.rewind()

        HEAD_AT = NT + 3

        def search(b, of, before, more):
            to = 1 - of
            with nc.Block() as block:
                @block.sync
                def _(sp):
                    if more:
                        load(sp, b + 1)
                    if before:
                        store(sp, b - 1, to)

                @block.tensor
                def _(pe):
                    if before:
                        tail_products(pe, to)
                    if more:
                        head_products(pe, before)

                @block.vector
                def _(dve):
                    chain = Chain(dve, s_chain)
                    d = slice(0, len(DVE_TILES))
                    for r in range(ROUNDS):
                        for t in DVE_TILES:
                            dve.tensor_scalar(junk_d[:, t], s[:, of, t], cand[:, of, t:t + 1], None, ALU.is_ge, ALU.add,
                                              accum_out=cnt[:, of, t:t + 1]).then_inc(s_cd, 1)
                        dve.wait_ge(s_cd, len(DVE_TILES) * (r + 1))
                        chain(dve.scalar_tensor_tensor(hit[:, of, d], cnt[:, of, d], float(KEEP), rng[:, of, d], ALU.is_ge, ALU.mult))
                        chain(dve.scalar_tensor_tensor(low[:, of, d], hit[:, of, d], 0.5 ** (r + 1), low[:, of, d], ALU.mult, ALU.add))
                        if r + 1 < ROUNDS:
                            chain(dve.scalar_tensor_tensor(cand[:, of, d], rng[:, of, d], 0.5 ** (r + 2), low[:, of, d], ALU.mult, ALU.add))
                        if before:
                            if r < NT:
                                mask(dve, to, r)
                            if 3 <= r < NT + 3:
                                finish(dve, chain, to, r - 3)
                        if more:
                            if r == HEAD_AT:
                                norm(dve, chain)
                            elif r == HEAD_AT + 1:
                                keep_turned(dve)
                            elif HEAD_AT + 3 <= r < HEAD_AT + 3 + NT:
                                keep_scores(dve, chain, to, r - HEAD_AT - 3)
                    if more:
                        intervals(dve, chain, to)

                @block.gpsimd
                def _(pool):
                    for r in range(ROUNDS):
                        for g, tiles in enumerate(ACT_TILES):
                            a = slice(tiles[0], tiles[-1] + 1)
                            n = 4 * r
                            pool.wait_ge(s_ca[g], len(tiles) * (r + 1))
                            pool.tensor_scalar(hit[:, of, a], cnt[:, of, a], 0.0, 0.5 ** (r + 1), ALU.is_le, ALU.mult).then_inc(s_up[g], 1)
                            pool.wait_ge(s_up[g], n + 1)
                            pool.tensor_tensor(hit[:, of, a], hit[:, of, a], rng[:, of, a], ALU.mult).then_inc(s_up[g], 1)
                            pool.wait_ge(s_up[g], n + 2)
                            pool.tensor_tensor(low[:, of, a], low[:, of, a], hit[:, of, a], ALU.add).then_inc(s_up[g], 1)
                            pool.tensor_scalar(base[:, a], rng[:, of, a], 0.5 ** (r + 2), None, ALU.mult).then_inc(s_pchain, 1)
                            pool.wait_ge(s_up[g], n + 3)
                            pool.wait_ge(s_pchain, 2 * r + g + 1)
                            pool.tensor_tensor(cand[:, of, a], base[:, a], low[:, of, a], ALU.add).then_inc(s_up[g], 1)
                        if more and r == HEAD_AT:
                            if before:
                                pool.wait_ge(s_out, 32)
                            keep_residual(pool, to)

                @block.scalar
                def _(act):
                    for r in range(ROUNDS):
                        for g, tiles in enumerate(ACT_TILES):
                            if r:
                                act.wait_ge(s_up[g], 4 * r)
                            for t in tiles:
                                n = height(t)
                                act.activation(junk_a[0:n, t - ACT_TILES[0][0]], s[0:n, of, t], ACT.Sign, bias=cand[0:n, of, t:t + 1], scale=-1.0,
                                               accum_out=cnt[0:n, of, t:t + 1]).then_inc(s_ca[g], 1)
                        if before:
                            if r < NT:
                                exponents(act, to, r)
                            if 1 <= r < NT + 1:
                                keep_transposes(act, r - 1)
                        if more:
                            if r == HEAD_AT:
                                act.wait_ge(s_var, 1)
                                act.activation(std[:], var[:], ACT.Sqrt).then_inc(s_std, 1)
                            elif r == HEAD_AT + 2:
                                queries(act)
                                keep_keys(act)
                                keep_values(act, to)
            k.rewind()

        search(0, 0, False, True)
        with nc.Fori(0, (BATCH - 2) // 2) as i:
            search(2 * i + 1, 1, True, True)
            search(2 * i + 2, 0, True, True)
        search(BATCH - 1, 1, True, False)

        of = (BATCH - 1) % 2
        with nc.Block() as block:
            @block.sync
            def _(sp):
                store(sp, BATCH - 1, of)

            @block.tensor
            def _(pe):
                tail_products(pe, of)

            @block.scalar
            def _(act):
                for t in range(NT + 1):
                    if t < NT:
                        exponents(act, of, t)
                    if t >= 1:
                        keep_transposes(act, t - 1)

            @block.vector
            def _(dve):
                chain = Chain(dve, s_chain)
                for t in range(NT):
                    mask(dve, of, t)
                for t in range(NT):
                    if t >= 1:
                        finish(dve, chain, of, t - 1)
                finish(dve, chain, of, NT - 1)
        k.rewind()



NH = 4
NE = 4
D = C // NH
QK = NE * D + D
VS = D + 1
NEG = -1e30
STACK_Q = (0, 0, 0, 1, 1, 2)
STACK_K = (0, 1, 2, 0, 1, 0)
DEPTH = len(STACK_Q) * D
SHIFT = 3
FFN_EPS = 1e-8


def ffn_project(nc, w, h_in, qk3, vals, sxn):
    with ExitStack() as ctx:
        k = Space(nc, ctx, "g")
        hlt = k.sb("hlt", [D, NH, C + 1])
        wqk = k.sb("wqk", [D, NH, QK])
        wv = k.sb("wv", [D, NH, D])
        a_qk = k.sb("a_qk", [C + 1, NH, QK])
        a_sv = k.sb("a_sv", [C + 1, 2, C])
        eye = k.sb("eye", [128, 128])
        x = k.sb("x", [128, NT, C])
        xn = k.sb("xn", [128, NT, C])
        sq = k.sb("sq", [128, NT, C])
        mu = k.sb("mu", [128, NT])
        var = k.sb("var", [128, NT])
        std = k.sb("std", [128, NT])
        xt = k.sb("xt", [C + 1, 2, SEQ])
        sv = k.sb("sv", [128, NT, 2, C])
        hi = k.sb("hi", [QK, 2, SEQ], BF16)
        rest = k.sb("rest", [QK, 2, SEQ])
        mid = k.sb("mid", [QK, 2, SEQ], BF16)
        lo = k.sb("lo", [QK, 2, SEQ], BF16)
        ps_s = k.ps("ps_s", [128, 2, 3, 512])
        ps_m = k.ps("ps_m", [128, 2, 512])
        s_w = k.sem("weights_in")
        s_chain = k.sem("dve_step")
        s_pchain = k.sem("pool_step")
        s_mm = k.sem("weights_multiplied")
        s_x = k.sem("rows_in")
        s_var = k.sem("variance")
        s_std = k.sem("deviation")
        s_xn = k.sem("normed")
        s_tr = k.sem("transposed")
        s_xt = k.sem("transposes_kept")
        s_sv = k.sem("values")
        s_svk = k.sem("values_kept")
        s_p = k.sem("projections")
        s_hi = k.sem("high_parts")
        s_rest = k.sem("remainders")
        s_mid = k.sem("middle_parts")
        s_lo = k.sem("low_parts")
        s_out = k.sem("values_out")
        s_o = [k.sem("parts_out_0"), k.sem("parts_out_1")]

        with nc.Block() as block:
            @block.sync
            def _(sp):
                for dst, name in ((hlt, "g_hlt"), (wqk, "g_wqk"), (wv, "g_wv"), (eye, "eye")):
                    sp.dma_start(dst[:], w[name]).then_inc(s_w, 16)
                sp.dma_start(a_sv[:, 0], w["g_hl"]).then_inc(s_w, 16)
                sp.wait_ge(s_w, 80)

            @block.gpsimd
            def _(pool):
                chain = Chain(pool, s_pchain)
                chain(pool.memset(x[:], 0.0))
                chain(pool.memset(xt[C:C + 1], 1.0))

            @block.tensor
            def _(pe):
                pe.wait_ge(s_w, 80)
                for n in range(NH):
                    pe.matmul(ps_s[0:C + 1, 0, 0, QK * n:QK * n + QK], hlt[:, n], wqk[:, n], start=True, stop=True)
                    last = pe.matmul(ps_s[0:C + 1, 0, 1, D * n:D * n + D], hlt[:, n], wv[:, n], start=True, stop=True)
                last.then_inc(s_mm, 1)

            @block.vector
            def _(dve):
                dve.wait_ge(s_mm, 1)
                p = ps_s[0:C + 1, 0, 0, 0:NH * QK].rearrange("p (n m) -> p n m", n=NH)
                dve.tensor_scalar(a_qk[:, :, 0:NE * D], p[:, :, 0:NE * D], float(D) ** 0.5, None, ALU.mult)
                dve.tensor_copy(a_qk[:, :, NE * D:QK], p[:, :, NE * D:QK])
                dve.tensor_copy(a_sv[:, 1], ps_s[0:C + 1, 0, 1, 0:C])
        k.rewind()

        def load(sp, b):
            sp.dma_start(x[:, 0:8], h_in[bass.ds(b * SEQ, NIMG), :].rearrange("(t p) c -> p t c", p=128)).then_inc(s_x, 16)
            sp.dma_start(x[0:TAIL, 8], h_in[bass.ds(b * SEQ + NIMG, TAIL), :]).then_inc(s_x, 16)

        def norm(dve, chain):
            dve.wait_ge(s_x, 32)
            layer_norm(dve, chain, x[:], xn[:], sq[:], mu[:], var[:], std[:], s_var, s_std, LN_EPS, done=s_xn)

        def root(act):
            act.wait_ge(s_var, 1)
            act.activation(std[:], var[:], ACT.Sqrt).then_inc(s_std, 1)

        def turn(pe):
            pe.wait_ge(s_xn, 1)
            for t in range(NT):
                n = height(t)
                if t == NT - 1:
                    pe.wait_ge(s_xt, 1)
                last = pe.transpose(ps_m[0:C, (t // 4) % 2, 128 * (t % 4):128 * (t % 4) + n], xn[0:n, t, :], eye[0:n, 0:n])
                if t >= NT - 2:
                    last.then_inc(s_tr, 1)

        def keep_turned(dve, to):
            dve.wait_ge(s_tr, 1)
            dve.tensor_copy(xt[0:C, to, 0:NIMG], ps_m[0:C].rearrange("p a n -> p (a n)")).then_inc(s_xt, 1)
            dve.wait_ge(s_tr, 2)
            dve.tensor_copy(xt[0:C, to, NIMG:SEQ], ps_m[0:C, 0, 0:TAIL]).then_inc(s_xt, 1)

        with nc.Block() as block:
            @block.sync
            def _(sp):
                load(sp, 0)

            @block.tensor
            def _(pe):
                turn(pe)

            @block.scalar
            def _(act):
                root(act)

            @block.vector
            def _(dve):
                norm(dve, Chain(dve, s_chain))
                keep_turned(dve, 0)
        k.rewind()

        def project(b, of, more):
            with nc.Block() as block:
                @block.sync
                def _(sp):
                    if more:
                        load(sp, b + 1)
                    for n in range(NH):
                        for part, src, done in ((0, hi, s_hi), (1, mid, s_mid), (2, lo, s_lo)):
                            sp.wait_ge(done, n + 1)
                            row = b * (NH * 3 * QK) + (n * 3 + part) * QK
                            sp.dma_start(qk3[bass.ds(row, QK), :], src[:, n % 2]).then_inc(s_o[n % 2], 16)
                        if n == 1:
                            sp.wait_ge(s_svk, 3)
                            for dst, which in ((sxn, 0), (vals, 1)):
                                sp.dma_start(dst[bass.ds(b * SEQ, NIMG), :].rearrange("(t p) c -> p t c", p=128), sv[:, 0:8, which]).then_inc(s_out, 16)
                                sp.dma_start(dst[bass.ds(b * SEQ + NIMG, TAIL), :], sv[0:TAIL, 8, which]).then_inc(s_out, 16)
                    sp.wait_ge(s_out, 64)
                    for o in s_o:
                        sp.wait_ge(o, 96)

                @block.tensor
                def _(pe):
                    for n in range(NH):
                        if n >= 2:
                            pe.wait_ge(s_hi, n - 1)
                            pe.wait_ge(s_rest, n - 1)
                        for c in range(3):
                            last = pe.matmul(ps_s[0:QK, n % 2, c, 0:PIECE], a_qk[:, n], xt[:, of, PIECE * c:PIECE * (c + 1)], start=True, stop=True)
                        last.then_inc(s_p, 1)
                        if n == 1:
                            for t in range(NT):
                                m = height(t)
                                if t == 8:
                                    pe.wait_ge(s_svk, 1)
                                last = pe.matmul(ps_m[0:m, (t // 4) % 2, 128 * (t % 4):128 * (t % 4) + 128], xt[:, of, 128 * t:128 * t + m],
                                                 a_sv[:].rearrange("p a c -> p (a c)"), start=True, stop=True)
                                if t % 4 == 3 or t == NT - 1:
                                    last.then_inc(s_sv, 1)
                    if more:
                        pe.wait_ge(s_svk, 3)
                        turn(pe)

                @block.vector
                def _(dve):
                    chain = Chain(dve, s_chain)
                    for n in range(NH):
                        dve.wait_ge(s_hi, n + 1)
                        if n >= 2:
                            dve.wait_ge(s_lo, n - 1)
                        dve.tensor_tensor(rest[:, n % 2], ps_s[0:QK, n % 2, :, 0:PIECE], hi[:, n % 2].rearrange("p (c s) -> p c s", c=3),
                                          ALU.subtract).then_inc(s_rest, 1)
                        if n == 1:
                            for i in range(3):
                                dve.wait_ge(s_sv, i + 1)
                                m, hs = (4, 128) if i < 2 else (1, TAIL)
                                src = ps_m[0:hs, i % 2, 0:128 * m].rearrange("p (t a c) -> p t a c", t=m, a=2)
                                dve.tensor_copy(sv[0:hs, 4 * i:4 * i + m], src).then_inc(s_svk, 1)
                        if n == 2 and more:
                            norm(dve, chain)
                    if more:
                        keep_turned(dve, 1 - of)

                @block.scalar
                def _(act):
                    for n in range(NH):
                        act.wait_ge(s_p, n + 1)
                        if n >= 2:
                            act.wait_ge(s_o[n % 2], 48)
                            act.wait_ge(s_rest, n - 1)
                        act.activation(hi[:, n % 2].rearrange("p (c s) -> p c s", c=3), ps_s[0:QK, n % 2, :, 0:PIECE], ACT.Copy).then_inc(s_hi, 1)
                    if more:
                        root(act)

                @block.gpsimd
                def _(pool):
                    for n in range(NH):
                        pool.wait_ge(s_rest, n + 1)
                        if n >= 2:
                            pool.wait_ge(s_o[n % 2], 48)
                        pool.tensor_copy(mid[:, n % 2], rest[:, n % 2]).then_inc(s_mid, 1)
                        pool.wait_ge(s_mid, n + 1)
                        pool.tensor_tensor(lo[:, n % 2], rest[:, n % 2], mid[:, n % 2], ALU.subtract).then_inc(s_lo, 1)
            k.rewind()

        with nc.Fori(0, BATCH // 2 - 1) as i:
            project(2 * i, 0, True)
            project(2 * i + 1, 1, True)
        project(BATCH - 2, 0, True)
        project(BATCH - 1, 1, False)


def max_units():
    units = []
    for i in range(8):
        for c in range(i // 4 + 1):
            for pair in range(2):
                units.append((i, c, pair, min(512, 128 * (i + 1) - 512 * c)))
    return units + [(8, 0, 0, 1024), (8, 1, 0, TAIL)]


def exp_units():
    units = []
    for c in range(2):
        for j in range(4 * (c + 1)):
            s0 = max(512 * c, 128 * j)
            wide = 512 * (c + 1) - s0
            per = 1 if wide > 256 else 2 if wide > 128 else 4
            for e0 in range(0, NE, per):
                units.append((c, [(e0 + i, j, wide * i, s0, wide) for i in range(per)]))
    for j0, j1 in ((0, 4), (4, 8), (8, 9)):
        units.append((2, [(e, j, TAIL * (NE * (j - j0) + e), NIMG, TAIL) for j in range(j0, j1) for e in range(NE)]))
    return units


def exp_order(units):
    order = [("scores", 0), ("scores", 1)]
    for u in range(len(units)):
        order += [("scores", u + 2)] * (u + 2 < len(units)) + [("mix", u)]
    return order


def ffn_attend(nc, w, qk3, vals, mrow, att):
    with ExitStack() as ctx:
        k = Space(nc, ctx, "d")
        q = k.sb("q", [DEPTH + SHIFT, NH, NE, SEQ], BF16)
        ky = k.sb("ky", [DEPTH + SHIFT, NH, SEQ], BF16)
        v = k.sb("v", [128, NH, NT, 32])
        eyeb = k.sb("eyeb", [128, 128], BF16)
        eye4 = k.sb("eye4", [128, TAIL], BF16)
        consts = k.sb("consts", [128, 3 * 128 + TAIL])
        hide = k.sb("hide", [128, 128], BF16)
        hide_t = k.sb("hide_t", [128, 128], BF16)
        mx = k.sb("mx", [128, 8, 2, NE])
        mx8 = k.sb("mx8", [128, 2])
        m_ = k.sb("m_", [128, NT, NE])
        mr = k.sb("mr", [128, NT, NE])
        parts = k.sb("parts", [128, NT, 3, NE], BF16)
        p8 = k.sb("p8", [128, 3], BF16)
        mt = k.sb("mt", [12, SEQ], BF16)
        NP = 8
        pt = k.sb("pt", [128, NP, 512])
        ot = k.sb("ot", [128, 2, SEQ])
        ps1 = k.ps("ps1", [128, 2, 2, 512])
        ps2 = k.ps("ps2", [128, 2, 512])
        pso = k.ps("pso", [128, 2, 512])
        s_w = k.sem("constants_in")
        s_pchain = k.sem("pool_step")
        s_q = [k.sem(f"head_{n}_in") for n in range(NH)]
        s_p1 = k.sem("first_scores")
        s_p1k = k.sem("first_scores_read")
        s_mm = k.sem("maxima")
        s_m3 = k.sem("maxima_parts")
        s_mo = k.sem("maxima_out")
        s_row = k.sem("maxima_rows")
        s_p2 = k.sem("second_scores")
        s_e = k.sem("exponents")
        s_pv = k.sem("values_mixed")
        s_ok = k.sem("outputs_kept")
        s_out = [k.sem("outputs_out_0"), k.sem("outputs_out_1")]

        firsts = max_units()
        seconds = exp_units()
        N1 = len(firsts) + 2
        N2 = len(seconds)
        ends = [max(i for i, (c, _) in enumerate(seconds) if c == chunk) for chunk in range(3)]
        LOADS = 2 * len(STACK_Q) + 2
        order = exp_order(seconds)
        FIRSTS_BY = 24
        TURN_AT = 32

        with nc.Block() as block:
            @block.sync
            def _(sp):
                sp.dma_start(consts[:], w["d_consts"]).then_inc(s_w, 16)

            @block.vector
            def _(dve):
                dve.wait_ge(s_w, 16)
                for n, dst in enumerate((eyeb, hide, hide_t, eye4)):
                    dve.tensor_copy(dst[:], consts[:, 128 * n:min(128 * (n + 1), 3 * 128 + TAIL)])

            @block.gpsimd
            def _(pool):
                chain = Chain(pool, s_pchain)
                chain(pool.memset(v[:], 0.0))
                chain(pool.memset(v[:, :, :, D:VS], 1.0))
                chain(pool.memset(ky[DEPTH:DEPTH + SHIFT], 1.0))
                chain(pool.memset(mx[:], NEG))
                chain(pool.memset(parts[:], 0.0))
                chain(pool.memset(m_[:], 0.0))
        k.rewind()

        def load(sp, b, n):
            for g in range(len(STACK_Q)):
                row = b * (NH * 3 * QK) + (3 * n + STACK_Q[g]) * QK
                sp.dma_start(q[D * g:D * g + D, n], qk3[bass.ds(row, NE * D), :].rearrange("(e o) s -> o e s", e=NE)).then_inc(s_q[n], 16)
                row = b * (NH * 3 * QK) + (3 * n + STACK_K[g]) * QK + NE * D
                sp.dma_start(ky[D * g:D * g + D, n], qk3[bass.ds(row, D), :]).then_inc(s_q[n], 16)
            sp.dma_start(v[:, n, 0:8, 0:D], vals[bass.ds(b * SEQ, NIMG), D * n:D * n + D].rearrange("(t p) c -> p t c", p=128)).then_inc(s_q[n], 16)
            sp.dma_start(v[0:TAIL, n, 8, 0:D], vals[bass.ds(b * SEQ + NIMG, TAIL), D * n:D * n + D]).then_inc(s_q[n], 16)


        def maxima_rows(sp, n, r):
            sp.wait_ge(s_p1k, N1 * (r + 1))
            rows = slice(SHIFT * NE * n, SHIFT * NE * (n + 1))
            sp.dma_start(mrow[rows, :], mt[:]).then_inc(s_mo, 16)
            sp.wait_ge(s_mo, 16 * (r + 1))
            sp.dma_start(q[DEPTH:DEPTH + SHIFT, n], mrow[rows, :].rearrange("(j e) s -> j e s", e=NE)).then_inc(s_row, 16)

        def first(pe, n, r, i):
            u = N1 * r + i
            if u >= 2:
                pe.wait_ge(s_p1k, u - 1)
            p = ps1[:, u % 2]
            qn, kn = q[0:DEPTH, n], ky[0:DEPTH, n]
            t, c, pair, wide = firsts[i]
            if t < 8:
                for a in range(2):
                    edge = c == t // 4
                    last = pe.matmul(p[:, a, 0:wide], qn[:, 2 * pair + a, 128 * t:128 * t + 128],
                                     kn[:, 512 * c:512 * c + wide], start=True, stop=not edge)
                    if edge:
                        last = pe.matmul(p[:, a, wide - 128:wide], eyeb[:], hide[:], start=False, stop=True)
            else:
                for e in range(NE):
                    for a in range(2 - c):
                        at = 1024 if c else 512 * a
                        m = TAIL if c else 512
                        last = pe.matmul(p[32 * e:32 * e + 32, a, 0:m], qn[:, e, NIMG:SEQ], kn[:, at:at + m],
                                         start=True, stop=not c)
                    if c:
                        last = pe.matmul(p[32 * e:32 * e + 32, 0, 0:m], eyeb[:, 0:TAIL], hide[:, 0:TAIL], start=False, stop=True)
            last.then_inc(s_p1, 1)

        def turn_maxima(pe, r):
            for half in range(2):
                u = N1 * (r + 1) - 2 + half
                pe.wait_ge(s_p1k, u - 1)
                if half == 0:
                    pe.wait_ge(s_m3, r + 1)
                    for t in range(8):
                        last = pe.matmul(ps1[0:12, u % 2, t // 4, 128 * (t % 4):128 * (t % 4) + 128],
                                         parts[:, t].rearrange("p j e -> p (j e)"), eyeb[:], start=True, stop=True)
                else:
                    last = pe.matmul(ps1[0:12, u % 2, 0, 0:TAIL], parts[:, 8].rearrange("p j e -> p (j e)"), eye4[:], start=True, stop=True)
                last.then_inc(s_p1, 1)

        def read(dve, r, i):
            u = N1 * r + i
            t, c, pair, wide = firsts[i]
            if r and i == 0:
                dve.wait_ge(s_m3, r)
            dve.wait_ge(s_p1, u + 1)
            if t < 8:
                dve.reduce_max(mx[:, t, c, 2 * pair:2 * pair + 2], ps1[:, u % 2, :, 0:wide], axis=AX).then_inc(s_p1k, 1)
            elif c == 0:
                dve.tensor_reduce(mx8[:, 0:1], ps1[:, u % 2].rearrange("p a n -> p (a n)"), axis=AX, op=ALU.max).then_inc(s_p1k, 1)
            else:
                dve.reduce_max(mx8[:, 1:2], ps1[:, u % 2, 0, 0:TAIL], axis=AX).then_inc(s_p1k, 1)

        def join_maxima(dve, r):
            dve.wait_ge(s_p1k, N1 * r + len(firsts))
            dve.tensor_tensor(m_[:, 0:8], mx[:, :, 0], mx[:, :, 1], ALU.max)
            dve.tensor_tensor(m_[:, 8, 0:1], mx8[:, 0:1], mx8[:, 1:2], ALU.max).then_inc(s_mm, 1)

        def keep_maxima(dve, r):
            u = N1 * (r + 1) - 2
            if r:
                dve.wait_ge(s_mo, 16 * r)
            dve.wait_ge(s_p1, u + 1)
            dve.tensor_copy(mt[:, 0:NIMG], ps1[0:12, u % 2].rearrange("p a n -> p (a n)")).then_inc(s_p1k, 1)
            dve.wait_ge(s_p1, u + 2)
            dve.tensor_copy(mt[:, NIMG:SEQ], ps1[0:12, (u + 1) % 2, 0, 0:TAIL]).then_inc(s_p1k, 1)

        def split_maxima(pool, chain, r):
            pool.wait_ge(s_mm, r + 1)
            chain(pool.tensor_scalar(m_[:], m_[:], -1.0, 1.0, ALU.mult, ALU.mult))
            for part in range(SHIFT):
                dst = parts[:, 0:8, part]
                pool.tensor_copy(dst, m_[:, 0:8])
                chain(pool.tensor_copy(p8[:, part:part + 1], m_[:, 8, 0:1]))
                if part < 2:
                    pool.tensor_tensor(m_[:, 0:8], m_[:, 0:8], dst, ALU.subtract)
                    chain(pool.tensor_tensor(m_[:, 8, 0:1], m_[:, 8, 0:1], p8[:, part:part + 1], ALU.subtract))
            for e in range(NE):
                rows = slice(32 * e, 32 * e + 32)
                chain(pool.tensor_copy(parts[rows, 8, :, e], p8[rows, :]))
            pool.tensor_copy(mr[0:1, 0, 0:1], m_[0:1, 0, 0:1]).then_inc(s_m3, 1)
            pool.wait_ge(s_m3, r + 1)

        with nc.Block() as block:
            @block.sync
            def _(sp):
                for n in range(NH - 1):
                    load(sp, 0, n)
                maxima_rows(sp, 0, 0)
                for n in range(NH - 1):
                    sp.wait_ge(s_q[n], 16 * LOADS)
                sp.wait_ge(s_row, 16)

            @block.tensor
            def _(pe):
                pe.wait_ge(s_q[0], 16 * LOADS)
                for i in range(len(firsts)):
                    first(pe, 0, 0, i)
                turn_maxima(pe, 0)

            @block.vector
            def _(dve):
                for i in range(len(firsts)):
                    read(dve, 0, i)
                join_maxima(dve, 0)
                keep_maxima(dve, 0)

            @block.gpsimd
            def _(pool):
                split_maxima(pool, Chain(pool, s_pchain), 0)
        k.rewind()

        def store(sp, b, n):
            for e in range(NE):
                row = b * (NH * NE * VS) + (NE * n + e) * VS
                sp.dma_start(att[bass.ds(row, VS), :], ot[32 * e:32 * e + VS, n % 2]).then_inc(s_out[n % 2], 16)

        def batch(b, before, more):
            late = 1 if before else 0
            passes = NH if more else NH - 1

            def due(i):
                return min(len(firsts), -(-i * len(firsts) // FIRSTS_BY))

            with nc.Block() as block:
                @block.sync
                def _(sp):
                    if before:
                        store(sp, b - 1, NH - 1)
                    load(sp, b, NH - 1)
                    for n in range(NH):
                        if n < passes:
                            maxima_rows(sp, (n + 1) % NH, n)
                        if n < NH - 1 and more:
                            sp.wait_ge(s_pv, N2 * (n + 1))
                            load(sp, b + 1, n)
                        if n < NH - 1:
                            sp.wait_ge(s_ok, 3 * (n + 1))
                            store(sp, b, n)
                    sp.wait_ge(s_out[0], 2 * NE * 16)
                    sp.wait_ge(s_out[1], (late + 1) * NE * 16)
                    for n in range(NH):
                        if more or n == NH - 1:
                            sp.wait_ge(s_q[n], 16 * LOADS)
                    sp.wait_ge(s_row, 16 * passes)

                @block.tensor
                def _(pe):
                    def second(n, i):
                        u = N2 * n + i
                        if i == 0 and n:
                            pe.wait_ge(s_row, 16 * n)
                        if u >= 2:
                            pe.wait_ge(s_e, u - 1)
                        for e, j, col, s0, wide in seconds[i][1]:
                            m = height(j)
                            edge = s0 == 128 * j
                            last = pe.matmul(ps2[0:m, u % 2, col:col + wide], ky[:, n, 128 * j:128 * j + m],
                                             q[:, n, e, s0:s0 + wide], start=True, stop=not edge)
                            if edge:
                                d = min(128, wide)
                                last = pe.matmul(ps2[0:m, u % 2, col:col + d], eyeb[:, 0:m], hide_t[:, 0:d], start=False, stop=True)
                        last.then_inc(s_p2, 1)

                    def mix(n, i):
                        u = N2 * n + i
                        c, parts_ = seconds[i]
                        o = 3 * n + c
                        if i == 0 or seconds[i - 1][0] != c:
                            if o >= 2:
                                pe.wait_ge(s_ok, o - 1)
                        pe.wait_ge(s_e, u + 1)
                        for e, j, col, s0, wide in parts_:
                            m = height(j)
                            at = s0 - 512 * c
                            lastj = (3, 7, 8)[c]
                            last = pe.matmul(pso[32 * e:32 * e + 32, o % 2, at:at + wide], v[0:m, n, j, :], pt[0:m, u % NP, col:col + wide],
                                             start=j == 0, stop=j == lastj)
                        last.then_inc(s_pv, 1)

                    for n in range(NH):
                        for step, i in order:
                            if step == "mix":
                                mix(n, i)
                                continue
                            second(n, i)
                            if n < passes:
                                if i == 0 and n >= NH - 2:
                                    pe.wait_ge(s_q[(n + 1) % NH], 16 * LOADS)
                                for a in range(due(i), due(i + 1)):
                                    first(pe, (n + 1) % NH, n, a)
                                if i == TURN_AT:
                                    turn_maxima(pe, n)

                @block.vector
                def _(dve):
                    def keep_outputs(n, c):
                        stores = n // 2 + late * (n % 2)
                        if stores and c == 0:
                            dve.wait_ge(s_out[n % 2], NE * 16 * stores)
                        dve.wait_ge(s_pv, N2 * n + ends[c] + 1)
                        wide = (512, 512, TAIL)[c]
                        dve.tensor_copy(ot[:, n % 2, 512 * c:512 * c + wide], pso[:, (3 * n + c) % 2, 0:wide]).then_inc(s_ok, 1)

                    for n in range(NH):
                        for step, i in order:
                            if step == "mix":
                                if i in ends:
                                    keep_outputs(n, ends.index(i))
                                continue
                            if n < passes:
                                for a in range(due(i), due(i + 1)):
                                    read(dve, n, a)
                                if i == FIRSTS_BY:
                                    join_maxima(dve, n)
                                if i == TURN_AT:
                                    keep_maxima(dve, n)

                @block.gpsimd
                def _(pool):
                    chain = Chain(pool, s_pchain)
                    for n in range(passes):
                        split_maxima(pool, chain, n)

                @block.scalar
                def _(act):
                    for n in range(NH):
                        for i, (c, parts_) in enumerate(seconds):
                            u = N2 * n + i
                            m = height(parts_[0][1])
                            wide = parts_[-1][2] + parts_[-1][4]
                            act.wait_ge(s_p2, u + 1)
                            if u >= NP:
                                act.wait_ge(s_pv, u - NP + 1)
                            act.activation(pt[0:m, u % NP, 0:wide], ps2[0:m, u % 2, 0:wide], ACT.Exp).then_inc(s_e, 1)
            k.rewind()

        batch(0, False, True)
        with nc.Fori(1, BATCH - 1) as b:
            batch(b, True, True)
        batch(BATCH - 1, True, False)
        with nc.Block() as block:
            @block.sync
            def _(sp):
                store(sp, BATCH - 1, NH - 1)
                sp.wait_ge(s_out[1], NE * 16)
        k.rewind()



G = NH * NE


def ffn_finish(nc, w, h_in, att, sxn, h_out):
    with ExitStack() as ctx:
        k = Space(nc, ctx, "h")
        eye = k.sb("eye", [128, 128])
        gw = k.sb("gw", [128, 2, 2 * NE])
        gbias = k.sb("gbias", [128, G])
        fc1 = k.sb("fc1", [C + 1, C])
        fc2 = k.sb("fc2", [C + 1, C])
        fgate = k.sb("fgate", [C, NH])
        lng = k.sb("lng", [128, D])
        lnb = k.sb("lnb", [128, D])
        fng = k.sb("fng", [128, D])
        fnb = k.sb("fnb", [128, D])
        resid = k.sb("resid", [128, NT, C])
        x = k.sb("x", [128, NT, C])
        sx = k.sb("sx", [128, NT, C])
        ot = k.sb("ot", [NE * VS, NH, SEQ])
        rz = k.sb("rz", [128, 2, G])
        a = k.sb("a", [128, NT, G * D])
        at = k.sb("at", [128, 2, 2, 128])
        lg = k.sb("lg", [128, NT * NH, NE])
        gm = k.sb("gm", [128, NT * NH])
        y = k.sb("y", [128, 2, NT, C])
        sq = k.sb("sq", [128, NT, C])
        fx = k.sb("fx", [128, NT, C])
        nz = k.sb("nz", [128, NT, C])
        fnz = k.sb("fnz", [128, NT, C])
        fgm = k.sb("fgm", [128, NT])
        hx = k.sb("hx", [128, NT, C])
        mu = k.sb("mu", [128, NT * NH])
        var = k.sb("var", [128, NT * NH])
        std = k.sb("std", [128, NT * NH])
        ft = k.sb("ft", [C + 1, SEQ])
        fg = k.sb("fg", [128, NT, NH])
        ps_t = k.ps("ps_t", [128, 2, 512])
        ps_a = k.ps("ps_a", [128, 2, 512])
        ps_g = k.ps("ps_g", [128, 512])
        ps_x = k.ps("ps_x", [128, 3, 512])
        s_w = k.sem("weights_in")
        s_x = k.sem("rows_in")
        s_ot = k.sem("attention_in")
        s_chain = k.sem("dve_step")
        s_pchain = k.sem("pool_step")
        s_t = k.sem("attention_transposed")
        s_a = k.sem("attention_divided")
        s_am = k.sem("attention_masked")
        s_at = k.sem("attention_turned")
        s_atk = k.sem("attention_turned_kept")
        s_g = k.sem("gate_logits")
        s_gx = k.sem("gate_shifted")
        s_ge = k.sem("gate_exponents")
        s_fgx = k.sem("head_gate_shifted")
        s_fge = k.sem("head_gate_exponents")
        s_var = k.sem("variance")
        s_std = k.sem("deviation")
        s_f = k.sem("layer_inputs")
        s_ft = k.sem("layer_inputs_turned")
        s_ftk = k.sem("layer_inputs_turned_kept")
        s_l = k.sem("layer_outputs")
        s_y = k.sem("results")
        s_out = k.sem("rows_out")

        with nc.Block() as block:
            @block.sync
            def _(sp):
                for dst, name in ((eye, "eye"), (gw, "h_gw"), (fc1, "h_fc1"), (fc2, "h_fc2"), (fgate, "h_fgate")):
                    sp.dma_start(dst[:], w[name]).then_inc(s_w, 16)
                for dst, name in ((gbias, "h_gbias"), (lng, "h_lng"), (lnb, "h_lnb"), (fng, "h_fng"), (fnb, "h_fnb")):
                    sp.dma_start(dst[:], w[name].partition_broadcast(128)).then_inc(s_w, 16)
                sp.wait_ge(s_pchain, 1)
                for n in range(NH):
                    cols = slice(D * n, D * n + D)
                    sp.dma_start(resid[:, 0:8, cols], sxn[SEQ * n:SEQ * n + NIMG, cols].rearrange("(t p) c -> p t c", p=128)).then_inc(s_w, 16)
                    sp.dma_start(resid[0:TAIL, 8, cols], sxn[SEQ * n + NIMG:SEQ * n + SEQ, cols]).then_inc(s_w, 16)
                sp.wait_ge(s_w, 18 * 16)

            @block.gpsimd
            def _(pool):
                chain = Chain(pool, s_pchain)
                chain(pool.memset(resid[:, 8], 0.0))
                chain(pool.memset(x[:], 0.0))
                chain(pool.memset(a[:], 0.0))
                chain(pool.memset(sx[:], 1.0))
                chain(pool.memset(lg[:], 0.0))
                chain(pool.memset(hx[:], 0.0))
                chain(pool.memset(fg[:], 0.0))
                chain(pool.memset(ft[C:C + 1], 1.0))
        k.rewind()

        def store(sp, b, half):
            sp.dma_start(h_out[bass.ds(b * SEQ, NIMG), :].rearrange("(t p) c -> p t c", p=128), y[:, half, 0:8]).then_inc(s_out, 16)
            sp.dma_start(h_out[bass.ds(b * SEQ + NIMG, TAIL), :], y[0:TAIL, half, 8]).then_inc(s_out, 16)

        def parts(b1, to, b2, of, b3=None):
            one, two = b1 is not None, b2 is not None
            with nc.Block() as block:
                @block.sync
                def _(sp):
                    if b3 is not None:
                        store(sp, b3, to)
                    if one:
                        for n in range(NH):
                            row = b1 * (G * VS) + n * (NE * VS)
                            sp.dma_start(ot[:, n], att[bass.ds(row, NE * VS), :]).then_inc(s_ot, 16)
                        sp.dma_start(sx[:, 0:8], sxn[bass.ds(b1 * SEQ, NIMG), :].rearrange("(t p) c -> p t c", p=128)).then_inc(s_ot, 16)
                        sp.dma_start(sx[0:TAIL, 8], sxn[bass.ds(b1 * SEQ + NIMG, TAIL), :]).then_inc(s_ot, 16)
                    if two:
                        sp.dma_start(x[:, 0:8], h_in[bass.ds(b2 * SEQ, NIMG), :].rearrange("(t p) c -> p t c", p=128)).then_inc(s_x, 16)
                        sp.dma_start(x[0:TAIL, 8], h_in[bass.ds(b2 * SEQ + NIMG, TAIL), :]).then_inc(s_x, 16)
                    if b3 is not None:
                        sp.wait_ge(s_out, 32)

                @block.tensor
                def _(pe):
                    def turn_back(t):
                        m = height(t)
                        if t >= 2:
                            pe.wait_ge(s_a, t - 1)
                        for n in range(NH):
                            last = pe.transpose(ps_t[0:m, t % 2, NE * VS * n:NE * VS * (n + 1)], ot[:, n, 128 * t:128 * t + m],
                                                eye[0:NE * VS, 0:NE * VS])
                        last.then_inc(s_t, 1)

                    def turn(t):
                        m = height(t)
                        pe.wait_ge(s_am, t + 1)
                        if t >= 2:
                            pe.wait_ge(s_atk, t - 1)
                        for i in range(2):
                            last = pe.transpose(ps_a[:, t % 2, 128 * i:128 * i + m], a[0:m, t, 128 * i:128 * i + 128], eye[0:m, 0:m])
                        last.then_inc(s_at, 1)

                    def gate(t):
                        m = height(t)
                        pe.wait_ge(s_atk, t + 1)
                        for i in range(2):
                            last = pe.matmul(ps_g[0:m, G * t + 8 * i:G * t + 8 * i + 8], at[:, t % 2, i, 0:m], gw[:, i], start=True, stop=True)
                        last.then_inc(s_g, 1)

                    def turn_layer(layer):
                        src = (fx, hx, hx)[layer]
                        pe.wait_ge(s_f, layer + 1)
                        for t in range(NT):
                            m = height(t)
                            last = pe.transpose(ps_x[0:C, t // 4, 128 * (t % 4):128 * (t % 4) + m], src[0:m, t, :], eye[0:m, 0:m])
                        last.then_inc(s_ft, 1)

                    def layer_products(layer):
                        pe.wait_ge(s_ftk, layer + 1)
                        for t in range(NT):
                            m = height(t)
                            if layer < 2:
                                wl = (fc1, fc2)[layer]
                                last = pe.matmul(ps_x[0:m, t // 5, C * (t % 5):C * (t % 5) + C], ft[:, 128 * t:128 * t + m], wl[:], start=True, stop=True)
                            else:
                                last = pe.matmul(ps_x[0:m, 0, NH * t:NH * t + NH], ft[0:C, 128 * t:128 * t + m], fgate[:], start=True, stop=True)
                        last.then_inc(s_l, 1)

                    if one:
                        pe.wait_ge(s_ot, 96)
                        turn_back(0)
                        turn_back(1)
                    if two:
                        turn_layer(0)
                    for t in range(NT):
                        if one:
                            turn(t)
                            if t + 2 < NT:
                                turn_back(t + 2)
                            if t >= 1:
                                gate(t - 1)
                        if two and t == 2:
                            layer_products(0)
                        if two and t == 4:
                            turn_layer(1)
                    if one:
                        gate(NT - 1)
                    if two:
                        layer_products(1)
                        turn_layer(2)
                        layer_products(2)

                @block.scalar
                def _(act):
                    if two:
                        act.wait_ge(s_var, 1)
                        act.activation(std[:], var[:], ACT.Sqrt).then_inc(s_std, 1)
                    if one:
                        for t in range(NT):
                            m = height(t)
                            act.wait_ge(s_at, t + 1)
                            if t >= 2:
                                act.wait_ge(s_g, t - 1)
                            act.activation(at[:, t % 2, :, 0:m], ps_a[:, t % 2, 0:256].rearrange("p (i s) -> p i s", i=2)[:, :, 0:m], ACT.Copy).then_inc(s_atk, 1)
                        act.wait_ge(s_gx, 1)
                        act.activation(lg[:], lg[:], ACT.Exp).then_inc(s_ge, 1)
                    if two:
                        act.wait_ge(s_var, 2)
                        act.activation(std[:], var[:], ACT.Sqrt).then_inc(s_std, 1)
                        act.wait_ge(s_fgx, 1)
                        act.activation(fg[:], fg[:], ACT.Exp).then_inc(s_fge, 1)

                @block.gpsimd
                def _(pool):
                    for t in range(NT if one else 0):
                        m = height(t)
                        pool.wait_ge(s_a, t + 1)
                        av = a[0:m, t].rearrange("p (n e d) -> p n e d", n=NH, e=NE)
                        mask = nz[0:m, t].rearrange("p (n d) -> p n d", n=NH).unsqueeze(2).to_broadcast([m, NH, NE, D])
                        pool.tensor_tensor(av, av, mask, ALU.mult).then_inc(s_am, 1)

                @block.vector
                def _(dve):
                    chain = Chain(dve, s_chain)
                    heads = lambda u: u.rearrange("p t (n d) -> p (t n) d", n=NH)
                    rows = lambda u: u[:].unsqueeze(1).to_broadcast([128, NT * NH, D])

                    def divide(tiles):
                        for t in tiles:
                            m = height(t)
                            dve.wait_ge(s_t, t + 1)
                            p = ps_t[0:m, t % 2, 0:G * VS].rearrange("p (g v) -> p g v", g=G)
                            chain(dve.reciprocal(rz[0:m, t % 2], p[:, :, D]))
                            dve.tensor_tensor(a[0:m, t].rearrange("p (g d) -> p g d", g=G), p[:, :, 0:D],
                                              spread(rz[0:m, t % 2], [m, G, D]), ALU.mult).then_inc(s_a, 1)

                    def expert_gates():
                        dve.wait_ge(s_g, NT)
                        lgt = lg[:].rearrange("p (t n) e -> p t (n e)", t=NT)
                        gp = ps_g[:, 0:NT * G].rearrange("p (t g) -> p t g", t=NT)
                        dve.tensor_tensor(lgt[:, 0:8], gp[:, 0:8], gbias[:].unsqueeze(1).to_broadcast([128, 8, G]), ALU.add)
                        chain(dve.tensor_tensor(lgt[0:TAIL, 8], gp[0:TAIL, 8], gbias[0:TAIL], ALU.add))
                        softmax_shift(chain, dve, lg[:], gm[:], s_gx)

                    def mix_experts():
                        softmax_divide(chain, dve, lg[:], gm[:], s_ge)
                        dve.wait_ge(s_am, NT)
                        a4 = a[:].rearrange("p t (n e d) -> p (t n) e d", n=NH, e=NE)
                        chain(dve.tensor_tensor(a4, a4, lg[:].unsqueeze(3).to_broadcast([128, NT * NH, NE, D]), ALU.mult))
                        if b3 is not None:
                            dve.wait_ge(s_out, 32)
                        chain(dve.reduce_sum(heads(y[:, to]), a4.rearrange("p m e d -> p m d e"), axis=AX))
                        chain(dve.tensor_tensor(y[:, to], y[:, to], resid[:], ALU.add))

                    def layer_input():
                        layer_norm(dve, chain, heads(y[:, of]), heads(fx[:]), heads(sq[:]), mu[:], var[:], std[:], s_var, s_std, FFN_EPS, n_var=1, depth=D)
                        chain(dve.tensor_tensor(heads(fx[:]), heads(fx[:]), rows(lng), ALU.mult))
                        dve.tensor_tensor(heads(fx[:]), heads(fx[:]), rows(lnb), ALU.add).then_inc(s_f, 1)
                        dve.wait_ge(s_f, 1)
                        chain(dve.tensor_scalar(fnz[:], fx[:], 0.0, None, ALU.not_equal))

                    def keep_turned(i):
                        dve.wait_ge(s_ft, i)
                        dve.tensor_copy(ft[0:C, 0:NIMG], ps_x[0:C, 0:2, :].rearrange("p a n -> p (a n)"))
                        dve.tensor_copy(ft[0:C, NIMG:SEQ], ps_x[0:C, 2, 0:TAIL]).then_inc(s_ftk, 1)

                    blocks = ((0, 5, 128, 0, 0), (5, 8, 128, 1, 0), (8, 9, TAIL, 1, 3))

                    def first_layer():
                        dve.wait_ge(s_l, 1)
                        for t0, t1, m, bank, at0 in blocks:
                            p = ps_x[0:m, bank, C * at0:C * (at0 + t1 - t0)].rearrange("p (t c) -> p t c", c=C)
                            last = dve.scalar_tensor_tensor(hx[0:m, t0:t1], p, 0.0, fnz[0:m, t0:t1], ALU.max, ALU.mult)
                        last.then_inc(s_f, 1)

                    def second_layer():
                        dve.wait_ge(s_l, 2)
                        for t0, t1, m, bank, at0 in blocks:
                            p = ps_x[0:m, bank, C * at0:C * (at0 + t1 - t0)].rearrange("p (t c) -> p t c", c=C)
                            last = dve.tensor_tensor(hx[0:m, t0:t1], p, fnz[0:m, t0:t1], ALU.mult)
                        chain(last)
                        yv = y[:, of]
                        chain(dve.tensor_tensor(yv, hx[:], fx[:], ALU.add))
                        layer_norm(dve, chain, heads(yv), heads(hx[:]), heads(sq[:]), mu[:], var[:], std[:], s_var, s_std, FFN_EPS, n_var=2, depth=D)
                        chain(dve.tensor_tensor(heads(hx[:]), heads(hx[:]), rows(fng), ALU.mult))
                        dve.tensor_tensor(heads(hx[:]), heads(hx[:]), rows(fnb), ALU.add).then_inc(s_f, 1)

                    def head_gates():
                        dve.wait_ge(s_l, 3)
                        gp = ps_x[:, 0, 0:NT * NH].rearrange("p (t g) -> p t g", t=NT)
                        dve.tensor_copy(fg[:, 0:8], gp[:, 0:8])
                        chain(dve.tensor_copy(fg[0:TAIL, 8], gp[0:TAIL, 8]))
                        softmax_shift(chain, dve, fg[:], fgm[:], s_fgx)
                        softmax_divide(chain, dve, fg[:], fgm[:], s_fge)
                        dve.wait_ge(s_f, 3)
                        yv = y[:, of]
                        chain(dve.tensor_tensor(heads(yv), heads(hx[:]), spread(fg[:].rearrange("p t n -> p (t n)"), [128, NT * NH, D]), ALU.mult))
                        dve.wait_ge(s_x, 32)
                        dve.tensor_tensor(yv, yv, x[:], ALU.add).then_inc(s_y, 1)

                    if two:
                        layer_input()
                    if one:
                        dve.wait_ge(s_ot, 96)
                        chain(dve.tensor_scalar(nz[:], sx[:], 0.0, None, ALU.not_equal))
                        divide((0, 1, 2))
                    if two:
                        keep_turned(1)
                    if one:
                        divide((3, 4, 5))
                    if two:
                        first_layer()
                    if one:
                        divide((6, 7, 8))
                    if two:
                        keep_turned(2)
                    if one:
                        expert_gates()
                    if two:
                        second_layer()
                    if one:
                        mix_experts()
                    if two:
                        keep_turned(3)
                        head_gates()
            k.rewind()

        parts(0, 0, None, None)
        parts(1, 1, 0, 0)
        with nc.Fori(0, BATCH // 2 - 1) as i:
            parts(2 * i + 2, 0, 2 * i + 1, 1, 2 * i)
            parts(2 * i + 3, 1, 2 * i + 2, 0, 2 * i + 1)
        parts(None, 0, BATCH - 1, 1, BATCH - 2)
        parts(None, 1, None, None, BATCH - 1)


def softmax_shift(chain, dve, x, m, s_shifted):
    chain(dve.reduce_max(m, x, axis=AX))
    dve.tensor_tensor(x, x, spread(m, list(x.shape)), ALU.subtract).then_inc(s_shifted, 1)


def softmax_divide(chain, dve, x, m, s_exp):
    dve.wait_ge(s_exp, 1)
    chain(dve.reduce_sum(m, x, axis=AX))
    chain(dve.reciprocal(m, m))
    chain(dve.tensor_tensor(x, x, spread(m, list(x.shape)), ALU.mult))



THIRD = ROWS // 3
PART = SEQ // 3
WID = (128, 128, 96)


def l1_attention(nc, w, h_in, h_out):
    with ExitStack() as ctx:
        k = Space(nc, ctx, "e")
        w_qkf = k.sb("w_qkf", [2 * C, 3 * HEADS * C])
        w_mid = k.sb("w_mid", [2 * C, 3 * HEADS * C], BF16)
        w_qk = k.sb("w_qk", [2 * C, 2, 3 * HEADS * C], BF16)
        b_qk = k.sb("b_qk", [128, 3, 4])
        w_vt = k.sb("w_vt", [C, 3, HEADS, 2 * C])
        b_vt = k.sb("b_vt", [C, 3, HEADS, 2 * 32 + 1])
        w_0 = k.sb("w_0", [C, HEADS, C])
        w_v0 = k.sb("w_v0", [2 * C, 2, 3 * HEADS * C], BF16)
        b_v0 = k.sb("b_v0", [2 * 32 + 1, 3 * HEADS * C], BF16)
        ones = k.sb("ones", [2 * 32 + 1, 128], BF16)
        bias0 = k.sb("bias0", [128, C])
        eye = k.sb("eye", [128, 128])
        half = k.sb("half", [128, 2])
        x = k.sb("x", [128, NT, C])
        xc = k.sb("xc", [128, NT, C])
        xn = k.sb("xn", [128, NT, 2, C])
        sq = k.sb("sq", [128, NT, C])
        mu = k.sb("mu", [128, NT])
        var = k.sb("var", [128, NT])
        std = k.sb("std", [128, NT])
        xt = k.sb("xt", [2 * C, 2, 3, 3, PART], BF16)
        rest = k.sb("rest", [2 * C, PART])
        qt = k.sb("qt", [128, 2, 3, PART])
        kz = k.sb("kz", [128, 2, 2, 3, PART])
        prod = k.sb("prod", [128, 2, 3 * PART])
        NB = 4
        sc = k.sb("sc", [128, NB, 3, PART])
        ex = k.sb("ex", [128, 2, 3, PART], BF16)
        nmax = k.sb("nmax", [128, NT, HEADS])
        z = k.sb("z", [128, NT, HEADS])
        dz = k.sb("dz", [128, NT, HEADS])
        attn = k.sb("attn", [128, NT, HEADS])
        ya = k.sb("ya", [128, 2, HEADS, C])
        res = k.sb("res", [128, 3, 3, C])
        out = k.sb("out", [128, 3, 3, C])
        ps_s = k.ps("ps_s", [128, 2, 3, 512])
        ps_p = k.ps("ps_p", [128, 2, 512])
        s_w = k.sem("weights_in")
        s_chain = k.sem("dve_step")
        s_pchain = k.sem("pool_step")
        s_mv = k.sem("value_weights_made")
        s_mvc = k.sem("value_weights_kept")
        s_x = k.sem("rows_in")
        s_res = k.sem("residual_in")
        s_var = k.sem("variance")
        s_std = k.sem("deviation")
        s_xn = k.sem("normed")
        s_mu = k.sem("means")
        s_sq = k.sem("squares")
        s_inv = k.sem("inverse_deviations")
        s_tr = k.sem("transposed")
        s_xt = k.sem("transposes_kept")
        s_pq = k.sem("queries_projected")
        s_pk = k.sem("keys_projected")
        s_qt = k.sem("queries_kept")
        s_kt = k.sem("keys_kept")
        s_s = k.sem("scores")
        s_sc = k.sem("scores_kept")
        s_ex = k.sem("exponents_summed")
        s_prod = k.sem("query_key_products")
        s_dg = k.sem("diagonals")
        s_dsub = k.sem("diagonal_shifted")
        s_dexp = k.sem("diagonal_exponents")
        s_y = k.sem("values_projected")
        s_ya = k.sem("values_weighted")
        s_sum = k.sem("heads_summed")
        s_out = k.sem("rows_out")

        with nc.Block() as block:
            @block.sync
            def _(sp):
                for dst, name in ((w_qkf, "e_wqk"), (b_qk, "e_bqk"), (w_vt, "e_wvt"), (b_vt, "e_bvt"), (w_0, "e_w0"), (eye, "eye")):
                    sp.dma_start(dst[:], w[name]).then_inc(s_w, 16)
                sp.dma_start(bias0[:], w["e_b0"].partition_broadcast(128)).then_inc(s_w, 16)
                sp.wait_ge(s_w, 112)

            @block.gpsimd
            def _(pool):
                chain = Chain(pool, s_pchain)
                chain(pool.memset(half[0:64, 0:1], 1.0))
                chain(pool.memset(half[0:64, 1:2], 0.0))
                chain(pool.memset(half[64:128, 0:1], 0.0))
                chain(pool.memset(half[64:128, 1:2], 1.0))
                chain(pool.memset(kz[64:128, :, 0], 0.0))
                chain(pool.memset(kz[0:64, :, 1], 0.0))
                chain(pool.memset(x[:], 0.0))
                chain(pool.memset(ones[:], 1.0))
                chain(pool.memset(nmax[:], 0.0))
                chain(pool.memset(z[:], 1.0))
                chain(pool.memset(dz[:], 0.0))

            @block.tensor
            def _(pe):
                pe.wait_ge(s_w, 112)
                for j in range(3):
                    for h in range(HEADS):
                        last = pe.matmul(ps_s[:, 0, j, h * C:(h + 1) * C], w_vt[:, j, h, :], w_0[:, h, :], start=True, stop=True)
                        last = pe.matmul(ps_s[0:65, 1, j, h * C:(h + 1) * C], b_vt[:, j, h, :], w_0[:, h, :], start=True, stop=True)
                last.then_inc(s_mv, 1)

            @block.vector
            def _(dve):
                chain = Chain(dve, s_chain)
                dve.wait_ge(s_w, 112)
                chain(dve.memset(b_v0[:], 0.0))
                split_weights(dve, chain, w_qkf[:], w_mid[:], w_qk[:])
                dve.wait_ge(s_mv, 1)
                chain(dve.tensor_copy(w_qkf[:], ps_s[:, 0].rearrange("p j n -> p (j n)")))
                split_weights(dve, chain, w_qkf[:], w_mid[:], w_v0[:])
                b = w_qkf[0:65]
                chain(dve.tensor_copy(b, ps_s[0:65, 1].rearrange("p j n -> p (j n)")))
                for part in range(3):
                    row = slice(32 * part, 32 * part + 1)
                    chain(dve.tensor_copy(w_mid[0:65], b))
                    chain(dve.tensor_copy(b_v0[row], w_mid[row]))
                    if part < 2:
                        chain(dve.tensor_tensor(b, b, w_mid[0:65], ALU.subtract))
        k.rewind()

        units = [(p, hh, t) for p in range(4) for hh in range(2) for t in range(NT)]
        PER = 2 * NT
        PROJECT_AT = (5, 8, 11)
        KEEP_AT = PROJECT_AT
        TAIL_AT = 14
        NORM_AT = 2 * PER + 2
        TURN_AT = tuple(2 * PER + 14 + g for g in range(3))

        def load(sp, b):
            for g in range(3):
                first = h_in[bass.ds(b * PART + g * THIRD, 256), :]
                sp.dma_start(x[:, 3 * g:3 * g + 2, :], first.rearrange("(t p) c -> p t c", p=128)).then_inc(s_x, 16)
                sp.dma_start(x[0:96, 3 * g + 2, :], h_in[bass.ds(b * PART + g * THIRD + 256, 96), :]).then_inc(s_x, 16)

        def load_residual(sp, b):
            sp.dma_start(res[:, 0:2], h_in[bass.ds(b * SEQ, 768), :].rearrange("(t p j) c -> p t j c", p=128, j=3)).then_inc(s_res, 16)
            sp.dma_start(res[0:96, 2], h_in[bass.ds(b * SEQ + 768, 288), :].rearrange("(p j) c -> p j c", j=3)).then_inc(s_res, 16)

        def store(sp, b):
            sp.wait_ge(s_sum, NT)
            sp.dma_start(h_out[bass.ds(b * SEQ, 768), :].rearrange("(t p j) c -> p t j c", p=128, j=3), out[:, 0:2]).then_inc(s_out, 16)
            sp.dma_start(h_out[bass.ds(b * SEQ + 768, 288), :].rearrange("(p j) c -> p j c", j=3), out[0:96, 2]).then_inc(s_out, 16)
            sp.wait_ge(s_out, 32)


        def minus_mean(dve, chain):
            dve.wait_ge(s_x, 96)
            chain(dve.reduce_sum(mu[:], x[:], axis=AX))
            dve.tensor_scalar(mu[:], mu[:], -1.0 / C, None, ALU.mult).then_inc(s_mu, 1)

        def center(pool, chain):
            pool.wait_ge(s_mu, 1)
            chain(pool.tensor_tensor(xc[:], x[:], spread(mu[:], [128, NT, C]), ALU.add))
            pool.tensor_tensor(sq[:], xc[:], xc[:], ALU.mult).then_inc(s_sq, 1)

        def variance(dve, chain):
            dve.wait_ge(s_sq, 1)
            chain(dve.reduce_sum(var[:], sq[:], axis=AX))
            dve.tensor_scalar(var[:], var[:], 1.0 / C, LN_EPS, ALU.mult, ALU.add).then_inc(s_var, 1)

        def invert(dve):
            dve.wait_ge(s_std, 1)
            dve.reciprocal(std[:], std[:]).then_inc(s_inv, 1)

        def normalise(pool):
            pool.wait_ge(s_inv, 1)
            pair = [128, NT, 2, C]
            pool.tensor_tensor(xn[:], xc[:].unsqueeze(2).to_broadcast(pair), std[:].unsqueeze(2).unsqueeze(3).to_broadcast(pair), ALU.mult).then_inc(s_xn, 1)

        def root(act):
            act.wait_ge(s_var, 1)
            act.activation(std[:], var[:], ACT.Sqrt).then_inc(s_std, 1)

        def turn(pe, g):
            if g == 0:
                pe.wait_ge(s_xn, 1)
            else:
                pe.wait_ge(s_xt, g)
            for t, n in enumerate(WID):
                last = pe.transpose(ps_p[:, 1, 128 * t:128 * t + n], xn[0:n, 3 * g + t].rearrange("p a c -> p (a c)"), eye[0:n, 0:n])
            last.then_inc(s_tr, 1)

        def keep_turned(dve, chain, to, g):
            dve.wait_ge(s_tr, g + 1)
            split_moving(dve, chain, ps_p[:, 1, 0:PART], xt[:, to, g], rest[:], s_xt)


        def project(pe, of, p, r, j):
            if 3 * r + j >= 1:
                pe.wait_ge(s_qt, 3 * r + j)
            at = HEADS * C * j + 128 * p
            for a, (mine, theirs) in enumerate(PASSES):
                last = pe.matmul(ps_p[:, 0, 0:PART], w_qk[:, theirs, at:at + 128], xt[:, of, 0, mine], start=a == 0, stop=a == 2)
            last.then_inc(s_pq, 1)
            if 3 * r + j >= 1:
                pe.wait_ge(s_kt, 3 * r + j)
            for a, (mine, theirs) in enumerate(PASSES):
                last = pe.matmul(ps_p[:, 1, 0:PART], w_qk[:, theirs, at:at + 128], xt[:, of, 1, mine], start=a == 0, stop=a == 2)
            last.then_inc(s_pk, 1)

        def keep_queries(act, p, r, j):
            act.wait_ge(s_pq, 3 * r + j + 1)
            act.activation(qt[:, p % 2, j, :], ps_p[:, 0, 0:PART], ACT.Identity, bias=b_qk[:, j, p % 4:p % 4 + 1]).then_inc(s_qt, 1)

        def keep_keys(act, p, r, j):
            act.wait_ge(s_pk, 3 * r + j + 1)
            bias = b_qk[:, j, p % 4:p % 4 + 1]
            act.activation(kz[0:64, p % 2, 0, j, :], ps_p[0:64, 1, 0:PART], ACT.Identity, bias=bias[0:64])
            act.activation(kz[64:128, p % 2, 1, j, :], ps_p[64:128, 1, 0:PART], ACT.Identity, bias=bias[64:128]).then_inc(s_kt, 1)


        def values(pe, of, t):
            n = WID[t % 3]
            if t >= 1:
                pe.wait_ge(s_ya, t)
            cols = slice(HEADS * C * (t // 3), HEADS * C * (t // 3 + 1))
            for a, (mine, theirs) in enumerate(PASSES):
                pe.matmul(ps_p[0:n, 1, :], xt[:, of, 2, mine, 128 * (t % 3):128 * (t % 3) + n], w_v0[:, theirs, cols], start=a == 0, stop=False)
            pe.matmul(ps_p[0:n, 1, :], ones[:, 0:n], b_v0[:, cols], start=False, stop=True).then_inc(s_y, 1)

        def weigh(dve, t):
            n = WID[t % 3]
            dve.wait_ge(s_y, t + 1)
            if t >= 2:
                dve.wait_ge(s_sum, t - 1)
            dve.tensor_tensor(ya[0:n, t % 2], ps_p[0:n, 1, :].rearrange("p (h c) -> p h c", h=HEADS),
                              spread(attn[0:n, t], [n, HEADS, C]), ALU.mult).then_inc(s_ya, 1)

        def add_bias(pool, chain):
            pool.wait_ge(s_res, 32)
            chain(pool.tensor_tensor(res[:, 0:2], res[:, 0:2], spread_b(bias0[:], 2), ALU.add))
            chain(pool.tensor_tensor(res[0:96, 2], res[0:96, 2], bias0[0:96].unsqueeze(1).to_broadcast([96, 3, C]), ALU.add))

        def sum_heads(pool, chain, t):
            j, ti, n = t // 3, t % 3, WID[t % 3]
            pool.wait_ge(s_ya, t + 1)
            y = ya[0:n, t % 2]
            for m in (4, 2, 1):
                chain(pool.tensor_tensor(y[:, 0:m], y[:, 0:m], y[:, m:2 * m], ALU.add))
            pool.tensor_tensor(out[0:n, ti, j], y[:, 0], res[0:n, ti, j], ALU.add).then_inc(s_sum, 1)

        with nc.Block() as block:
            @block.sync
            def _(sp):
                load(sp, 0)

            @block.tensor
            def _(pe):
                for g in range(3):
                    turn(pe, g)
                pe.wait_ge(s_xt, 3)
                for j in range(3):
                    project(pe, 0, 0, 0, j)

            @block.gpsimd
            def _(pool):
                center(pool, Chain(pool, s_pchain))
                normalise(pool)

            @block.scalar
            def _(act):
                root(act)
                for j in range(3):
                    keep_queries(act, 0, 0, j)
                    keep_keys(act, 0, 0, j)

            @block.vector
            def _(dve):
                chain = Chain(dve, s_chain)
                minus_mean(dve, chain)
                variance(dve, chain)
                invert(dve)
                for g in range(3):
                    keep_turned(dve, chain, 0, g)
        k.rewind()

        def attend(b, of, before, more):
            to = 1 - of

            def projected(p):
                return (of, p + 1) if p < 3 else (to, 0) if more else None

            with nc.Block() as block:
                @block.sync
                def _(sp):
                    if before:
                        load_residual(sp, b - 1)
                    if more:
                        load(sp, b + 1)
                    if before:
                        store(sp, b - 1)

                @block.scalar
                def _(act):
                    for u, (p, hh, t) in enumerate(units):
                        n = WID[t % 3]
                        h = 2 * p + hh
                        if u % PER in KEEP_AT and projected(p):
                            if u % PER == KEEP_AT[0] and p >= 1:
                                act.wait_ge(s_s, PER * p)
                                act.wait_ge(s_prod, p)
                            keep_queries(act, p + 1, p, KEEP_AT.index(u % PER))
                            keep_keys(act, p + 1, p, KEEP_AT.index(u % PER))
                        if more and u == NORM_AT + 6:
                            root(act)
                        act.wait_ge(s_sc, u + 1)
                        if u >= 2:
                            act.wait_ge(s_ex, u - 1)
                        act.activation(ex[0:n, u % 2], sc[0:n, u % NB], ACT.Exp, bias=nmax[0:n, t, h:h + 1],
                                       scale=-1.0, accum_out=z[0:n, t, h:h + 1]).then_inc(s_ex, 1)
                    act.wait_ge(s_dsub, 1)
                    act.activation(attn[:], dz[:], ACT.Exp).then_inc(s_dexp, 1)

                @block.vector
                def _(dve):
                    chain = Chain(dve, s_chain)
                    for u, (p, hh, t) in enumerate(units):
                        n = WID[t % 3]
                        h = 2 * p + hh
                        if before and TAIL_AT <= u < TAIL_AT + NT:
                            weigh(dve, u - TAIL_AT)
                        if more and u == NORM_AT:
                            minus_mean(dve, chain)
                        if more and u == NORM_AT + 4:
                            variance(dve, chain)
                        if more and u == NORM_AT + 7:
                            invert(dve)
                        if more and u in TURN_AT:
                            keep_turned(dve, chain, to, TURN_AT.index(u))
                        dve.wait_ge(s_s, u + 1)
                        if u >= NB:
                            dve.wait_ge(s_ex, u - NB + 1)
                        dve.tensor_scalar(sc[0:n, u % NB], ps_s[0:n, u % 2, :, 0:PART], -0.125, None, ALU.mult,
                                          ALU.min, accum_out=nmax[0:n, t, h:h + 1]).then_inc(s_sc, 1)
                    dve.wait_ge(s_dg, 4)
                    dg = ps_p[:, 0, 352:352 + NT * HEADS].rearrange("p (j t h) -> p j t h", j=3, t=3)
                    dz4 = dz[:].rearrange("p (j t) h -> p j t h", j=3)
                    nm4 = nmax[:].rearrange("p (j t) h -> p j t h", j=3)
                    dve.wait_ge(s_sc, len(units))
                    for t, n in enumerate(WID):
                        last = dve.scalar_tensor_tensor(dz4[0:n, :, t], dg[0:n, :, t], 0.125, nm4[0:n, :, t], ALU.mult, ALU.add)
                    last.then_inc(s_dsub, 1)
                    dve.wait_ge(s_ex, len(units))
                    chain(dve.reciprocal(z[:], z[:]))
                    dve.wait_ge(s_dexp, 1)
                    chain(dve.tensor_tensor(attn[:], attn[:], z[:], ALU.mult))

                @block.gpsimd
                def _(pool):
                    chain = Chain(pool, s_pchain)

                    def products(p):
                        if p:
                            pool.wait_ge(s_qt, 3 * p)
                            pool.wait_ge(s_kt, 3 * p)
                        if p >= 2:
                            pool.wait_ge(s_dg, p - 1)
                        q2 = qt[:].rearrange("p a j n -> p a (j n)")
                        k2 = kz[:].rearrange("p a z j n -> p a z (j n)")
                        chain(pool.tensor_tensor(prod[0:64, p % 2], q2[0:64, p % 2], k2[0:64, p % 2, 0], ALU.mult))
                        pool.tensor_tensor(prod[64:128, p % 2], q2[64:128, p % 2], k2[64:128, p % 2, 1], ALU.mult).then_inc(s_prod, 1)
                        pool.wait_ge(s_prod, p + 1)

                    products(0)
                    if before:
                        add_bias(pool, chain)
                        for t in range(NT):
                            if t == 4:
                                products(1)
                            sum_heads(pool, chain, t)
                    else:
                        products(1)
                    products(2)
                    if more:
                        center(pool, chain)
                        normalise(pool)
                    products(3)

                @block.tensor
                def _(pe):
                    def diagonal(p):
                        pe.wait_ge(s_prod, p + 1)
                        if projected(p):
                            pe.wait_ge(s_qt, 3 * (p + 1))
                        for t in range(NT):
                            n = WID[t % 3]
                            at = PART * (t // 3) + 128 * (t % 3)
                            col = 352 + HEADS * t + 2 * p
                            last = pe.matmul(ps_p[0:n, 0, col:col + 2], prod[:, p % 2, at:at + n], half[:], start=True, stop=True)
                        last.then_inc(s_dg, 1)

                    for u, (p, hh, t) in enumerate(units):
                        n = WID[t % 3]
                        if before and u == TAIL_AT + NT:
                            pe.wait_ge(s_ya, NT)
                        if u % PER in PROJECT_AT and projected(p):
                            half_, pair = projected(p)
                            if p == 3 and u % PER == PROJECT_AT[0]:
                                pe.wait_ge(s_xt, 3)
                            project(pe, half_, pair, p, PROJECT_AT.index(u % PER))
                        if before and TAIL_AT <= u < TAIL_AT + NT:
                            if u == TAIL_AT:
                                pe.wait_ge(s_kt, 3)
                            values(pe, to, u - TAIL_AT)
                        if more and u in TURN_AT:
                            if u == TURN_AT[0]:
                                pe.wait_ge(s_kt, 9)
                            turn(pe, TURN_AT.index(u))
                        if u % PER == 16:
                            diagonal(p)
                        if u % PER == 0 and p:
                            pe.wait_ge(s_qt, 3 * p)
                            pe.wait_ge(s_kt, 3 * p)
                        if u >= 2:
                            pe.wait_ge(s_sc, u - 1)
                        for j in range(3):
                            last = pe.matmul(ps_s[0:n, u % 2, j, 0:PART],
                                             kz[:, p % 2, hh, t // 3, 128 * (t % 3):128 * (t % 3) + n],
                                             qt[:, p % 2, j, :], start=True, stop=True)
                        last.then_inc(s_s, 1)
            k.rewind()

        attend(0, 0, False, True)
        with nc.Fori(0, (BATCH - 2) // 2) as i:
            attend(2 * i + 1, 1, True, True)
            attend(2 * i + 2, 0, True, True)
        attend(BATCH - 1, 1, True, False)

        with nc.Block() as block:
            @block.sync
            def _(sp):
                load_residual(sp, BATCH - 1)
                store(sp, BATCH - 1)

            @block.tensor
            def _(pe):
                for t in range(NT):
                    values(pe, (BATCH - 1) % 2, t)

            @block.vector
            def _(dve):
                for t in range(NT):
                    weigh(dve, t)

            @block.gpsimd
            def _(pool):
                chain = Chain(pool, s_pchain)
                add_bias(pool, chain)
                for t in range(NT):
                    sum_heads(pool, chain, t)
        k.rewind()


def spread_b(bias, n):
    return bias.unsqueeze(1).unsqueeze(1).to_broadcast([128, n, 3, C])



EXPERTS = 16
FF = 128
CHUNK = 352
WIDTHS = (128, 128, 96)


def l1_experts(nc, w, h_in, h_out):
    with ExitStack() as ctx:
        k = Space(nc, ctx, "f")
        w1f = k.sb("w1f", [2 * C, EXPERTS * FF])
        w1m = k.sb("w1m", [2 * C, EXPERTS * FF], BF16)
        w1 = k.sb("w1", [2 * C, 2, EXPERTS * FF], BF16)
        b1 = k.sb("b1", [FF, EXPERTS])
        w2 = k.sb("w2", [FF, EXPERTS, C])
        wgf = k.sb("wgf", [2 * C, EXPERTS])
        wgm = k.sb("wgm", [2 * C, EXPERTS], BF16)
        wg = k.sb("wg", [2 * C, 2, EXPERTS], BF16)
        bg = k.sb("bg", [128, EXPERTS])
        b2 = k.sb("b2", [EXPERTS, C])
        gamma = k.sb("gamma", [128, C])
        beta = k.sb("beta", [128, C])
        eye = k.sb("eye", [128, 128])
        iota = k.sb("iota", [128, EXPERTS])
        x = k.sb("x", [128, NT, C])
        xc = k.sb("xc", [128, NT, C])
        xn = k.sb("xn", [128, NT, 2, C])
        sq = k.sb("sq", [128, NT, C])
        mu = k.sb("mu", [128, NT])
        var = k.sb("var", [128, NT])
        std = k.sb("std", [128, NT])
        xt = k.sb("xt", [2 * C, 2, 3, 3, CHUNK], BF16)
        rest = k.sb("rest", [2 * C, CHUNK])
        lg = k.sb("lg", [128, NT, EXPERTS])
        top = k.sb("top", [128, NT, 8])
        who = k.sb("who", [128, NT, 8], U32)
        whof = k.sb("whof", [128, NT, 2])
        e2 = k.sb("e2", [128, NT])
        den = k.sb("den", [128, NT])
        w1st = k.sb("w1st", [128, NT])
        w2nd = k.sb("w2nd", [128, NT])
        ga = k.sb("ga", [128, 2, NT, EXPERTS])
        gb = k.sb("gb", [128, NT, EXPERTS])
        gt = k.sb("gt", [EXPERTS, 3, CHUNK])
        ht = k.sb("ht", [FF, 2, EXPERTS, CHUNK])
        wo = k.sb("wo", [128, 2, EXPERTS, C])
        moe = k.sb("moe", [128, NT, C])
        res = k.sb("res", [128, 2, NT, C])
        base = k.sb("base", [128, 2, NT, C])
        y = k.sb("y", [128, 2, NT, C])
        ps_a = k.ps("ps_a", [128, 2, 512])
        ps_h = k.ps("ps_h", [128, 2, 512])
        ps_o = k.ps("ps_o", [128, 2, 2, 512])
        s_w = k.sem("weights_in")
        s_chain = k.sem("dve_step")
        s_pchain = k.sem("pool_step")
        s_x = k.sem("rows_in")
        s_var = k.sem("variance")
        s_std = k.sem("deviation")
        s_xn = k.sem("normed")
        s_tr = k.sem("transposed")
        s_xt = k.sem("transposes_kept")
        s_lg = k.sem("logits")
        s_lgk = k.sem("logits_kept")
        s_d2 = k.sem("second_less_first")
        s_e2 = k.sem("second_exponent")
        s_g = k.sem("gates")
        s_gt = k.sem("gates_transposed")
        s_gtk = k.sem("gates_transposed_kept")
        s_h = k.sem("hidden")
        s_ht = k.sem("hidden_kept")
        s_o = k.sem("expert_outputs")
        s_wo = k.sem("outputs_weighted")
        s_res = k.sem("residual_kept")
        s_b2 = k.sem("output_biases")
        s_y = k.sem("results")
        s_late = k.sem("last_results")
        s_out = k.sem("rows_out")

        with nc.Block() as block:
            @block.sync
            def _(sp):
                for dst, name in ((w1f, "f_w1"), (b1, "f_b1"), (w2, "f_w2"), (wgf, "f_wg"), (b2, "f_b2"), (eye, "eye"), (iota, "f_iota")):
                    sp.dma_start(dst[:], w[name]).then_inc(s_w, 16)
                sp.dma_start(bg[:], w["f_bg"].partition_broadcast(128)).then_inc(s_w, 16)
                sp.dma_start(gamma[:], w["f_gamma"].partition_broadcast(128)).then_inc(s_w, 16)
                sp.dma_start(beta[:], w["f_beta"].partition_broadcast(128)).then_inc(s_w, 16)
                sp.wait_ge(s_w, 160)

            @block.gpsimd
            def _(pool):
                chain = Chain(pool, s_pchain)
                chain(pool.memset(x[:], 0.0))
                chain(pool.memset(lg[:], 0.0))
                chain(pool.memset(top[:], 0.0))
                chain(pool.memset(who[:], 0))
                chain(pool.memset(moe[:], 0.0))
                chain(pool.memset(base[:], 0.0))

            @block.vector
            def _(dve):
                chain = Chain(dve, s_chain)
                dve.wait_ge(s_w, 160)
                split_weights(dve, chain, w1f[:], w1m[:], w1[:])
                split_weights(dve, chain, wgf[:], wgm[:], wg[:])
        k.rewind()


        def load(sp, b):
            for c in range(3):
                at = b * SEQ + c * CHUNK
                sp.dma_start(x[:, 3 * c:3 * c + 2], h_in[bass.ds(at, 256), :].rearrange("(t p) c -> p t c", p=128)).then_inc(s_x, 16)
                sp.dma_start(x[0:96, 3 * c + 2], h_in[bass.ds(at + 256, 96), :]).then_inc(s_x, 16)

        def keep_residual(pool, r, to):
            pool.wait_ge(s_x, 96 * (r + 1))
            pool.tensor_tensor(res[:, to], x[:], beta[:].unsqueeze(1).to_broadcast([128, NT, C]), ALU.add).then_inc(s_res, 1)

        def norm(dve, chain, r, n_var):
            dve.wait_ge(s_x, 96 * (r + 1))
            layer_norm(dve, chain, x[:], xc[:], sq[:], mu[:], var[:], std[:], s_var, s_std, LN_EPS, n_var=n_var, done=s_xn, twice=xn[:])

        def turn(pe, r):
            pe.wait_ge(s_xn, r + 1)
            for c in range(3):
                if c == 2:
                    pe.wait_ge(s_xt, 3 * r + 1)
                for t, n in enumerate(WIDTHS):
                    last = pe.transpose(ps_a[:, c % 2, 128 * t:128 * t + n], xn[0:n, 3 * c + t].rearrange("p a c -> p (a c)"), eye[0:n, 0:n])
                last.then_inc(s_tr, 1)

        def keep_turned(dve, chain, r, to):
            for c in range(3):
                dve.wait_ge(s_tr, 3 * r + c + 1)
                split_moving(dve, chain, ps_a[:, c % 2, 0:CHUNK], xt[:, to, c], rest[:], s_xt)

        def logits(pe, r, to):
            pe.wait_ge(s_xt, 3 * (r + 1))
            for t in range(NT):
                n = WIDTHS[t % 3]
                col = 352 + EXPERTS * t
                for a, (mine, theirs) in enumerate(PASSES):
                    last = pe.matmul(ps_a[0:n, 1, col:col + EXPERTS], xt[:, to, t // 3, mine, 128 * (t % 3):128 * (t % 3) + n], wg[:, theirs],
                                     start=a == 0, stop=a == 2)
            last.then_inc(s_lg, 1)

        def second_exponent(act, r):
            act.wait_ge(s_d2, r + 1)
            act.activation(e2[:], e2[:], ACT.Exp).then_inc(s_e2, 1)

        def gates(dve, chain, r, to):
            dve.wait_ge(s_lg, r + 1)
            lgp = ps_a[:, 1, 352:352 + NT * EXPERTS].rearrange("p (c t e) -> p c t e", c=3, t=3)
            lg4 = lg[:].rearrange("p (c t) e -> p c t e", c=3)
            dve.tensor_tensor(lg4[:, :, 0:2], lgp[:, :, 0:2], bg[:].unsqueeze(1).unsqueeze(1).to_broadcast([128, 3, 2, EXPERTS]), ALU.add)
            dve.tensor_tensor(lg4[0:96, :, 2], lgp[0:96, :, 2], bg[0:96].unsqueeze(1).to_broadcast([96, 3, EXPERTS]), ALU.add).then_inc(s_lgk, 1)
            dve.wait_ge(s_lgk, r + 1)
            for t in range(NT):
                last = dve.max(top[:, t], lg[:, t])
            chain(last)
            dve.tensor_tensor(e2[:], top[:, :, 1], top[:, :, 0], ALU.subtract).then_inc(s_d2, 1)
            for t in range(NT):
                last = dve.max_index(who[:, t], top[:, t], lg[:, t])
            chain(last)
            chain(dve.tensor_copy(whof[:], who[:, :, 0:2]))
            shape = [128, NT, EXPERTS]
            every = iota[:].unsqueeze(1).to_broadcast(shape)
            chain(dve.tensor_tensor(ga[:, to], every, spread(whof[:, :, 0], shape), ALU.is_equal))
            chain(dve.tensor_tensor(gb[:], every, spread(whof[:, :, 1], shape), ALU.is_equal))
            dve.wait_ge(s_e2, r + 1)
            chain(dve.tensor_scalar(den[:], e2[:], 1.0, None, ALU.add))
            chain(dve.reciprocal(w1st[:], den[:]))
            chain(dve.tensor_tensor(w2nd[:], e2[:], w1st[:], ALU.mult))
            chain(dve.tensor_tensor(ga[:, to], ga[:, to], spread(w1st[:], shape), ALU.mult))
            chain(dve.tensor_tensor(gb[:], gb[:], spread(w2nd[:], shape), ALU.mult))
            dve.tensor_tensor(ga[:, to], ga[:, to], gb[:], ALU.add).then_inc(s_g, 1)

        def turn_gates(pe, r, to):
            pe.wait_ge(s_g, r + 1)
            for c in range(3):
                if c == 2:
                    pe.wait_ge(s_gtk, 3 * r + 1)
                for t, n in enumerate(WIDTHS):
                    last = pe.transpose(ps_a[0:EXPERTS, c % 2, 128 * t:128 * t + n], ga[0:n, to, 3 * c + t, :], eye[0:n, 0:n])
                last.then_inc(s_gt, 1)

        def keep_gates(dve, r):
            for c in range(3):
                dve.wait_ge(s_gt, 3 * r + c + 1)
                dve.tensor_copy(gt[:, c], ps_a[0:EXPERTS, c % 2, 0:CHUNK]).then_inc(s_gtk, 1)

        def biases(pe, r):
            pe.wait_ge(s_gtk, 3 * (r + 1))
            for t in range(NT):
                n = WIDTHS[t % 3]
                last = pe.matmul(ps_a[0:n, t // 8, C * (t % 8):C * (t % 8) + C], gt[:, t // 3, 128 * (t % 3):128 * (t % 3) + n], b2[:],
                                 start=True, stop=True)
            last.then_inc(s_b2, 1)

        def keep_base(dve, chain, r, to):
            dve.wait_ge(s_xn, r + 1)
            dve.wait_ge(s_b2, r + 1)
            for t in range(NT):
                n = WIDTHS[t % 3]
                last = dve.tensor_tensor(base[0:n, to, t], xn[0:n, t, 0], ps_a[0:n, t // 8, C * (t % 8):C * (t % 8) + C], ALU.add)
            chain(last)

        with nc.Block() as block:
            @block.sync
            def _(sp):
                load(sp, 0)

            @block.gpsimd
            def _(pool):
                keep_residual(pool, 0, 0)

            @block.tensor
            def _(pe):
                turn(pe, 0)
                logits(pe, 0, 0)
                turn_gates(pe, 0, 0)
                biases(pe, 0)

            @block.scalar
            def _(act):
                act.wait_ge(s_var, 1)
                act.activation(std[:], var[:], ACT.Sqrt).then_inc(s_std, 1)
                second_exponent(act, 0)

            @block.vector
            def _(dve):
                chain = Chain(dve, s_chain)
                norm(dve, chain, 0, 1)
                keep_turned(dve, chain, 0, 0)
                gates(dve, chain, 0, 0)
                keep_gates(dve, 0)
                keep_base(dve, chain, 0, 0)
        k.rewind()

        def store(sp, b, j):
            for c in range(3):
                at = b * SEQ + c * CHUNK
                sp.dma_start(h_out[bass.ds(at, 256), :].rearrange("(t p) c -> p t c", p=128), y[:, j, 3 * c:3 * c + 2]).then_inc(s_out, 16)
                sp.dma_start(h_out[bass.ds(at + 256, 96), :], y[0:96, j, 3 * c + 2]).then_inc(s_out, 16)

        def finish(dve, chain, j, n_var, done):
            yj = y[:, j]
            chain(dve.tensor_tensor(moe[:], moe[:], base[:, j], ALU.add))
            layer_norm(dve, chain, moe[:], yj, sq[:], mu[:], var[:], std[:], s_var, s_std, LN_EPS, n_var=n_var)
            chain(dve.tensor_tensor(yj, yj, gamma[:].unsqueeze(1).to_broadcast([128, NT, C]), ALU.mult))
            dve.tensor_tensor(yj, yj, res[:, j], ALU.add).then_inc(done, 1)

        def two_batches(b, before, more):
            CHUNKS = 6
            inputs = 2 if more else 1
            late = 1 if before else 0

            with nc.Block() as block:
                @block.sync
                def _(sp):
                    for j in range(2):
                        if j < inputs:
                            if j:
                                sp.wait_ge(s_xn, j)
                                sp.wait_ge(s_res, j)
                            load(sp, b + 1 + j)
                    if before:
                        sp.wait_ge(s_late, 1)
                        store(sp, b - 1, 1)
                    sp.wait_ge(s_y, 1)
                    store(sp, b, 0)
                    sp.wait_ge(s_out, 96 * (late + 1))

                @block.gpsimd
                def _(pool):
                    if before:
                        pool.wait_ge(s_late, 1)
                    keep_residual(pool, 0, 1)
                    if more:
                        pool.wait_ge(s_y, 1)
                        keep_residual(pool, 1, 0)

                @block.tensor
                def _(pe):
                    def hidden(u):
                        if u == 3:
                            pe.wait_ge(s_xt, 3)
                        for e in range(EXPERTS):
                            n = u * EXPERTS + e
                            if n >= 2:
                                pe.wait_ge(s_ht, n - 1)
                            for a, (mine, theirs) in enumerate(PASSES):
                                last = pe.matmul(ps_h[:, n % 2, 0:CHUNK], w1[:, theirs, FF * e:FF * (e + 1)], xt[:, u // 3, u % 3, mine],
                                                 start=a == 0, stop=a == 2)
                            last.then_inc(s_h, 1)

                    def outputs(u):
                        pe.wait_ge(s_ht, EXPERTS * (u + 1))
                        for ti, n in enumerate(WIDTHS):
                            t = 3 * u + ti
                            if t >= 2:
                                pe.wait_ge(s_wo, t - 1)
                            for e in range(EXPERTS):
                                last = pe.matmul(ps_o[0:n, t % 2, e // 8, C * (e % 8):C * (e % 8) + C],
                                                 ht[:, u % 2, e, 128 * ti:128 * ti + n], w2[:, e], start=True, stop=True)
                            last.then_inc(s_o, 1)

                    hidden(0)
                    for u in range(CHUNKS):
                        r, c = u // 3, u % 3
                        if u + 1 < CHUNKS:
                            hidden(u + 1)
                        if c == 2 and r < inputs:
                            biases(pe, r)
                        if c == 0 and r < inputs:
                            turn(pe, r)
                        outputs(u)
                        if c == 0 and r < inputs:
                            logits(pe, r, 1 - r)
                        if c == 1 and r < inputs:
                            turn_gates(pe, r, 1 - r)

                @block.scalar
                def _(act):
                    def root(n):
                        act.wait_ge(s_var, n)
                        act.activation(std[:], var[:], ACT.Sqrt).then_inc(s_std, 1)

                    for u in range(CHUNKS):
                        for e in range(EXPERTS):
                            n = u * EXPERTS + e
                            if e == 0 and u >= 2:
                                act.wait_ge(s_o, 3 * (u - 1))
                            act.wait_ge(s_h, n + 1)
                            act.activation(ht[:, u % 2, e], ps_h[:, n % 2, 0:CHUNK], ACT.Relu, bias=b1[:, e:e + 1]).then_inc(s_ht, 1)
                            if (u, e) == (0, 8) and before:
                                root(1)
                            if (u, e) == (1, 4):
                                root(late + 1)
                            if (u, e) == (4, 4) and more:
                                root(late + 2)
                            if (u, e) == (4, 10):
                                root(late + inputs + 1)
                            if u % 3 == 2 and e == 6 and u // 3 < inputs:
                                second_exponent(act, u // 3)

                @block.vector
                def _(dve):
                    chain = Chain(dve, s_chain)

                    def tile(t):
                        n = WIDTHS[t % 3]
                        dve.wait_ge(s_o, t + 1)
                        dve.tensor_tensor(wo[0:n, t % 2], ps_o[0:n, t % 2].rearrange("p a (e c) -> p (a e) c", c=C),
                                          spread(ga[0:n, t // NT, t % NT], [n, EXPERTS, C]), ALU.mult).then_inc(s_wo, 1)
                        dve.wait_ge(s_wo, t + 1)
                        chain(dve.reduce_sum(moe[0:n, t % NT], wo[0:n, t % 2].rearrange("p e c -> p c e"), axis=AX))

                    if before:
                        finish(dve, chain, 1, 1, s_late)
                    norm(dve, chain, 0, late + 1)
                    for u in range(CHUNKS):
                        r, c = u // 3, u % 3
                        if r < inputs:
                            if c == 0:
                                keep_turned(dve, chain, r, 1 - r)
                            if c == 1:
                                gates(dve, chain, r, 1 - r)
                            if c == 2:
                                keep_gates(dve, r)
                                keep_base(dve, chain, r, 1 - r)
                        if u == 3:
                            dve.wait_ge(s_g, 1)
                        for ti in range(3):
                            tile(3 * u + ti)
                        if u == 2:
                            if more:
                                norm(dve, chain, 1, late + 2)
                            finish(dve, chain, 0, late + inputs + 1, s_y)
            k.rewind()

        two_batches(0, False, True)
        with nc.Fori(1, BATCH // 2 - 1) as i:
            two_batches(2 * i, True, True)
        two_batches(BATCH - 2, True, False)

        with nc.Block() as block:
            @block.scalar
            def _(act):
                act.wait_ge(s_var, 1)
                act.activation(std[:], var[:], ACT.Sqrt).then_inc(s_std, 1)

            @block.vector
            def _(dve):
                finish(dve, Chain(dve, s_chain), 1, 1, s_late)

            @block.sync
            def _(sp):
                sp.wait_ge(s_late, 1)
                store(sp, BATCH - 1, 1)
                sp.wait_ge(s_out, 96)
        k.rewind()


def early_fusion(nc, w, out):
    def dram(name, shape, dt=F32):
        return nc.dram_tensor(name, shape, dt).ap()

    tokens, h1, h2, h3 = (dram(name, (ROWS, C)) for name in ("tokens", "h1", "h2", "h3"))
    image_tokens(nc, w, tokens)
    text_tokens(nc, w, tokens)
    l0_attention(nc, w, tokens, h1)
    qk3 = dram("qk3", (BATCH * NH * 3 * QK, SEQ), BF16)
    vals = dram("vals", (ROWS, C))
    split = dram("split", (ROWS, C))
    maxima = dram("maxima", (3 * NH * NE, SEQ), BF16)
    attended = dram("attended", (BATCH * NH * NE * VS, SEQ))
    ffn_project(nc, w, h1, qk3, vals, split)
    ffn_attend(nc, w, qk3, vals, maxima, attended)
    ffn_finish(nc, w, h1, attended, split, h2)
    l1_attention(nc, w, h2, h3)
    l1_experts(nc, w, h3, out)


def layout(i):
    a = {}
    a["eye"] = np.eye(128, dtype=np.float32)
    wb = np.concatenate([i["L1_attn_Wqkv"], i["L1_attn_bqkv"][None]], 0).reshape(65, 3, 64, 8)
    a["e_wqk"] = np.tile(wb[:64].transpose(0, 1, 3, 2).reshape(64, -1), (2, 1))
    a["e_bqk"] = wb[64].transpose(2, 1, 0).reshape(4, 128, 3).transpose(1, 2, 0)
    vt = wb.transpose(2, 1, 3, 0)
    a["e_wvt"] = np.concatenate([vt[..., :64]] * 2, 3)
    a["e_bvt"] = np.zeros((64, 3, 8, 65), np.float32)
    a["e_bvt"][..., 0::32] = vt[..., 64:]
    a["e_w0"] = i["L1_attn_W0"].reshape(64, 8, 64)
    a["e_b0"] = i["L1_attn_b0"]
    a["f_w1"] = np.tile(i["L1_ffn_w1"].transpose(1, 0, 2).reshape(64, -1), (2, 1))
    a["f_b1"] = i["L1_ffn_b1"].T
    a["f_w2"] = i["L1_ffn_w2"].transpose(1, 0, 2)
    a["f_wg"] = np.tile(i["L1_ffn_gate_w"], (2, 1))
    a["f_bg"] = i["L1_ffn_gate_b"]
    a["f_b2"] = i["L1_ffn_b2"]
    a["f_gamma"] = i["L1_ffn_gamma"]
    a["f_beta"] = i["L1_ffn_beta"]
    a["f_iota"] = np.tile(np.arange(16, dtype=np.float32), (128, 1))
    wb = np.concatenate([i["L0_attn_W_qkv"], i["L0_attn_b_qkv"][None]], 0).reshape(65, 3, 64)
    a["c_wqk"] = wb[:, 0:2]
    a["c_wvt"] = wb[:, 2].T
    a["c_wout"] = i["L0_attn_W_out"]
    a["c_bout"] = i["L0_attn_b_out"]
    hl = np.concatenate([i["L0_ffn_hl_w"].reshape(64, 64).T, i["L0_ffn_hl_b"].reshape(1, 64)], 0)
    a["g_hl"] = hl
    a["g_hlt"] = hl.T.reshape(4, 16, 65).transpose(1, 0, 2)
    wq = i["L0_ffn_wq"].transpose(3, 0, 1, 2).reshape(16, 4, 64)
    wk = i["L0_ffn_wk"].transpose(2, 0, 1)
    a["g_wqk"] = np.concatenate([wq, wk], 2)
    a["g_wv"] = i["L0_ffn_wv"].transpose(2, 0, 1)
    gw = np.zeros((2, 64, 2, 2, 4), np.float32)
    g4 = i["L0_ffn_gate_w"].reshape(2, 2, 4, 64)
    for n in range(2):
        gw[n, :, :, n, :] = g4[:, n].transpose(2, 0, 1)
    a["h_gw"] = gw.reshape(128, 2, 8)
    a["h_gbias"] = i["L0_ffn_gate_b"].reshape(16)
    for m in (1, 2):
        fc = np.zeros((65, 64), np.float32)
        for n in range(4):
            fc[16 * n:16 * n + 16, 16 * n:16 * n + 16] = i[f"L0_ffn_fc{m}_w"].T
            fc[64, 16 * n:16 * n + 16] = i[f"L0_ffn_fc{m}_b"]
        a[f"h_fc{m}"] = fc
    a["h_fgate"] = i["L0_ffn_fgate_w"].T
    a["h_lng"], a["h_lnb"], a["h_fng"], a["h_fnb"] = (i["L0_ffn_" + x] for x in ("ln_g", "ln_b", "fnorm_g", "fnorm_b"))
    x = i["x"].transpose(0, 2, 3, 1)
    a["fmap"] = np.concatenate([x[:, :-1], x[:, 1:]], 3).reshape(-1, 2 * C)
    lin = np.linspace(-1.0, 1.0, 32).astype(np.float32)
    px = (lin + np.float32(1)) * np.float32(0.5) * np.float32(127)
    p0 = np.clip(np.floor(px), 0, 126).astype(np.float32)
    fr = np.clip(px - p0, 0, 1).astype(np.float32)
    tok = np.arange(1024)
    yi, xi = tok // 32, tok % 32
    by_tile = lambda u: u.reshape((8, 128) + u.shape[1:]).swapaxes(0, 1)
    fx, fy = fr[xi], fr[yi]
    a["a_wq4"] = by_tile(np.stack([(1 - fx) * (1 - fy), (1 - fx) * fy, fx * (1 - fy), fx * fy], 1).astype(np.float32))
    a["a_ref"] = by_tile(np.stack([lin[xi], lin[yi]], 1))
    q0 = by_tile((p0[yi] * 128 + p0[xi]).astype(np.uint32))
    off = (np.arange(16) * (127 * 128)).astype(np.uint32)
    a["a_qidx"] = (off[:, None, None] + q0[None]).reshape(16 * 128, 8)
    a["a_first"] = np.repeat(off.astype(np.float32), 128)[:, None]
    w1 = np.zeros((65, 80), np.float32)
    w1[:64, :64] = i["L0_tok_W_q"].T
    w1[:64, 64:] = i["L0_tok_W_o1"]
    w1[64, 64:] = i["L0_tok_b_o1"]
    a["a_w1"] = w1
    w2 = np.zeros((33, 16), np.float32)
    w2[:16] = i["L0_tok_W_o2"]
    w2[32] = i["L0_tok_b_o2"]
    a["a_w2"] = w2
    a["a_lng"], a["a_lnb"] = i["L0_tok_ln_g"], i["L0_tok_ln_b"]
    kv = np.zeros((2, 64, 2, 2, 64), np.float32)
    for p in range(2):
        kv[p, :, p, 0] = i["L0_tok_W_k"].T
        kv[p, :, p, 1] = i["L0_tok_W_v"].T
    a["b_wkv"] = kv.reshape(128, 256)
    a["x_txt"] = i["x_txt"].reshape(4, 128).T
    a["pos_S"] = i["pos_S"][:, None]
    a["t_heads"] = np.kron(np.eye(8), np.ones((8, 1))).astype(np.float32)
    s = np.arange(32, dtype=np.float32)
    h = np.arange(8, dtype=np.float32)[None, :, None]
    dist = np.abs(s[:, None, None] - s[None, None, :])
    upper = s[:, None, None] < s[None, None, :]
    slope = np.where(upper, -np.float32(2) ** -(np.float32(0.5) + h), -np.float32(2) ** -(np.float32(1) + h))
    a["t_alibi"] = np.tile((slope * dist).astype(np.float32), (4, 1, 1))
    freq = np.float32(1) / np.float32(10000) ** (np.arange(0, 64, 2, dtype=np.float32) / np.float32(64))
    angle = (np.arange(1024, dtype=np.float32)[:, None] * freq[None]).astype(np.float32)
    a["t_table"] = np.concatenate([np.sin(angle), np.cos(angle)], 1).astype(np.float32)
    a["t_emb"] = i["L0_txt_emb_table"]
    a["t_iw"], a["t_pw"] = i["L0_txt_input_weight"], i["L0_txt_position_weight"]
    a["t_lnfw"], a["t_lnfb"] = i["L0_txt_lnf_w"], i["L0_txt_lnf_b"]
    for n in ("ln1_w", "ln1_b", "ln2_w", "ln2_b"):
        a["t_" + n.replace("_", "")] = i["L0_txt_" + n]
    a["t_w1"] = np.concatenate([i["L0_txt_w1"], i["L0_txt_b1"][:, None]], 1).reshape(6 * 65, 256)
    a["t_w2"] = i["L0_txt_w2"].reshape(6 * 256, 64)
    a["t_b2"] = i["L0_txt_b2"]
    n = np.arange(128)
    later = np.where(n[None, :] > n[:, None], -1e30, 0)
    a["d_consts"] = np.concatenate([np.eye(128), later, later.T, np.tile(np.eye(32), (4, 1))], 1).astype(np.float32)
    return {k: np.ascontiguousarray(v) for k, v in a.items()}


def kernel(**inputs):
    from concourse import bacc
    from concourse.bass_utils import run_bass_kernel_spmd

    nc = bacc.Bacc("TRN2", target_bir_lowering=False, num_devices=1)
    arrays = {f"in_{name}": array for name, array in layout(inputs).items()}
    w = {name[3:]: nc.dram_tensor(name, array.shape, mybir.dt.from_np(array.dtype), kind="ExternalInput").ap()
         for name, array in arrays.items()}
    out = nc.dram_tensor("out_0_dram", (ROWS, C), F32, kind="ExternalOutput").ap()
    early_fusion(nc, w, out)
    r = run_bass_kernel_spmd(nc, [arrays], core_ids=[0])
    return r.results[0]["out_0_dram"].reshape(BATCH, SEQ, C)
```
